# Optimizing a Trainium2 kernel written in Bass

```python
import numpy as np
import jax
import jax.numpy as jnp

def _softmax(x, axis=-1):
    return jax.nn.softmax(x, axis=axis)

def _gelu(x):
    return jax.nn.gelu(x, approximate=True)

def _silu(x):
    return jax.nn.silu(x)

def _sigmoid(x):
    return jax.nn.sigmoid(x)

def _layernorm(x, axis=-1, eps=1e-05):
    m = jnp.mean(x, axis=axis, keepdims=True)
    v = jnp.var(x, axis=axis, keepdims=True)
    return (x - m) / jnp.sqrt(v + eps)

def _scatter_add(tgt, idx, src, axis=0):
    return tgt.at[idx].add(src)

def _segment_sum(src, seg, n):
    return jax.ops.segment_sum(src, seg, n)
kernel_name = 'mk_gps_d1_gnn_r8_b9fd58'

def setup_inputs(seed: int=0):
    np.random.seed(seed)
    _w = jnp.asarray

    def _rec_inputs():
        import jax
        import jax.numpy as jnp
        _gk = jax.random.key(seed)
        x = -6.415e-05 + 1 * jax.random.normal(jax.random.fold_in(_gk, 1), (1250, 512), jnp.float32)
        src = jax.random.randint(jax.random.fold_in(_gk, 2), (20000,), 0, 1250, jnp.int32)
        dst = jax.random.randint(jax.random.fold_in(_gk, 3), (20000,), 0, 1250, jnp.int32)
        _o = jnp.argsort(dst, stable=True)
        src = src[_o]
        dst = dst[_o]
        edge_attr_8 = 0.0012443 + 1.0001 * jax.random.normal(jax.random.fold_in(_gk, 11), (20000, 8), jnp.float32)
        return (x, src, dst, edge_attr_8)
    x, src, dst, edge_attr_8 = _rec_inputs()

    def _L0_gnn_setup():
        import jax, jax.numpy as jnp
        import numpy as np
        N = 2500
        E = 40000
        D = 512
        H = 8
        DK = D // H
        key = jax.random.key(seed)
        ks = jax.random.split(key, 12)
        x = jax.random.normal(ks[0], (N, D), jnp.float32)
        rows = jnp.sort(jax.random.randint(ks[1], (E,), 0, N))
        cols = jax.random.randint(ks[2], (E,), 0, N)
        edge_index = jnp.stack([rows, cols]).astype(jnp.int32)
        att_bias = jax.random.normal(ks[3], (E, H), jnp.float32)
        s = float(1.0 / np.sqrt(D))
        Wq = jax.random.normal(ks[4], (D, D), jnp.float32) * s
        Wk = jax.random.normal(ks[5], (D, D), jnp.float32) * s
        Wv = jax.random.normal(ks[6], (D, D), jnp.float32) * s
        Wo = jax.random.normal(ks[7], (D, D), jnp.float32) * s
        bq = jnp.zeros((D,), jnp.float32)
        bk = jnp.zeros((D,), jnp.float32)
        bv = jnp.zeros((D,), jnp.float32)
        bo = jnp.zeros((D,), jnp.float32)
        return dict(x=x, edge_index=edge_index, att_bias=att_bias, Wq=Wq, bq=bq, Wk=Wk, bk=bk, Wv=Wv, bv=bv, Wo=Wo, bo=bo)
    _L0_gnn_all = _L0_gnn_setup()
    _L0_gnn_in = {k: v for k, v in _L0_gnn_all.items() if k in ('Wq', 'bq', 'Wk', 'bk', 'Wv', 'bv', 'Wo', 'bo')}
    del _L0_gnn_all

    def _L0_mix_setup():
        import jax, jax.numpy as jnp
        import numpy as np
        EPS = 1e-05

        def gamma_layer_norm(x, gamma):
            mu = jnp.mean(x, axis=-1, keepdims=True)
            var = jnp.var(x, axis=-1, keepdims=True)
            return (x - mu) * jax.lax.rsqrt(var + EPS) * gamma
        key = jax.random.key(seed)
        k1, k2, k3, k4 = jax.random.split(key, 4)
        b, n, dim = (8, 512, 512)
        heads, head_size = (8, 64)
        hidden = heads * head_size
        x = jax.random.normal(k1, (b, n, dim), dtype=jnp.float32)
        w_qkv = jax.random.normal(k2, (3 * hidden, dim), dtype=jnp.float32) * dim ** (-0.5)
        w_out = jax.random.normal(k3, (dim, hidden), dtype=jnp.float32) * hidden ** (-0.5)
        gamma = 1.0 + 0.02 * jax.random.normal(k4, (dim,), dtype=jnp.float32)
        return {'x': x, 'w_qkv': w_qkv, 'w_out': w_out, 'gamma': gamma}
    _L0_mix_all = _L0_mix_setup()
    _L0_mix_in = {k: v for k, v in _L0_mix_all.items() if k in ('w_qkv', 'w_out', 'gamma')}
    del _L0_mix_all

    def _L0_ffn_setup():
        import jax, jax.numpy as jnp
        import numpy as np
        B, S, D, H, O, E, TOPK = (4, 256, 512, 1024, 512, 8, 2)
        key = jax.random.key(seed)
        ks = jax.random.split(key, 6)
        s = lambda d: 1.0 / np.sqrt(d)
        return {'x': jax.random.normal(ks[0], (B, S, D), dtype=jnp.float32), 'Wg': jax.random.normal(ks[1], (D, E), dtype=jnp.float32) * s(D), 'W1': jax.random.normal(ks[2], (E, D, H), dtype=jnp.float32) * s(D), 'b1': jnp.zeros((E, H), dtype=jnp.float32), 'W2': jax.random.normal(ks[3], (E, H, O), dtype=jnp.float32) * s(H), 'b2': jnp.zeros((E, O), dtype=jnp.float32)}
    _L0_ffn_all = _L0_ffn_setup()
    _L0_ffn_in = {k: v for k, v in _L0_ffn_all.items() if k in ('Wg', 'W1', 'b1', 'W2', 'b2')}
    del _L0_ffn_all
    return {'x': x, 'src': src, 'dst': dst, 'edge_attr_8': edge_attr_8, 'L0_gnn_Wq': _L0_gnn_in['Wq'], 'L0_gnn_bq': _L0_gnn_in['bq'], 'L0_gnn_Wk': _L0_gnn_in['Wk'], 'L0_gnn_bk': _L0_gnn_in['bk'], 'L0_gnn_Wv': _L0_gnn_in['Wv'], 'L0_gnn_bv': _L0_gnn_in['bv'], 'L0_gnn_Wo': _L0_gnn_in['Wo'], 'L0_gnn_bo': _L0_gnn_in['bo'], 'L0_mix_w_qkv': _L0_mix_in['w_qkv'], 'L0_mix_w_out': _L0_mix_in['w_out'], 'L0_mix_gamma': _L0_mix_in['gamma'], 'L0_ffn_Wg': _L0_ffn_in['Wg'], 'L0_ffn_W1': _L0_ffn_in['W1'], 'L0_ffn_b1': _L0_ffn_in['b1'], 'L0_ffn_W2': _L0_ffn_in['W2'], 'L0_ffn_b2': _L0_ffn_in['b2']}

def reference(x, src, dst, edge_attr_8, L0_gnn_Wq, L0_gnn_bq, L0_gnn_Wk, L0_gnn_bk, L0_gnn_Wv, L0_gnn_bv, L0_gnn_Wo, L0_gnn_bo, L0_mix_w_qkv, L0_mix_w_out, L0_mix_gamma, L0_ffn_Wg, L0_ffn_W1, L0_ffn_b1, L0_ffn_W2, L0_ffn_b2):
    import jax
    import jax.numpy as jnp

    def _L0_gnn_ref(x, edge_index, att_bias, Wq, bq, Wk, bk, Wv, bv, Wo, bo):
        import jax, jax.numpy as jnp
        import numpy as np
        N = 2500
        E = 40000
        D = 512
        H = 8
        DK = D // H
        n = x.shape[0]
        rows, cols = (edge_index[0], edge_index[1])
        q = (x @ Wq + bq).reshape(n, H, DK)
        k = (x @ Wk + bk).reshape(n, H, DK)
        v = (x @ Wv + bv).reshape(n, H, DK)
        scale = 1.0 / jnp.sqrt(jnp.asarray(DK, x.dtype))
        logits = jnp.einsum('ehd,ehd->eh', q[rows] * scale, k[cols]) + att_bias
        row_max = jax.ops.segment_max(logits, rows, num_segments=n)
        p = jnp.exp(logits - row_max[rows])
        denom = jax.ops.segment_sum(p, rows, num_segments=n)
        att = p / denom[rows]
        y = jax.ops.segment_sum(att[:, :, None] * v[cols], rows, num_segments=n)
        out = y.reshape(n, H * DK) @ Wo + bo
        return out

    def _L0_mix_ref(x, w_qkv, w_out, gamma):
        import jax, jax.numpy as jnp
        import numpy as np
        EPS = 1e-05

        def gamma_layer_norm(x, gamma):
            mu = jnp.mean(x, axis=-1, keepdims=True)
            var = jnp.var(x, axis=-1, keepdims=True)
            return (x - mu) * jax.lax.rsqrt(var + EPS) * gamma
        b, n, dim = x.shape
        heads, head_size = (8, 64)
        scale = head_size ** (-0.5)
        qkv = jnp.einsum('bnd,hd->bnh', x, w_qkv)
        q, k, v = jnp.split(qkv, 3, axis=-1)

        def to_heads(t):
            return t.reshape(b, n, heads, head_size).transpose(0, 2, 1, 3)
        q, k, v = (to_heads(q), to_heads(k), to_heads(v))
        q = jax.nn.softmax(q, axis=-1) * scale
        k = jax.nn.softmax(k, axis=-2)
        context = jnp.einsum('bhnd,bhne->bhde', k, v)
        out = jnp.einsum('bhde,bhnd->bhne', context, q)
        out = out.transpose(0, 2, 1, 3).reshape(b, n, heads * head_size)
        out = jnp.einsum('bnh,dh->bnd', out, w_out)
        out = gamma_layer_norm(out, gamma)
        return out

    def _L0_ffn_ref(x, Wg, W1, b1, W2, b2):
        import jax, jax.numpy as jnp
        import numpy as np
        B, S, D, H, O, E, TOPK = (4, 256, 512, 1024, 512, 8, 2)
        Bsz, Seq, Din = x.shape
        T = Bsz * Seq
        xm = x.reshape(T, Din)
        probs = jax.nn.softmax(xm @ Wg, axis=-1)
        top_p, top_i = jax.lax.top_k(probs, TOPK)
        gates = jnp.zeros((T, E), dtype=probs.dtype).at[jnp.arange(T)[:, None], top_i].set(top_p)
        h = jax.nn.gelu(jnp.einsum('td,edh->teh', xm, W1) + b1[None])
        y = jnp.einsum('teh,eho->teo', h, W2) + b2[None]
        out = jnp.einsum('te,teo->to', gates, y)
        return out.reshape(Bsz, Seq, O)
    edge_index = jnp.stack([src, dst])
    xn = _layernorm(x, axis=-1)
    x = x + _L0_gnn_ref(xn, edge_index, edge_attr_8, L0_gnn_Wq, L0_gnn_bq, L0_gnn_Wk, L0_gnn_bk, L0_gnn_Wv, L0_gnn_bv, L0_gnn_Wo, L0_gnn_bo) + _L0_mix_ref(xn[None], L0_mix_w_qkv, L0_mix_w_out, L0_mix_gamma)[0]
    x = x + _L0_ffn_ref(_layernorm(x, axis=-1)[None], L0_ffn_Wg, L0_ffn_W1, L0_ffn_b1, L0_ffn_W2, L0_ffn_b2)[0]
    return x

_drawn_inputs = setup_inputs


def setup_inputs(seed=0):
    import zlib

    import numpy as np

    out = dict(_drawn_inputs(seed))
    spreads = {'L0_gnn_bq': (0.0, 0.272),
     'L0_gnn_bk': (0.0, 0.8),
     'L0_gnn_bv': (0.0, 0.1),
     'L0_gnn_bo': (0.0, 0.1),
     'L0_ffn_b1': (0.0, 0.397),
     'L0_ffn_b2': (0.0, 0.268)}
    factors = {'L0_mix_gamma': 3.337}
    for name, (base, spread) in spreads.items():
        noise = np.random.default_rng([zlib.crc32(name.encode()), seed]).standard_normal(out[name].shape)
        drawn = base * np.exp(spread * noise) if base else spread * noise
        out[name] = jnp.asarray(drawn.astype(out[name].dtype))
    for name, factor in factors.items():
        out[name] = (out[name] * factor).astype(out[name].dtype)
    return out
```

```python
import numpy as np
import concourse.bass as bass
from concourse import mybir
from contextlib import ExitStack

F32, BF16, I32 = mybir.dt.float32, mybir.dt.bfloat16, mybir.dt.int32
ALU, ACT, AX = mybir.AluOpType, mybir.ActivationFunctionType, mybir.AxisListType

P = 128
N, D = 1250, 512
HEADS, DK = 8, 64
E = 20000
NT = (N + P - 1) // P
NPAD = NT * P
LAST = N - (NT - 1) * P
KC = D // P
EPS = 1e-5

EP = 125
ET = E // EP
EG = 4
LG = 16
S = 4
ROWS = N + E // S
RT = 2 * ((ROWS + 2 * P - 1) // (2 * P))
MG = (RT + 3) // 4
REC = 2 + HEADS
BIG = 1e30
NOBODY = 1e6
NONODE = 4096.0
YW = DK + 1

NE, HID = 8, 1024
HC = HID // P
NCH = [(0, 512), (512, 512), (1024, N - 1024)]
KB = 1024


class Steps:

    def __init__(self, eng, sem):
        self.eng, self.sem, self.done, self.base, self.k = eng, sem, 0, None, 0

    def link(self, ins):
        ins.then_inc(self.sem, 1)
        self.k += 1
        self.eng.wait_ge(self.sem, self.k + (self.done if self.base is None else self.base))

    def enter(self, n, per_turn):
        self.done += self.k
        self.k, self.per_turn = 0, per_turn
        self.base = n * per_turn + self.done

    def leave(self, turns):
        assert self.k == self.per_turn, self.k
        self.done += turns * self.per_turn
        self.base, self.k = None, 0


def gps_layer(nc, x, src, dst, edge_attr, Wq, bq, Wk, bk, Wv, bv, Wo, bo, w_qkv, w_out, gamma,
              Wg, W1, b1, W2, b2, out):
    ctx = ExitStack()
    with ctx:
        base = ((nc.sbuf_base + 63) // 64) * 64

        def at(name, kb, shape, dt=F32):
            return place(name, shape, dt, base + int(kb * KB))

        def place(name, shape, dt, offset):
            size = int(np.prod(shape[1:])) * mybir.dt.size(dt)
            assert offset + size <= base + 206 * KB, name
            return nc.alloc_sbuf_tensor_at(name, shape, dt, offset=offset)

        def sem(name):
            return ctx.enter_context(nc.semaphore(name))

        ident = at("ident", 0, [P, P])
        low_f = at("low_f", 0.5, [P, P])
        ones_f = at("ones_f", 1, [P, P])
        identb = at("identb", 1.5, [P, P], BF16)
        lowb = at("lowb", 1.75, [P, P], BF16)
        iotab = at("iotab", 2, [P, P], BF16)
        iota256 = at("iota256", 2.25, [P, 2 * P])
        iota_i = at("iota_i", 3.25, [P, 2 * P], I32)
        iota10 = at("iota10", 4.25, [P, NT], BF16)
        tile0 = at("tile0", 4.375, [P, RT])
        tile0_i = at("tile0_i", 4.625, [P, RT], I32)
        zeros_r = at("zeros_r", 4.875, [P, ET])
        eps_c = at("eps_c", 5.5, [P, 1])
        pos8 = at("pos8", 5.5625, [P, NE])
        bias_q = at("bias_q", 6, [P, D])
        bias_k = at("bias_k", 8, [P, D])
        bias_v = at("bias_v", 10, [P, D])
        bias_o = at("bias_o", 12, [P, D])
        gamma_b = at("gamma_b", 14, [P, D])

        X = at("X", 16, [P, NT, D])

        att = at("att", 36, [P, ET * HEADS])
        empty = at("empty", 41, [P, RT * S, REC])
        onehot_lo = at("onehot_lo", 49, [P, 2, EG, P], BF16)
        before = at("before", 51, [P, 2, EG, P], BF16)
        src_i = at("src_i", 53, [P, ET], I32)
        dst_i = at("dst_i", 53.75, [P, ET], I32)
        part_i = at("part_i", 54.5, [P, ET], I32)
        lo_b = at("lo_b", 55.25, [P, ET], BF16)
        hi_b = at("hi_b", 55.625, [P, ET], BF16)
        records = at("records", 120, [P, ET, REC])
        place_i = at("place_i", 126.25, [P, ET], I32)
        stage_r = [at(f"stage_r{j}", 126.875 + 0.0625 * j, [P, REC]) for j in range(8)]
        stage_i = [at(f"stage_i{j}", 127.375 + 0.0625 * j, [P, 1], I32) for j in range(8)]
        onehot_loT = at("onehot_loT", 128, [P, ET, P], BF16)
        onehot_hi = at("onehot_hi", 168, [P, ET, NT], BF16)
        count = at("count", 172, [P, ET, NT])
        upto = at("upto", 178.5, [P, ET, NT])
        within = at("within", 185, [P, ET, NT])
        first_b = at("first_b", 191.5, [P, ET, 2, NT], BF16)
        first_f = at("first_f", 198, [P, ET, NT])
        first_i = at("first_i", 172, [P, ET, NT], I32)
        halves_i = at("halves_i", 178.5, [P, ET, NT], I32)
        found = at("found", 172, [P, LG, 2, NT])
        parts = at("parts", 174, [P, ET, 2])
        ranks = at("ranks", 176, [P, ET])
        place_f = at("place_f", 177, [P, ET])
        deg = at("deg", 204.5, [P, NT])
        deg_i = at("deg_i", 204.5625, [P, NT], I32)
        rows_f = at("rows_f", 204.625, [P, NT])
        rows_in = at("rows_in", 204.6875, [P, NT])
        blk0 = at("blk0", 204.75, [P, NT])
        start4 = at("start4", 204.8125, [P, NT])
        tot = at("tot", 204.875, [P, NT])
        cmp_b = at("cmp_b", 178.5, [P, RT, NT])
        block_f = at("block_f", 5.625, [P, RT])
        block_i = at("block_i", 205, [P, RT], I32)
        nodebase = at("nodebase", 205.25, [P, RT])

        XNT = at("XNT", 36, [P, KC, NPAD])
        Wqkv = at("Wqkv", 56, [P, 3, KC, D])
        raw = at("raw", 80, [P, 12, D])
        raw_o = at("raw_o", 104, [P, KC, D])
        WoT = at("WoT", 112, [P, KC, D])
        mixT = at("mixT", 128, [P, KC, 3 * D])
        QT = at("QT", 152, [P, KC, NPAD])
        KT = at("KT", 172, [P, KC, NPAD])
        KE = at("KE", 56, [P, NT, D])
        V = at("V", 80, [P, NT, D])
        Mx = at("Mx", 192, [P, KC, D])
        ctxbd = at("ctxbd", 200, [P, KC, P])
        xn = [at(f"xn{j}", 172 + 2 * j, [P, D]) for j in range(2)]
        qs = [at(f"qs{j}", 76 + 2 * j, [P, D]) for j in range(2)]
        send = [at(f"send{j}", 100 + 2 * j, [P, D]) for j in range(2)]
        mixo = at("mixo", 172, [P, NT, D])
        sm = 202
        stats = at("stats", sm, [P, 6])
        mv = at("mv", sm + 0.0625, [P, NT, 2])
        rstd = at("rstd", sm + 0.1875, [P, NT])
        kmax3 = at("kmax3", sm + 0.25, [P, KC, 3])
        kneg = at("kneg", sm + 0.3125, [P, KC])
        ksum3 = at("ksum3", sm + 0.375, [P, KC, 3])
        krec = at("krec", sm + 0.4375, [P, KC])
        qmax = at("qmax", sm + 0.5, [P, HEADS])
        qsum = at("qsum", sm + 0.5625, [P, HEADS])
        qrec = at("qrec", sm + 0.625, [P, HEADS])

        table = at("table", 36, [P, RT, S, REC])
        YR = at("YR", 44, [P, RT, HEADS, YW])
        KV = at("KV", 148, [P, 2, S, 2 * D])
        QG = at("QG", 180, [P, 2, D])
        prod = at("prod", 184, [P, S, D])
        pv = at("pv", 192, [P, S, D])
        logit = at("logit", 200, [P, 2, S, HEADS])
        prob = at("prob", 200.25, [P, 2, S, HEADS])
        rowmax = at("rowmax", 200.5, [P, RT, HEADS])
        rowfloor = at("rowfloor", 202.125, [P, HEADS])
        nbr_i = [at(f"nbr_i{j}", 202.25 + 0.0625 * j, [P, 8], I32) for j in range(2)]
        idx1 = [[at(f"idx{j}_{s}", 202.375 + 0.0625 * (5 * j + s), [P, 1], I32) for s in range(5)] for j in range(2)]
        nodes8 = at("nodes8", 145.75, [P, RT, HEADS])
        LT = at("LT", 148, [HEADS, RT * P])
        seg = at("seg", 173.25, [HEADS, RT * P + 1])
        nodes_c = at("nodes_c", 198.4375, [HEADS, 4 * P + 1])
        node_off = at("node_off", 205.5, [P, RT])
        Mrow = at("Mrow", 203.125, [P, RT, HEADS])
        onehot_n = at("onehot_n", 148, [P, 2, 2 * P])
        Y = at("Y", 176, [P, NT + 1, HEADS, YW])
        yden = at("yden", 203.125, [P, NT, HEADS])
        YN = at("YN", 44, [P, NT, D])
        YT = at("YT", 64, [P, KC, NPAD])
        Wo_s = at("Wo_s", 84, [P, KC, D])

        HT = at("HT", 36, [P, KC, NPAD])
        hn = [at(f"hn{j}", 56 + 2 * j, [P, D]) for j in range(2)]
        Wg_s = at("Wg_s", 60, [P, KC, NE])
        b1raw = at("b1raw", 60.125, [NE * HC, P])
        b1T = at("b1T", 60.625, [P, NE * HC])
        b2_s = at("b2_s", 61, [NE, D])
        rl = at("rl", 63, [P, NT, NE])
        rp = at("rp", 63.375, [P, NT, NE])
        rt = at("rt", 63.75, [P, NT, NE])
        pick = at("pick", 64.125, [P, NT, NE])
        gate = at("gate", 64.5, [P, NT, NE])
        r1 = at("r1", 64.875, [P, NT])
        gateT = at("gateT", 66, [NE, NPAD])
        W1_s = at("W1_s", 92, [P, 2, KC, HID])
        W2_s = at("W2_s", 124, [P, 2, HC, D])
        G = at("G", 156, [P, HC, NPAD])

        psum = ctx.enter_context(nc.psum_tensor("psum", [P, 8, 512], F32))
        bank = [psum[:, i, :] for i in range(8)]

        def bf(b):
            return bank[b][:, 0:256].bitcast(BF16)

        q_dram = nc.dram_tensor("q_rows", [N, D], F32, kind="Internal").ap()
        kv_dram = nc.dram_tensor("kv_rows", [N, 2 * D], F32, kind="Internal").ap()
        table_d = nc.dram_tensor("sorted_edges", [RT * P * S, REC], F32, kind="Internal").ap()

        names = """const_ready consts edges_in pad_ready x_in weights_in empty_ready empty_out onehot_lo_ready
            loT_psum loT_ready same_psum before_ready counts_psum counts_ready first_ready
            rowcount_ready prefix_psum found_psum places_ready staged dve gp se
            xn_ready tr_psum tr_done unit_psum unit_done send_ready kt_psum kmax_ready kt_exp
            ke_psum ke_done q_sub q_exp q_ready qt_psum qt_done ctx_psum ctx_ready m_psum m_ready
            mix_psum mix_copied mixvar_ready mixstd_ready var_ready std_ready
            table_ready kv_zero idx_ready turn_free logit_ready prob_ready pv_ready
            y_psum y_copied lt_psum lt_done nodes_ready seg_chunk m_back m_scan w_ready w_exp
            onehot_n_ready yr_scaled merge_psum merged yn_ready yt_psum yt_done wo_psum wo_done
            x_done h_ready ht_psum ht_done r_psum r_ready r_exp gate_ready gt_psum gt_done b1_psum b1_done
            b2_psum h_psum h_gelu e_psum e_done out_done dense_psum_free gates_added lt_nodes seg_done sent_q records_ready
            act_passed pool_passed""".split()
        q = {n: sem(n) for n in names}
        scat = [sem(f"scattered{j}") for j in range(8)]
        gath = [sem(f"gathered{j}") for j in range(2)]
        sent = [sem(f"sent{j}") for j in range(2)]
        wl = [sem(f"expert_in{j}") for j in range(2)]
        wts = {n: sem("in_" + n) for n in ("wqkv", "raw", "rawo", "bias", "table", "wo", "small")}
        q = type("Semaphores", (), q)

        block = ctx.enter_context(nc.Block())

        UNITS = 5 * NT

        def apart(eng):
            eng.sem_inc(q.act_passed if eng.engine == mybir.EngineType.Activation else q.pool_passed, 1)

        @block.sync
        def _(sp):
            sp.wait_ge(q.pad_ready, 1)
            sp.dma_start(src_i[0:EP, :], src.rearrange("(p t) -> p t", t=ET)).then_inc(q.edges_in, 16)
            sp.dma_start(dst_i[0:EP, :], dst.rearrange("(p t) -> p t", t=ET)).then_inc(q.edges_in, 16)
            sp.dma_start(att[0:EP, :], edge_attr.rearrange("(p t) h -> p (t h)", t=ET)).then_inc(q.edges_in, 16)
            sp.wait_ge(q.pad_ready, 2)
            sp.dma_start(X[:, 0:NT - 1, :], x[0:(NT - 1) * P, :].rearrange("(t p) d -> p t d", p=P)).then_inc(q.x_in, 16)
            sp.dma_start(X[0:LAST, NT - 1, :], x[(NT - 1) * P:N, :]).then_inc(q.x_in, 16)
            sp.dma_start(raw[:, :, :], w_qkv.rearrange("(g p) d -> p g d", p=P)).then_inc(wts["raw"], 16)
            sp.dma_start(raw_o[:, :, :], w_out.rearrange("(g p) d -> p g d", p=P)).then_inc(wts["rawo"], 16)
            for i, w in enumerate((Wq, Wk, Wv)):
                sp.dma_start(Wqkv[:, i, :, :], w.rearrange("(k p) d -> p k d", p=P)).then_inc(wts["wqkv"], 16)
            for t, b in ((bias_q, bq), (bias_k, bk), (bias_v, bv), (bias_o, bo), (gamma_b, gamma)):
                sp.dma_start(t[:, :], b.rearrange("(a d) -> a d", a=1).broadcast_to([P, D])).then_inc(wts["bias"], 16)
            sp.wait_ge(q.empty_ready, 1)
            sp.dma_start(table_d.rearrange("(p r) c -> p (r c)", p=P), empty[:, :, :]).then_inc(q.empty_out, 16)

            for u in range(3 * NT):
                i, w = divmod(u, 3)
                rows = P if i < NT - 1 else LAST
                to = q_dram[i * P:i * P + rows, :] if w == 0 else kv_dram[i * P:i * P + rows, (w - 1) * D:w * D]
                sp.wait_ge(q.send_ready, u + 1)
                sp.dma_start(to, send[u % 2][0:rows, :]).then_inc(sent[u % 2], 16)

            for j in range(8):
                sp.wait_ge(scat[j], 16 * (ET // 8))
            sp.wait_ge(q.x_done, 1)
            sp.dma_start(table[:, :, :, :], table_d.rearrange("(t p s) c -> p t (s c)", p=P, s=S)
                         .rearrange("p t (s c) -> p t s c", s=S)).then_inc(wts["table"], 16)

            sp.wait_ge(q.merged, RT + 2)
            sp.dma_start(Wo_s[:, :, :], Wo.rearrange("(k p) d -> p k d", p=P)).then_inc(wts["wo"], 16)
            for j in range(2):
                sp.dma_start(W1_s[:, j, :, :], W1[j, :, :].rearrange("(k p) h -> p k h", p=P)).then_inc(wl[j], 16)
                sp.dma_start(W2_s[:, j, :, :], W2[j, :, :].rearrange("(k p) h -> p k h", p=P)).then_inc(wl[j], 16)
            sp.wait_ge(q.wo_psum, 1)
            sp.dma_start(Wg_s[:, :, :], Wg.rearrange("(k p) e -> p k e", p=P)).then_inc(wts["small"], 16)
            sp.dma_start(b1raw[:, :], b1.rearrange("e (c p) -> (e c) p", p=P)).then_inc(wts["small"], 16)
            sp.dma_start(b2_s[:, :], b2).then_inc(wts["small"], 16)
            with sp.Fori(0, NE // 2 - 1) as n:
                for j in range(2):
                    sp.wait_ge(q.e_psum, n * (2 * NT) + (j + 1) * NT)
                    ex = n * 2 + j + 2
                    sp.dma_start(W1_s[:, j, :, :], W1[bass.ds(ex, 1), :, :].rearrange("e (k p) h -> p (e k) h", p=P)).then_inc(wl[j], 16)
                    sp.dma_start(W2_s[:, j, :, :], W2[bass.ds(ex, 1), :, :].rearrange("e (k p) h -> p (e k) h", p=P)).then_inc(wl[j], 16)
            sp.wait_ge(q.e_done, NE * NT + 2)
            sp.dma_start(out[0:(NT - 1) * P, :].rearrange("(t p) d -> p t d", p=P), X[:, 0:NT - 1, :]).then_inc(q.out_done, 16)
            sp.dma_start(out[(NT - 1) * P:N, :], X[0:LAST, NT - 1, :]).then_inc(q.out_done, 16)
            sp.wait_ge(q.out_done, 32)

        @block.gpsimd
        def _(gp):
            st = Steps(gp, q.gp)
            gp.memset(dst_i[:, :], 0)
            gp.memset(att[:, :], 0.0)
            gp.memset(src_i[:, :], 1 << 20).then_inc(q.pad_ready, 1)
            gp.memset(X[:, NT - 1, :], 0.0).then_inc(q.pad_ready, 1)
            for m in (ident, identb):
                st.link(gp.memset(m[:, :], 0.0))
                st.link(gp.affine_select(out=m[:, :], in_=m[:, :], compare_op=ALU.not_equal, fill=1.0, base=0,
                                         pattern=[[-1, P]], channel_multiplier=1))
            for m in (low_f, lowb):
                st.link(gp.memset(m[:, :], 0.0))
                st.link(gp.affine_select(out=m[:, :], in_=m[:, :], compare_op=ALU.is_ge, fill=1.0, base=0,
                                         pattern=[[-1, P]], channel_multiplier=1))
            gp.memset(ones_f[:, :], 1.0)
            gp.memset(zeros_r[:, :], 0.0)
            gp.memset(eps_c[:, :], EPS)
            st.link(gp.iota(iota_i[:, :], pattern=[[1, 2 * P]], base=0, channel_multiplier=0))
            st.link(gp.iota(tile0_i[:, :], pattern=[[P, RT]], base=0, channel_multiplier=0))
            gp.tensor_copy(tile0[:, :], tile0_i[:, :])
            gp.tensor_copy(iota256[:, :], iota_i[:, :])
            gp.tensor_copy(pos8[:, :], iota_i[:, 0:NE])
            gp.tensor_copy(iota10[:, :], iota_i[:, 0:NT])
            gp.tensor_copy(iotab[:, :], iota_i[:, 0:P]).then_inc(q.consts, 1)
            gp.memset(empty[:, :, 0:1], NOBODY)
            gp.memset(empty[:, :, 1:2], NONODE)
            gp.memset(empty[:, :, 2:REC], -BIG).then_inc(q.empty_ready, 1)

            gp.wait_ge(q.places_ready, 1)
            gp.wait_ge(q.empty_out, 16)
            with gp.Fori(0, ET // 8) as n:
                for j in range(8):
                    t = n * 8 + j
                    gp.tensor_copy(stage_i[j][:, :], place_i[:, bass.ds(t, 1)])
                    gp.tensor_copy(stage_r[j][:, :], records[:, bass.ds(t, 1), :]).then_inc(q.staged, 1)
                    gp.wait_ge(q.staged, t + 1)
                    apart(gp)
                    gp.indirect_dma_start(table_d, bass.IndirectOffsetOnAxis(ap=stage_i[j][0:EP, :], axis=0),
                                          stage_r[j][0:EP, :], None,
                                          bounds_check=RT * P * S - 1, oob_is_err=False).then_inc(scat[j], 16)
                for j in range(8):
                    gp.wait_ge(scat[j], n * 16 + 16)
                    apart(gp)

            gp.wait_ge(q.x_done, 1)
            gp.memset(KV[:, :, :, :], 0.0)
            gp.memset(QG[:, :, :], 0.0).then_inc(q.kv_zero, 1)
            gp.wait_ge(q.kv_zero, 1)
            gp.wait_ge(wts["table"], 16)
            for j in range(2):
                gp.wait_ge(sent[j], 16 * (3 * NT // 2))
            with gp.Fori(0, RT // 2) as n:
                for j in range(2):
                    t = n * 2 + j
                    gp.wait_ge(q.turn_free, t + 1)
                    apart(gp)
                    for s in range(S):
                        gp.tensor_copy(idx1[j][s][:, :], table[:, bass.ds(t, 1), s, 0])
                    gp.tensor_copy(idx1[j][S][:, :], table[:, bass.ds(t, 1), 0, 1]).then_inc(q.idx_ready, 1)
                    gp.wait_ge(q.idx_ready, t + 1)
                    apart(gp)
                    gp.indirect_dma_start(QG[:, j, :], None, q_dram,
                                          bass.IndirectOffsetOnAxis(ap=idx1[j][S][:, :], axis=0),
                                          bounds_check=N - 1, oob_is_err=False).then_inc(gath[j], 16)
                    for s in range(S):
                        gp.indirect_dma_start(KV[:, j, s, :], None, kv_dram,
                                              bass.IndirectOffsetOnAxis(ap=idx1[j][s][:, :], axis=0),
                                              bounds_check=N - 1, oob_is_err=False).then_inc(gath[j], 16)

        @block.scalar
        def _(act):
            with act.Fori(0, ET // EG) as g:
                act.wait_ge(q.loT_psum, g + 1)
                apart(act)
                act.copy(onehot_loT[:, bass.ds(g * EG, EG), :], bf(0).rearrange("p (a b) -> p a b", a=EG)).then_inc(q.loT_ready, 1)
                act.wait_ge(q.counts_psum, g + 1)
                apart(act)
                act.copy(count[:, bass.ds(g * EG, EG), :], bank[2][:, 0:EG * NT].rearrange("p (a b) -> p a b", a=EG))
                act.copy(within[:, bass.ds(g * EG, EG), :],
                         bank[2][:, EG * NT:2 * EG * NT].rearrange("p (a b) -> p a b", a=EG)).then_inc(q.counts_ready, 1)

            act.wait_ge(q.places_ready, 1)
            act.wait_ge(q.empty_out, 16)
            for g in range(16 + NT):
                if g == 16:
                    act.wait_ge(q.var_ready, 1)
                    act.activation(rstd[:, :], mv[:, :, 1], ACT.Sqrt, bias=eps_c[:, :]).then_inc(q.std_ready, 1)
                act.wait_ge(q.tr_psum, g + 1)
                if g < 12:
                    to = mixT[:, :, g * P:(g + 1) * P]
                elif g < 16:
                    to = WoT[:, :, (g - 12) * P:(g - 11) * P]
                else:
                    to = XNT[:, :, (g - 16) * P:(g - 15) * P]
                act.copy(to, bank[g % 2][:, :].rearrange("p (a b) -> p a b", a=KC)).then_inc(q.tr_done, 1)
            for c in range(KC):
                act.wait_ge(q.kmax_ready, c + 1)
                for i, (o, w) in enumerate(NCH):
                    act.activation(KT[:, c, o:o + w], bank[4 + i][:, 0:w], ACT.Exp, bias=kneg[:, c:c + 1],
                                   accum_out=ksum3[:, c, i:i + 1]).then_inc(q.kt_exp, 1)
            for i in range(NT):
                act.wait_ge(q.ke_psum, i + 1)
                act.copy(KE[0:rows_of(i), i, :], bank[i % 2][0:rows_of(i), :]).then_inc(q.ke_done, 1)
            for i in range(NT):
                act.wait_ge(q.q_sub, i + 1)
                act.activation(qs[i % 2][:, :], qs[i % 2][:, :], ACT.Exp).then_inc(q.q_exp, 1)
                if i >= 1:
                    act.wait_ge(q.qt_psum, i)
                    act.copy(QT[:, :, (i - 1) * P:i * P], bank[(i - 1) % 2][:, :].rearrange("p (a b) -> p a b", a=KC)).then_inc(q.qt_done, 1)
            act.wait_ge(q.qt_psum, NT)
            act.copy(QT[:, :, (NT - 1) * P:NPAD], bank[(NT - 1) % 2][:, :].rearrange("p (a b) -> p a b", a=KC)).then_inc(q.qt_done, 1)
            for i in range(NT):
                act.wait_ge(q.mix_psum, i + 1)
                act.copy(mixo[:, i, :], bank[2 + i % 2][:, :]).then_inc(q.mix_copied, 1)
            act.wait_ge(q.mixvar_ready, 1)
            act.activation(rstd[:, :], mv[:, :, 1], ACT.Sqrt, bias=eps_c[:, :]).then_inc(q.mixstd_ready, 1)

            act.wait_ge(q.x_done, 1)
            act.nop().then_inc(q.y_copied, 2)
            with act.Fori(0, RT // 2) as n:
                for j in range(2):
                    t = n * 2 + j
                    act.wait_ge(q.logit_ready, t + 1)
                    act.activation(prob[:, j, :, :], logit[:, j, :, :], ACT.Exp).then_inc(q.prob_ready, 1)
                    act.wait_ge(q.y_psum, t + 2)
                    apart(act)
                    act.copy(YR[:, bass.ds(t, 1), :, 0:DK],
                             bank[j][:, :].rearrange("p (a h d) -> p a h d", a=1, h=HEADS)).then_inc(q.y_copied, 1)
            for g in range(MG):
                w = min(4 * P, RT * P - 4 * P * g)
                act.wait_ge(q.lt_psum, g + 1)
                act.copy(LT[:, 4 * P * g:4 * P * g + w], bank[g % 2][0:HEADS, 0:w]).then_inc(q.lt_done, 1)
            act.wait_ge(q.w_ready, 1)
            act.activation(rowmax[:, :, :], rowmax[:, :, :], ACT.Exp).then_inc(q.w_exp, 1)
            for i in range(NT):
                act.wait_ge(q.yt_psum, i + 1)
                act.copy(YT[:, :, i * P:(i + 1) * P], bank[i % 2][:, :].rearrange("p (a b) -> p a b", a=KC)).then_inc(q.yt_done, 1)
            act.wait_ge(q.var_ready, 2)
            act.activation(rstd[:, :], mv[:, :, 1], ACT.Sqrt, bias=eps_c[:, :]).then_inc(q.std_ready, 1)
            for i in range(NT):
                act.wait_ge(q.ht_psum, i + 1)
                act.copy(HT[:, :, i * P:(i + 1) * P], bank[i % 2][:, :].rearrange("p (a b) -> p a b", a=KC)).then_inc(q.ht_done, 1)
            act.wait_ge(q.b1_psum, 1)
            act.copy(b1T[:, :], bank[3][:, 0:NE * HC]).then_inc(q.b1_done, 1)
            act.wait_ge(q.r_ready, 1)
            act.activation(rp[:, :, :], rl[:, :, :], ACT.Exp).then_inc(q.r_exp, 1)
            for g in range(3):
                w = min(512, NPAD - 512 * g)
                act.wait_ge(q.gt_psum, g + 1)
                act.copy(gateT[:, 512 * g:512 * g + w], bank[4 + g][0:NE, 0:w]).then_inc(q.gt_done, 1)
            act.wait_ge(q.b1_done, 1)
            act.nop().then_inc(q.h_gelu, 4)
            with act.Fori(0, NE) as ex:
                m = 0
                for o, w in NCH:
                    for hc in range(HC):
                        act.wait_ge(q.h_psum, ex * (3 * HC) + m + 1)
                        apart(act)
                        act.activation(G[:, hc, o:o + w], bank[m % 4][:, 0:w], ACT.Gelu_apprx_tanh,
                                       bias=b1T[:, bass.ds(ex * HC + hc, 1)]).then_inc(q.h_gelu, 1)
                        m += 1

        @block.tensor
        def _(pe):
            pe.wait_ge(q.consts, 1)
            with pe.Fori(0, ET // EG) as g:
                pe.wait_ge(q.onehot_lo_ready, g + 1)
                for c in range(EG):
                    mm = nc.tensor.transpose(bf(0)[:, c * P:(c + 1) * P], onehot_lo[:, 0, c, :], identb[:, :])
                mm.then_inc(q.loT_psum, 1)
                pe.wait_ge(q.loT_ready, g + 1)
                for c in range(EG):
                    mm = nc.tensor.matmul(bank[1][:, c * P:(c + 1) * P], onehot_loT[:, bass.ds(g * EG + c, 1), :].rearrange("p a b -> p (a b)"),
                                          onehot_loT[:, bass.ds(g * EG + c, 1), :].rearrange("p a b -> p (a b)"), start=True, stop=True)
                mm.then_inc(q.same_psum, 1)
                pe.wait_ge(q.before_ready, g + 1)
                for c in range(EG):
                    nc.tensor.matmul(bank[2][:, c * NT:(c + 1) * NT], onehot_lo[:, 0, c, :],
                                     onehot_hi[:, bass.ds(g * EG + c, 1), :].rearrange("p a b -> p (a b)"), start=True, stop=True)
                for c in range(EG):
                    mm = nc.tensor.matmul(bank[2][:, (EG + c) * NT:(EG + c + 1) * NT], before[:, 0, c, :],
                                          onehot_hi[:, bass.ds(g * EG + c, 1), :].rearrange("p a b -> p (a b)"), start=True, stop=True)
                mm.then_inc(q.counts_psum, 1)
                pe.wait_ge(q.counts_ready, g + 1)
            pe.wait_ge(q.rowcount_ready, 1)
            nc.tensor.matmul(bank[3][:, 0:NT], low_f[:, :], rows_f[:, :], start=True, stop=True)
            nc.tensor.matmul(bank[3][:, NT:2 * NT], ones_f[:, :], rows_f[:, :], start=True, stop=True).then_inc(q.prefix_psum, 1)
            pe.wait_ge(q.first_ready, 1)
            with pe.Fori(0, ET // LG) as g:
                for c in range(LG):
                    mm = nc.tensor.matmul(bank[4][:, c * 2 * NT:(c + 1) * 2 * NT],
                                          onehot_loT[:, bass.ds(g * LG + c, 1), :].rearrange("p a b -> p (a b)"),
                                          first_b[:, bass.ds(g * LG + c, 1), :, :].rearrange("p a b c -> p (a b c)"), start=True, stop=True)
                mm.then_inc(q.found_psum, 1)
                pe.wait_ge(q.first_ready, g + 2)

            pe.wait_ge(wts["raw"], 16)
            pe.wait_ge(wts["rawo"], 16)
            for g in range(16 + NT):
                if g >= 16:
                    pe.wait_ge(q.xn_ready, g - 15)
                if g >= 2:
                    pe.wait_ge(q.tr_done, g - 1)
                for c in range(KC):
                    if g < 12:
                        a = raw[:, g, c * P:(c + 1) * P]
                    elif g < 16:
                        a = raw_o[:, g - 12, c * P:(c + 1) * P]
                    else:
                        a = xn[g % 2][:, c * P:(c + 1) * P]
                    mm = nc.tensor.transpose(bank[g % 2][:, c * P:(c + 1) * P], a, ident[:, :])
                mm.then_inc(q.tr_psum, 1)
            pe.wait_ge(q.tr_done, 16 + NT)
            pe.wait_ge(wts["wqkv"], 48)

            def project(u, i, w_of):
                if u >= 2:
                    pe.wait_ge(q.unit_done, u - 1)
                for c in range(KC):
                    mm = nc.tensor.matmul(bank[2 + u % 2][:, :], XNT[:, c, i * P:(i + 1) * P], w_of(c), start=c == 0, stop=c == KC - 1)
                mm.then_inc(q.unit_psum, 1)

            for u in range(3 * NT):
                i, w = divmod(u, 3)
                project(u, i, lambda c: Wqkv[:, w, c, :])
            for c in range(KC):
                if c >= 1:
                    pe.wait_ge(q.kt_exp, 3 * c)
                for i, (o, w) in enumerate(NCH):
                    for k in range(KC):
                        mm = nc.tensor.matmul(bank[4 + i][:, 0:w], mixT[:, k, D + c * P:D + (c + 1) * P], XNT[:, k, o:o + w],
                                              start=k == 0, stop=k == KC - 1)
                mm.then_inc(q.kt_psum, 1)
            for i in range(NT):
                project(3 * NT + i, i, lambda c: mixT[:, c, 2 * D:3 * D])
            pe.wait_ge(q.kt_exp, 3 * KC)
            for i in range(NT):
                r = rows_of(i)
                if i >= 2:
                    pe.wait_ge(q.ke_done, i - 1)
                for c in range(KC):
                    mm = nc.tensor.transpose(bank[i % 2][0:r, c * P:(c + 1) * P], KT[:, c, i * P:i * P + r], ident[:, :])
                mm.then_inc(q.ke_psum, 1)
            pe.wait_ge(q.ke_done, NT)
            for i in range(NT + 1):
                if i < NT:
                    project(4 * NT + i, i, lambda c: mixT[:, c, 0:D])
                if i >= 1:
                    pe.wait_ge(q.q_ready, i)
                    if i >= 3:
                        pe.wait_ge(q.qt_done, i - 2)
                    for c in range(KC):
                        mm = nc.tensor.transpose(bank[(i - 1) % 2][:, c * P:(c + 1) * P], qs[(i - 1) % 2][:, c * P:(c + 1) * P], ident[:, :])
                    mm.then_inc(q.qt_psum, 1)
            pe.wait_ge(q.unit_done, 4 * NT)
            for c in range(KC):
                for i in range(NT):
                    r = rows_of(i)
                    mm = nc.tensor.matmul(bank[7][:, c * P:(c + 1) * P], V[0:r, i, c * P:(c + 1) * P], KE[0:r, i, c * P:(c + 1) * P],
                                          start=i == 0, stop=i == NT - 1)
            mm.then_inc(q.ctx_psum, 1)
            pe.wait_ge(q.ctx_ready, 1)
            for c in range(KC):
                if c >= 2:
                    pe.wait_ge(q.m_ready, c - 1)
                nc.tensor.matmul(bank[4 + c % 2][:, :], ctxbd[:, c, :], WoT[:, c, :], start=True, stop=True).then_inc(q.m_psum, 1)
            pe.wait_ge(q.m_ready, KC)
            pe.wait_ge(q.qt_done, NT)
            pe.wait_ge(q.unit_done, UNITS)
            for i in range(NT):
                if i >= 2:
                    pe.wait_ge(q.mix_copied, i - 1)
                for c in range(KC):
                    mm = nc.tensor.matmul(bank[2 + i % 2][:, :], QT[:, c, i * P:(i + 1) * P], Mx[:, c, :], start=c == 0, stop=c == KC - 1)
                mm.then_inc(q.mix_psum, 1)

            pe.wait_ge(q.x_done, 1)
            pe.nop().then_inc(q.y_psum, 1)
            with pe.Fori(0, RT // 2) as n:
                for j in range(2):
                    t = n * 2 + j
                    pe.wait_ge(q.pv_ready, t + 1)
                    pe.wait_ge(q.y_copied, t + 1)
                    for s in range(S):
                        mm = nc.tensor.matmul(bank[j][:, :], ident[:, :], pv[:, s, :], start=s == 0, stop=s == S - 1)
                    mm.then_inc(q.y_psum, 1)
            pe.wait_ge(q.nodes_ready, 1)
            pe.wait_ge(q.y_copied, RT + 2)
            for g in range(MG):
                if g >= 2:
                    pe.wait_ge(q.lt_done, g - 1)
                    pe.wait_ge(q.seg_chunk, g - 1)
                ts = range(4 * g, min(RT, 4 * g + 4))
                for t in ts:
                    nc.tensor.transpose(bank[g % 2][0:HEADS, (t % 4) * P:(t % 4 + 1) * P], rowmax[:, t, :], ident[:, :])
                for t in ts:
                    mm = nc.tensor.transpose(bank[2 + g % 2][0:HEADS, (t % 4) * P:(t % 4 + 1) * P], nodes8[:, t, :], ident[:, :])
                mm.then_inc(q.lt_psum, 1)
            pe.wait_ge(q.m_scan, 1)
            for t in range(RT):
                mm = nc.tensor.transpose(bank[4][:, t * HEADS:(t + 1) * HEADS], LT[:, t * P:(t + 1) * P], ident[0:HEADS, 0:HEADS])
            mm.then_inc(q.m_back, 1)
            with pe.Fori(0, RT // 2) as n:
                for j in range(2):
                    t = n * 2 + j
                    pe.wait_ge(q.onehot_n_ready, t + 1)
                    pe.wait_ge(q.merged, t + 1)
                    for b in range(2):
                        for h in range(2):
                            mm = nc.tensor.matmul(bank[4 * j + 2 * b + h][:, 0:4 * YW], onehot_n[:, j, b * P:(b + 1) * P],
                                                  YR[:, bass.ds(t, 1), 4 * h:4 * h + 4, :].rearrange("p a h d -> p (a h d)"),
                                                  start=True, stop=True)
                    mm.then_inc(q.merge_psum, 1)
            for i in range(NT):
                pe.wait_ge(q.yn_ready, i + 1)
                if i >= 2:
                    pe.wait_ge(q.yt_done, i - 1)
                for c in range(KC):
                    mm = nc.tensor.transpose(bank[i % 2][:, c * P:(c + 1) * P], YN[:, i, c * P:(c + 1) * P], ident[:, :])
                mm.then_inc(q.yt_psum, 1)
            pe.wait_ge(wts["wo"], 16)
            for i in range(NT):
                pe.wait_ge(q.yt_done, i + 1)
                if i >= 2:
                    pe.wait_ge(q.wo_done, i - 1)
                for c in range(KC):
                    mm = nc.tensor.matmul(bank[2 + i % 2][:, :], YT[:, c, i * P:(i + 1) * P], Wo_s[:, c, :], start=c == 0, stop=c == KC - 1)
                mm.then_inc(q.wo_psum, 1)
            for i in range(NT):
                pe.wait_ge(q.h_ready, i + 1)
                if i >= 2:
                    pe.wait_ge(q.ht_done, i - 1)
                for c in range(KC):
                    mm = nc.tensor.transpose(bank[i % 2][:, c * P:(c + 1) * P], hn[i % 2][:, c * P:(c + 1) * P], ident[:, :])
                mm.then_inc(q.ht_psum, 1)
            pe.wait_ge(wts["small"], 48)
            pe.wait_ge(q.wo_done, NT)
            nc.tensor.transpose(bank[3][:, 0:NE * HC], b1raw[:, :], ident[0:NE * HC, 0:NE * HC]).then_inc(q.b1_psum, 1)
            pe.wait_ge(q.ht_done, NT)
            for i in range(NT):
                for c in range(KC):
                    mm = nc.tensor.matmul(bank[2][:, i * NE:(i + 1) * NE], HT[:, c, i * P:(i + 1) * P], Wg_s[:, c, :], start=c == 0, stop=c == KC - 1)
            mm.then_inc(q.r_psum, 1)
            pe.wait_ge(q.gate_ready, 1)
            for i in range(NT):
                mm = nc.tensor.transpose(bank[4 + i // 4][0:NE, (i % 4) * P:(i % 4 + 1) * P], gate[:, i, :], ident[:, :])
                if i % 4 == 3 or i == NT - 1:
                    mm.then_inc(q.gt_psum, 1)
            pe.wait_ge(q.gt_done, 3)
            for i in range(NT):
                if i >= 2:
                    pe.wait_ge(q.gates_added, i - 1)
                nc.tensor.matmul(bank[6 + i % 2][:, :], gateT[:, i * P:(i + 1) * P], b2_s[:, :], start=True, stop=True).then_inc(q.b2_psum, 1)
            pe.wait_ge(q.gates_added, NT)
            pe.wait_ge(q.b1_done, 1)
            with pe.Fori(0, NE // 2) as n:
                for j in range(2):
                    pe.wait_ge(wl[j], n * 32 + 32)
                    m = 0
                    for o, w in NCH:
                        for hc in range(HC):
                            pe.wait_ge(q.h_gelu, n * (2 * 3 * HC) + j * 3 * HC + m + 1)
                            for k in range(KC):
                                mm = nc.tensor.matmul(bank[m % 4][:, 0:w], W1_s[:, j, k, hc * P:(hc + 1) * P], HT[:, k, o:o + w],
                                                      start=k == 0, stop=k == KC - 1)
                            mm.then_inc(q.h_psum, 1)
                            m += 1
                    for i in range(NT):
                        r = rows_of(i)
                        if i % 4 == 0:
                            pe.wait_ge(q.h_gelu, n * (2 * 3 * HC) + j * 3 * HC + (i // 4 + 1) * HC + 4)
                        pe.wait_ge(q.e_done, n * (2 * NT) + j * NT + i + 1)
                        for k in range(HC):
                            mm = nc.tensor.matmul(bank[6 + i % 2][0:r, :], G[:, k, i * P:i * P + r], W2_s[:, j, k, :],
                                                  start=k == 0, stop=k == HC - 1)
                        mm.then_inc(q.e_psum, 1)

        @block.vector
        def _(dve):
            v = Steps(dve, q.dve)
            V_ = nc.vector
            dve.wait_ge(q.consts, 1)
            dve.wait_ge(q.edges_in, 48)
            v.link(V_.tensor_scalar(part_i[:, :], src_i[:, :], P - 1, None, ALU.bitwise_and))
            v.link(V_.tensor_copy(lo_b[:, :], part_i[:, :]))
            v.link(V_.tensor_scalar(part_i[:, :], src_i[:, :], 7, None, ALU.logical_shift_right))
            v.link(V_.tensor_copy(hi_b[:, :], part_i[:, :]))
            v.link(V_.tensor_tensor(onehot_hi[:, :, :], iota10[:, :].unsqueeze(1).broadcast_to([P, ET, NT]),
                                    hi_b[:, :].unsqueeze(2).broadcast_to([P, ET, NT]), ALU.is_equal))
            V_.tensor_copy(records[:, :, 0], dst_i[:, :])
            V_.tensor_copy(records[:, :, 1], src_i[:, :])
            V_.tensor_copy(records[:, :, 2:REC], att[:, :].rearrange("p (t h) -> p t h", h=HEADS)).then_inc(q.records_ready, 1)
            with dve.Fori(0, ET // EG) as g:
                V_.tensor_tensor(onehot_lo[:, 0, :, :], iotab[:, :].unsqueeze(1).broadcast_to([P, EG, P]),
                                 lo_b[:, bass.ds(g * EG, EG)].unsqueeze(2).broadcast_to([P, EG, P]), ALU.is_equal).then_inc(q.onehot_lo_ready, 1)
                dve.wait_ge(q.same_psum, g + 1)
                V_.tensor_tensor(before[:, 0, :, :], bank[1][:, :].rearrange("p (a b) -> p a b", a=EG),
                                 lowb[:, :].unsqueeze(1).broadcast_to([P, EG, P]), ALU.mult).then_inc(q.before_ready, 1)
                dve.wait_ge(q.counts_psum, g + 1)
            dve.wait_ge(q.counts_ready, ET // EG)
            for h in range(NT):
                V_.tensor_tensor_scan(upto[:, :, h], count[:, :, h], zeros_r[:, :], 0.0, ALU.add, ALU.add).then_inc(q.dve, 1)
                v.k += 1
            dve.wait_ge(q.dve, v.done + v.k)
            v.link(V_.tensor_scalar(deg[:, :], upto[:, ET - 1, :], float(S - 1), None, ALU.add))
            v.link(V_.tensor_copy(deg_i[:, :], deg[:, :]))
            v.link(V_.tensor_scalar(deg_i[:, :], deg_i[:, :], S.bit_length() - 1, None, ALU.logical_shift_right))
            v.link(V_.tensor_copy(deg[:, :], deg_i[:, :]))
            V_.tensor_scalar(rows_f[:, :], deg[:, :], 1.0, None, ALU.max).then_inc(q.rowcount_ready, 1)
            v.link(V_.tensor_tensor(first_f[:, :, :], upto[:, :, :], count[:, :, :], ALU.subtract))
            dve.wait_ge(q.prefix_psum, 1)
            v.link(V_.tensor_copy(rows_in[:, :], bank[3][:, 0:NT]))
            v.link(V_.tensor_copy(tot[:, :], bank[3][:, NT:2 * NT]))
            v.link(V_.tensor_tensor_scan(blk0[:, :], tot[:, :], zeros_r[:, 0:NT], 0.0, ALU.add, ALU.add))
            v.link(V_.tensor_tensor(blk0[:, :], blk0[:, :], tot[:, :], ALU.subtract))
            v.link(V_.tensor_tensor(start4[:, :], rows_in[:, :], blk0[:, :], ALU.add))
            v.link(V_.tensor_scalar(start4[:, :], start4[:, :], float(S), None, ALU.mult))
            v.link(V_.tensor_tensor(first_f[:, :, :], first_f[:, :, :], start4[:, :].unsqueeze(1).broadcast_to([P, ET, NT]), ALU.add))
            v.link(V_.tensor_copy(first_i[:, :, :], first_f[:, :, :]))
            v.link(V_.tensor_scalar(halves_i[:, :, :], first_i[:, :, :], 8, None, ALU.logical_shift_right))
            v.link(V_.tensor_copy(first_b[:, :, 0, :], halves_i[:, :, :]))
            v.link(V_.tensor_scalar(halves_i[:, :, :], first_i[:, :, :], 255, None, ALU.bitwise_and))
            v.link(V_.tensor_copy(first_b[:, :, 1, :], halves_i[:, :, :]))
            dve.nop().then_inc(q.first_ready, 1)
            v.link(V_.tensor_tensor(cmp_b[:, :, :], blk0[:, :].unsqueeze(1).broadcast_to([P, RT, NT]),
                                    tile0[:, :].unsqueeze(2).broadcast_to([P, RT, NT]), ALU.is_le))
            v.link(V_.tensor_reduce(block_f[:, :], cmp_b[:, :, :], AX.X, ALU.add))
            v.link(V_.tensor_scalar(block_f[:, :], block_f[:, :], -1.0, None, ALU.add))
            v.link(V_.tensor_scalar(nodebase[:, :], block_f[:, :], float(P), None, ALU.mult))
            v.link(V_.tensor_copy(block_i[:, :], block_f[:, :]))
            v.link(V_.tensor_tensor(within[:, :, :], within[:, :, :], onehot_hi[:, :, :], ALU.mult))
            v.link(V_.tensor_reduce(ranks[:, :], within[:, :, :], AX.X, ALU.add))
            with dve.Fori(0, ET // LG) as g:
                v.enter(g, 1)
                dve.wait_ge(q.found_psum, g + 1)
                v.link(V_.tensor_tensor(found[:, :, :, :], bank[4][:, 0:LG * 2 * NT].rearrange("p (a b c) -> p a b c", a=LG, b=2),
                                        onehot_hi[:, bass.ds(g * LG, LG), :].unsqueeze(2).broadcast_to([P, LG, 2, NT]), ALU.mult))
                V_.tensor_reduce(parts[:, bass.ds(g * LG, LG), :], found[:, :, :, :], AX.X, ALU.add).then_inc(q.first_ready, 1)
            v.leave(ET // LG)
            dve.wait_ge(q.first_ready, 1 + ET // LG)
            v.link(V_.scalar_tensor_tensor(place_f[:, :], parts[:, :, 0], 256.0, parts[:, :, 1], ALU.mult, ALU.add))
            v.link(V_.tensor_tensor(place_f[:, :], place_f[:, :], ranks[:, :], ALU.add))
            dve.wait_ge(q.records_ready, 1)
            v.link(V_.tensor_copy(place_i[:, :], place_f[:, :]))
            dve.nop().then_inc(q.places_ready, 1)

            def norm_stats(of, eps_done):
                for i in range(NT):
                    v.link(V_.bn_stats(stats[:, :], of(i)))
                    v.link(V_.bn_aggr(mv[:, i, :], stats[:, :]))

            dve.wait_ge(q.x_in, 32)
            norm_stats(lambda i: X[:, i, :], None)
            dve.nop().then_inc(q.var_ready, 1)
            dve.wait_ge(q.std_ready, 1)
            v.link(V_.reciprocal(rstd[:, :], rstd[:, :]))
            for i in range(NT):
                if i >= 2:
                    dve.wait_ge(q.tr_psum, 16 + i - 1)
                V_.tensor_scalar(xn[i % 2][:, :], X[:, i, :], mv[:, i, 0:1], rstd[:, i:i + 1], ALU.subtract, ALU.mult).then_inc(q.xn_ready, 1)
            dve.wait_ge(wts["bias"], 80)
            for u in range(3 * NT):
                dve.wait_ge(q.unit_psum, u + 1)
                if u >= 2:
                    dve.wait_ge(sent[u % 2], 16 * (u // 2))
                b = (bias_q, bias_k, bias_v)[u % 3]
                V_.tensor_tensor(send[u % 2][:, :], bank[2 + u % 2][:, :], b[:, :], ALU.add).then_inc(q.send_ready, 1)
                dve.wait_ge(q.send_ready, u + 1)
                dve.nop().then_inc(q.unit_done, 1)
            for c in range(KC):
                dve.wait_ge(q.kt_psum, c + 1)
                for i, (o, w) in enumerate(NCH):
                    v.link(V_.tensor_reduce(kmax3[:, c, i:i + 1], bank[4 + i][:, 0:w], AX.X, ALU.max))
                v.link(V_.tensor_reduce(kneg[:, c:c + 1], kmax3[:, c, :], AX.X, ALU.max))
                v.link(V_.tensor_scalar(kneg[:, c:c + 1], kneg[:, c:c + 1], -1.0, None, ALU.mult))
                dve.nop().then_inc(q.kmax_ready, 1)
            for i in range(NT):
                dve.wait_ge(q.unit_psum, 3 * NT + i + 1)
                V_.tensor_copy(V[:, i, :], bank[2 + i % 2][:, :]).then_inc(q.unit_done, 1)
            dve.wait_ge(q.kt_exp, 3 * KC)
            v.link(V_.tensor_reduce(krec[:, :], ksum3[:, :, :], AX.X, ALU.add))
            v.link(V_.reciprocal(krec[:, :], krec[:, :]))

            def q_finish(i):
                dve.wait_ge(q.q_exp, i + 1)
                t = qs[i % 2][:, :].rearrange("p (h d) -> p h d", h=HEADS)
                v.link(V_.tensor_reduce(qsum[:, :], t, AX.X, ALU.add))
                v.link(V_.reciprocal(qrec[:, :], qsum[:, :]))
                v.link(V_.tensor_scalar(qrec[:, :], qrec[:, :], DK ** -0.5, None, ALU.mult))
                V_.tensor_tensor(t, t, qrec[:, :].unsqueeze(2).broadcast_to([P, HEADS, DK]), ALU.mult).then_inc(q.q_ready, 1)

            for i in range(NT):
                u = 4 * NT + i
                dve.wait_ge(q.unit_psum, u + 1)
                if i >= 2:
                    dve.wait_ge(q.qt_psum, i - 1)
                b = bank[2 + u % 2][:, :].rearrange("p (h d) -> p h d", h=HEADS)
                v.link(V_.tensor_reduce(qmax[:, :], b, AX.X, ALU.max))
                v.link(V_.tensor_tensor(qs[i % 2][:, :].rearrange("p (h d) -> p h d", h=HEADS), b,
                                        qmax[:, :].unsqueeze(2).broadcast_to([P, HEADS, DK]), ALU.subtract))
                dve.nop().then_inc(q.unit_done, 1)
                dve.nop().then_inc(q.q_sub, 1)
                q_finish(i)
            v.link(V_.memset(ctxbd[:, :, :], 0.0))
            dve.wait_ge(q.ctx_psum, 1)
            for h in range(2):
                a = slice(h * DK, (h + 1) * DK)
                v.link(V_.tensor_copy(ctxbd[a, :, a], bank[7][:, :].rearrange("p (c d) -> p c d", c=KC)[a, :, a]))
            dve.nop().then_inc(q.ctx_ready, 1)
            for c in range(KC):
                dve.wait_ge(q.m_psum, c + 1)
                V_.tensor_scalar(Mx[:, c, :], bank[4 + c % 2][:, :], krec[:, c:c + 1], None, ALU.mult).then_inc(q.m_ready, 1)
            dve.wait_ge(q.mix_copied, NT)
            norm_stats(lambda i: mixo[:, i, :], None)
            dve.nop().then_inc(q.mixvar_ready, 1)
            dve.wait_ge(q.mixstd_ready, 1)
            v.link(V_.reciprocal(rstd[:, :], rstd[:, :]))
            for i in range(NT):
                v.link(V_.tensor_scalar(mixo[:, i, :], mixo[:, i, :], mv[:, i, 0:1], rstd[:, i:i + 1], ALU.subtract, ALU.mult))
                v.link(V_.tensor_tensor(mixo[:, i, :], mixo[:, i, :], gamma_b[:, :], ALU.mult))
                v.link(V_.tensor_tensor(X[:, i, :], X[:, i, :], mixo[:, i, :], ALU.add))
            dve.nop().then_inc(q.x_done, 1)

            dve.wait_ge(wts["table"], 16)
            dve.nop().then_inc(q.turn_free, 2)
            with dve.Fori(0, RT // 2) as n:
                v.enter(n, 2 * 8)
                for j in range(2):
                    t = n * 2 + j
                    dve.wait_ge(gath[j], n * (16 * 5) + 16 * 5)
                    v.link(V_.tensor_tensor(prod[:, :, :], KV[:, j, :, 0:D], QG[:, j:j + 1, :].broadcast_to([P, S, D]), ALU.mult))
                    v.link(V_.tensor_reduce(logit[:, j, :, :], prod[:, :, :].rearrange("p s (h d) -> p s h d", h=HEADS), AX.X, ALU.add))
                    v.link(V_.scalar_tensor_tensor(logit[:, j, :, :], logit[:, j, :, :], DK ** -0.5,
                                                   table[:, bass.ds(t, 1), :, 2:REC].rearrange("p a s h -> p (a s) h"), ALU.mult, ALU.add))
                    v.link(V_.tensor_reduce(rowmax[:, bass.ds(t, 1), :].rearrange("p a h -> p (a h)"),
                                            logit[:, j, :, :].rearrange("p s h -> p h s"), AX.X, ALU.max))
                    v.link(V_.tensor_scalar(rowfloor[:, :], rowmax[:, bass.ds(t, 1), :].rearrange("p a h -> p (a h)"), -BIG / 10, None, ALU.max))
                    v.link(V_.tensor_tensor(logit[:, j, :, :], logit[:, j, :, :], rowfloor[:, :].unsqueeze(1).broadcast_to([P, S, HEADS]), ALU.subtract))
                    dve.nop().then_inc(q.logit_ready, 1)
                    dve.wait_ge(q.prob_ready, t + 1)
                    dve.wait_ge(q.y_psum, t + 1)
                    v.link(V_.tensor_tensor(pv[:, :, :].rearrange("p s (h d) -> p s h d", h=HEADS),
                                            KV[:, j, :, D:2 * D].rearrange("p s (h d) -> p s h d", h=HEADS),
                                            prob[:, j, :, :].unsqueeze(3).broadcast_to([P, S, HEADS, DK]), ALU.mult))
                    dve.nop().then_inc(q.pv_ready, 1)
                    dve.nop().then_inc(q.turn_free, 1)
                    v.link(V_.tensor_reduce(YR[:, bass.ds(t, 1), :, DK].rearrange("p a h -> p (a h)"),
                                            prob[:, j, :, :].rearrange("p s h -> p h s"), AX.X, ALU.add))
            v.leave(RT // 2)

            v.link(V_.tensor_copy(nodes8[:, :, :], table[:, :, 0, 1:2].broadcast_to([P, RT, HEADS])))
            v.link(V_.tensor_tensor(node_off[:, :], table[:, :, 0, 1], nodebase[:, :], ALU.subtract))
            dve.nop().then_inc(q.nodes_ready, 1)
            dve.wait_ge(q.y_psum, RT + 1)
            V_.memset(seg[:, RT * P:RT * P + 1], -BIG)
            v.link(V_.memset(nodes_c[:, 0:1], -1.0))
            for g in range(MG):
                w = min(4 * P, RT * P - 4 * P * g)
                dve.wait_ge(q.lt_psum, g + 1)
                V_.tensor_copy(nodes_c[:, 1:w + 1], bank[2 + g % 2][0:HEADS, 0:w]).then_inc(q.seg_chunk, 1)
                dve.wait_ge(q.seg_chunk, g + 1)
                v.link(V_.tensor_tensor(seg[:, 4 * P * g:4 * P * g + w], nodes_c[:, 1:w + 1], nodes_c[:, 0:w], ALU.not_equal))
                v.link(V_.tensor_scalar(seg[:, 4 * P * g:4 * P * g + w], seg[:, 4 * P * g:4 * P * g + w], -BIG, None, ALU.mult))
                v.link(V_.tensor_copy(nodes_c[:, 0:1], nodes_c[:, w:w + 1]))
            dve.wait_ge(q.lt_done, MG)
            v.link(V_.tensor_tensor_scan(LT[:, :], seg[:, 0:RT * P], LT[:, :], -BIG, ALU.add, ALU.max))
            V_.tensor_tensor_scan(LT[:, ::-1], seg[:, 1:RT * P + 1][:, ::-1], LT[:, ::-1], -BIG, ALU.add, ALU.max).then_inc(q.m_scan, 1)
            dve.wait_ge(q.m_back, 1)
            v.link(V_.tensor_scalar(Mrow[:, :, :], bank[4][:, 0:RT * HEADS].rearrange("p (t h) -> p t h", h=HEADS), -BIG / 10, None, ALU.max))
            V_.tensor_tensor(rowmax[:, :, :], rowmax[:, :, :], Mrow[:, :, :], ALU.subtract).then_inc(q.w_ready, 1)
            v.link(V_.memset(Y[:, :, :, :], 0.0))
            dve.wait_ge(q.w_exp, 1)
            dve.nop().then_inc(q.merged, 2)
            with dve.Fori(0, RT // 2) as n:
                v.enter(n, 2 * 2)
                for j in range(2):
                    t = n * 2 + j
                    v.link(V_.tensor_tensor(YR[:, bass.ds(t, 1), :, :].rearrange("p a h d -> p (a h) d"),
                                            YR[:, bass.ds(t, 1), :, :].rearrange("p a h d -> p (a h) d"),
                                            rowmax[:, bass.ds(t, 1), :].rearrange("p a h -> p (a h)").unsqueeze(2).broadcast_to([P, HEADS, YW]), ALU.mult))
                    V_.tensor_scalar(onehot_n[:, j, :], iota256[:, :], node_off[:, bass.ds(t, 1)], None, ALU.is_equal).then_inc(q.onehot_n_ready, 1)
                    blk = dve.value_load(block_i[0:1, bass.ds(t, 1)], min_val=0, max_val=NT - 1)
                    dve.wait_ge(q.merge_psum, t + 1)
                    for b in range(2):
                        y = Y[:, bass.ds(blk + b, 1), :, :].rearrange("p a (g h) d -> p (a g) (h d)", g=2)
                        ins = V_.tensor_tensor(y, y, psum[:, 4 * j + 2 * b:4 * j + 2 * b + 2, 0:4 * YW], ALU.add)
                        if b == 0:
                            v.link(ins)
                        else:
                            ins.then_inc(q.merged, 1)
                            dve.wait_ge(q.merged, t + 3)
            v.leave(RT // 2)
            v.link(V_.tensor_scalar(yden[:, :, :], Y[:, 0:NT, :, DK], 1e-37, None, ALU.max))
            v.link(V_.reciprocal(yden[:, :, :], yden[:, :, :]))
            for i in range(NT):
                V_.tensor_tensor(YN[:, i, :].rearrange("p (h d) -> p h d", h=HEADS), Y[:, i, :, 0:DK],
                                 yden[:, i, :].unsqueeze(2).broadcast_to([P, HEADS, DK]), ALU.mult).then_inc(q.yn_ready, 1)
            for i in range(NT):
                v.link(V_.tensor_tensor(X[:, i, :], X[:, i, :], bias_o[:, :], ALU.add))
            for i in range(NT):
                dve.wait_ge(q.wo_psum, i + 1)
                V_.tensor_tensor(X[:, i, :], X[:, i, :], bank[2 + i % 2][:, :], ALU.add).then_inc(q.wo_done, 1)
            dve.wait_ge(q.wo_done, NT)

            norm_stats(lambda i: X[:, i, :], None)
            dve.nop().then_inc(q.var_ready, 1)
            dve.wait_ge(q.std_ready, 2)
            v.link(V_.reciprocal(rstd[:, :], rstd[:, :]))
            for i in range(NT):
                if i >= 2:
                    dve.wait_ge(q.ht_psum, i - 1)
                V_.tensor_scalar(hn[i % 2][:, :], X[:, i, :], mv[:, i, 0:1], rstd[:, i:i + 1], ALU.subtract, ALU.mult).then_inc(q.h_ready, 1)
            dve.wait_ge(q.r_psum, 1)

            def over(a):
                return a[:, :].unsqueeze(2).broadcast_to([P, NT, NE])

            pos = pos8[:, :].unsqueeze(1).broadcast_to([P, NT, NE])
            rb = bank[2][:, 0:NT * NE].rearrange("p (t e) -> p t e", e=NE)
            v.link(V_.tensor_reduce(r1[:, :], rb, AX.X, ALU.max))
            V_.tensor_tensor(rl[:, :, :], rb, over(r1), ALU.subtract).then_inc(q.r_ready, 1)
            dve.wait_ge(q.r_exp, 1)
            v.link(V_.tensor_reduce(r1[:, :], rp[:, :, :], AX.X, ALU.add))
            v.link(V_.reciprocal(r1[:, :], r1[:, :]))
            v.link(V_.tensor_tensor(rp[:, :, :], rp[:, :, :], over(r1), ALU.mult))
            v.link(V_.tensor_copy(rl[:, :, :], rp[:, :, :]))
            for k in range(2):
                v.link(V_.tensor_reduce(r1[:, :], rl[:, :, :], AX.X, ALU.max))
                v.link(V_.tensor_tensor(rt[:, :, :], rl[:, :, :], over(r1), ALU.is_equal))
                v.link(V_.tensor_scalar(rt[:, :, :], rt[:, :, :], -100.0, 100.0, ALU.mult, ALU.add))
                v.link(V_.tensor_tensor(rt[:, :, :], rt[:, :, :], pos, ALU.add))
                v.link(V_.tensor_reduce(r1[:, :], rt[:, :, :], AX.X, ALU.min))
                v.link(V_.tensor_tensor(rt[:, :, :], over(r1), pos, ALU.is_equal))
                if k == 0:
                    v.link(V_.tensor_copy(pick[:, :, :], rt[:, :, :]))
                    v.link(V_.tensor_scalar(rt[:, :, :], rt[:, :, :], -2.0, None, ALU.mult))
                    v.link(V_.tensor_tensor(rl[:, :, :], rl[:, :, :], rt[:, :, :], ALU.add))
                else:
                    v.link(V_.tensor_tensor(pick[:, :, :], pick[:, :, :], rt[:, :, :], ALU.add))
            V_.tensor_tensor(gate[:, :, :], pick[:, :, :], rp[:, :, :], ALU.mult).then_inc(q.gate_ready, 1)
            dve.wait_ge(q.gate_ready, 1)
            for i in range(NT):
                dve.wait_ge(q.b2_psum, i + 1)
                V_.tensor_tensor(X[:, i, :], X[:, i, :], bank[6 + i % 2][:, :], ALU.add).then_inc(q.gates_added, 1)
            dve.wait_ge(q.gates_added, NT)
            dve.nop().then_inc(q.e_done, 2)
            with dve.Fori(0, NE) as ex:
                for i in range(NT):
                    r = rows_of(i)
                    dve.wait_ge(q.e_psum, ex * NT + i + 1)
                    V_.scalar_tensor_tensor(X[0:r, i, :], bank[6 + i % 2][0:r, :], gate[0:r, i, bass.ds(ex, 1)], X[0:r, i, :],
                                            ALU.mult, ALU.add).then_inc(q.e_done, 1)


def rows_of(i):
    return P if i < NT - 1 else LAST


_INS = ["x", "src", "dst", "edge_attr_8", "L0_gnn_Wq", "L0_gnn_bq", "L0_gnn_Wk", "L0_gnn_bk", "L0_gnn_Wv", "L0_gnn_bv",
        "L0_gnn_Wo", "L0_gnn_bo", "L0_mix_w_qkv", "L0_mix_w_out", "L0_mix_gamma", "L0_ffn_Wg", "L0_ffn_W1", "L0_ffn_b1",
        "L0_ffn_W2", "L0_ffn_b2"]


def kernel(**inputs):
    import concourse.bacc as bacc
    from concourse.bass_utils import run_bass_kernel_spmd

    nc = bacc.Bacc("TRN2", target_bir_lowering=False, num_devices=1)
    arrays, args = {}, []
    for name in _INS:
        a = np.ascontiguousarray(inputs[name])
        arrays[f"in_{name}"] = a
        args.append(nc.dram_tensor(f"in_{name}", a.shape, mybir.dt.from_np(a.dtype), kind="ExternalInput").ap())
    args.append(nc.dram_tensor("out_x", (N, D), F32, kind="ExternalOutput").ap())
    gps_layer(nc, *args)
    r = run_bass_kernel_spmd(nc, [arrays], core_ids=[0])
    return r.results[0]["out_x"]
```

```python
import numpy as np
import concourse.bass as bass
from concourse import mybir
from contextlib import ExitStack

F32, BF16, I32 = mybir.dt.float32, mybir.dt.bfloat16, mybir.dt.int32
ALU, ACT, AX = mybir.AluOpType, mybir.ActivationFunctionType, mybir.AxisListType

P = 128
N, D = 1250, 512
HEADS, DK = 8, 64
E = 20000
NT = (N + P - 1) // P
NPAD = NT * P
LAST = N - (NT - 1) * P
KC = D // P
EPS = 1e-5

EP = 125
ET = E // EP
EG = 4
GROUPS = ET // EG
TURN = 4
KVB = 4
LG = 16
S = 4
ROWS = N + E // S
RT = (ROWS + P - 1) // P
MG = (RT + 3) // 4
REC = 2 + HEADS
BIG = 1e30
NOBODY = 1e6
NONODE = 4096.0
YW = DK + 1

NE, HID = 8, 1024
HC = HID // P
TOPK = 2
XT = (TOPK * N + NE * (P - 1) + NE) // P
HH = HID // 512
NCH = [(0, 512), (512, 512), (1024, N - 1024)]
KB = 1024


class Steps:

    def __init__(self, eng, sem):
        self.eng, self.sem, self.done, self.base, self.k = eng, sem, 0, None, 0

    def link(self, ins):
        ins.then_inc(self.sem, 1)
        self.k += 1
        self.eng.wait_ge(self.sem, self.k + (self.done if self.base is None else self.base))

    def enter(self, n, per_turn):
        self.done += self.k
        self.k, self.per_turn = 0, per_turn
        self.base = n * per_turn + self.done

    def leave(self, turns):
        assert self.k == self.per_turn, self.k
        self.done += turns * self.per_turn
        self.base, self.k = None, 0


def gps_layer(nc, x, src, dst, edge_attr, Wq, bq, Wk, bk, Wv, bv, Wo, bo, w_qkv, w_out, gamma,
              Wg, W1, b1, W2, b2, out):
    ctx = ExitStack()
    with ctx:
        base = ((nc.sbuf_base + 63) // 64) * 64

        def at(name, kb, shape, dt=F32):
            return place(name, shape, dt, base + int(kb * KB))

        def place(name, shape, dt, offset):
            size = int(np.prod(shape[1:])) * mybir.dt.size(dt)
            assert offset + size <= base + 206 * KB, name
            return nc.alloc_sbuf_tensor_at(name, shape, dt, offset=offset)

        def sem(name):
            return ctx.enter_context(nc.semaphore(name))

        ident = at("ident", 0, [P, P])
        low_f = at("low_f", 0.5, [P, P])
        ones_f = at("ones_f", 1, [P, P])
        identb = at("identb", 1.5, [P, P], BF16)
        lowb = at("lowb", 1.75, [P, P], BF16)
        iotab = at("iotab", 2, [P, P], BF16)
        iota256 = at("iota256", 2.25, [P, 2 * P])
        iota_i = at("iota_i", 3.25, [P, 2 * P], I32)
        iota10 = at("iota10", 4.25, [P, NT], BF16)
        tile0 = at("tile0", 4.375, [P, RT])
        tile0_i = at("tile0_i", 4.625, [P, RT], I32)
        zeros_r = at("zeros_r", 4.875, [P, ET])
        eps_c = at("eps_c", 5.5, [P, 1])
        pos8 = at("pos8", 5.5625, [P, NE])
        zero_rows = at("zero_rows", 112, [P, D])
        valid = at("valid", 205.75, [P, NT])
        bias_q = at("bias_q", 6, [P, D])
        bias_k = at("bias_k", 8, [P, D])
        bias_v = at("bias_v", 10, [P, D])
        bias_o = at("bias_o", 12, [P, D])
        gamma_b = at("gamma_b", 14, [P, D])

        X = at("X", 16, [P, NT, D])

        att = at("att", 36, [P, ET * HEADS])
        empty = at("empty", 41, [P, RT * S, REC])
        onehot_lo = at("onehot_lo", 49, [P, TURN, EG, P], BF16)
        before = at("before", 114, [P, 2, EG, P], BF16)
        src_i = at("src_i", 53, [P, ET], I32)
        dst_i = at("dst_i", 53.75, [P, ET], I32)
        part_i = at("part_i", 54.5, [P, ET], I32)
        lo_b = at("lo_b", 55.25, [P, ET], BF16)
        hi_b = at("hi_b", 55.625, [P, ET], BF16)
        records = at("records", 120, [P, ET, REC])
        place_i = at("place_i", 126.25, [P, ET], I32)
        stage_r = [at(f"stage_r{j}", 126.875 + 0.0625 * j, [P, REC]) for j in range(8)]
        stage_i = [at(f"stage_i{j}", 127.375 + 0.0625 * j, [P, 1], I32) for j in range(8)]
        onehot_loT = at("onehot_loT", 128, [P, ET, P], BF16)
        onehot_hi = at("onehot_hi", 168, [P, ET, NT], BF16)
        count = at("count", 172, [P, ET, NT])
        upto = at("upto", 178.5, [P, ET, NT])
        within = at("within", 185, [P, ET, NT])
        first_b = at("first_b", 191.5, [P, ET, 2, NT], BF16)
        first_f = at("first_f", 198, [P, ET, NT])
        first_i = at("first_i", 172, [P, ET, NT], I32)
        halves_i = at("halves_i", 178.5, [P, ET, NT], I32)
        found = at("found", 172, [P, LG, 2, NT])
        parts = at("parts", 174, [P, ET, 2])
        ranks = at("ranks", 176, [P, ET])
        place_f = at("place_f", 177, [P, ET])
        deg = at("deg", 204.5, [P, NT])
        deg_i = at("deg_i", 204.5625, [P, NT], I32)
        rows_f = at("rows_f", 204.625, [P, NT])
        rows_in = at("rows_in", 204.6875, [P, NT])
        blk0 = at("blk0", 204.75, [P, NT])
        start4 = at("start4", 204.8125, [P, NT])
        tot = at("tot", 204.875, [P, NT])
        cmp_b = at("cmp_b", 185, [P, RT, NT])
        block_f = at("block_f", 5.625, [P, RT])
        block_i = at("block_i", 205, [P, RT], I32)
        nodebase = at("nodebase", 205.25, [P, RT])

        XNT = at("XNT", 36, [P, KC, NPAD])
        Wqkv = at("Wqkv", 56, [P, 3, KC, D])
        raw = at("raw", 80, [P, 12, D])
        raw_o = at("raw_o", 104, [P, KC, D])
        WoT = at("WoT", 112, [P, KC, D])
        mixT = at("mixT", 128, [P, KC, 3 * D])
        QT = at("QT", 152, [P, KC, NPAD])
        KT = at("KT", 172, [P, KC, NPAD])
        KE = at("KE", 56, [P, NT, D])
        V = at("V", 80, [P, NT, D])
        Mx = at("Mx", 192, [P, KC, D])
        ctxbd = at("ctxbd", 200, [P, KC, P])
        xn = [at(f"xn{j}", 172 + 2 * j, [P, D]) for j in range(2)]
        qs = [at(f"qs{j}", 76 + 2 * j, [P, D]) for j in range(2)]
        send = [at(f"send{j}", 100 + 2 * j, [P, D]) for j in range(2)]
        mixo = at("mixo", 172, [P, NT, D])
        sm = 202
        stats = at("stats", sm, [P, 6])
        mv = at("mv", sm + 0.0625, [P, NT, 2])
        rstd = at("rstd", sm + 0.1875, [P, NT])
        kmax3 = at("kmax3", sm + 0.25, [P, KC, 3])
        kneg = at("kneg", sm + 0.3125, [P, KC])
        ksum3 = at("ksum3", sm + 0.375, [P, KC, 3])
        krec = at("krec", sm + 0.4375, [P, KC])
        qmax = at("qmax", sm + 0.5, [P, HEADS])
        qsum = at("qsum", sm + 0.5625, [P, HEADS])
        qrec = at("qrec", sm + 0.625, [P, HEADS])

        table = at("table", 36, [P, RT, S, REC])
        YR = at("YR", 44, [P, RT, HEADS, YW])
        kv_at = [148, 166, 184, 16]
        KV = [at(f"KV{b}", kv_at[b], [P, S, 2 * D]) for b in range(KVB)]
        QG = [at(f"QG{b}", kv_at[b] + 16, [P, D]) for b in range(KVB)]
        logit = at("logit", 6, [P, KVB, S, HEADS])
        prob = at("prob", 6.5, [P, KVB, S, HEADS])
        rowmax = at("rowmax", 7, [P, RT, HEADS])
        rowfloor = at("rowfloor", 8.625, [P, HEADS])
        idx = [[at(f"idx{b}_{s}", 8.75 + 0.0625 * (5 * b + s), [P, 1], I32) for s in range(S + 1)] for b in range(KVB)]
        nodes8 = at("nodes8", 145.75, [P, RT, HEADS])
        LT = at("LT", 148, [HEADS, RT * P])
        seg = at("seg", 173.25, [HEADS, RT * P + 1])
        nodes_c = at("nodes_c", 198.4375, [HEADS, 4 * P + 1])
        node_off = at("node_off", 205.5, [P, RT])
        Mrow = at("Mrow", 203.125, [P, RT, HEADS])
        onehot_n = at("onehot_n", 148, [P, 2, 2 * P])
        Y = at("Y", 176, [P, NT + 1, HEADS, YW])
        yden = at("yden", 203.125, [P, NT, HEADS])
        YN = at("YN", 44, [P, NT, D])
        YT = at("YT", 64, [P, KC, NPAD])
        Wo_s = at("Wo_s", 84, [P, KC, D])

        HT = at("HT", 36, [P, KC, NPAD])
        hn = at("hn", 72, [P, NT, D])
        b1_all = at("b1_all", 156, [P, NE, HID])
        b2_all = at("b2_all", 56, [P, NE, D])
        Wg_s = at("Wg_s", 188, [P, KC, NE])
        rl, rp, rt, both, pos_e, before_t, total_t, upto_t = (
            at(n, 189 + 0.375 * i, [P, NT, NE]) for i, n in enumerate(
                ["rl", "rp", "rt", "both", "pos_e", "before_t", "total_t", "upto_t"]))
        pick = at("pick", 192, [P, TOPK, NT, NE])
        picked = at("picked", 192.75, [P, TOPK, NT, NE])
        gate = at("gate", 193.5, [P, TOPK, NT])
        pos_f = at("pos_f", 193.625, [P, TOPK, NT])
        pos_i = at("pos_i", 193.75, [P, TOPK, NT], I32)
        r1 = at("r1", 193.875, [P, NT])
        tiles_f = at("tiles_f", 193.9375, [P, NE])
        tiles_i = at("tiles_i", 194, [P, NE], I32)
        tile_end = at("tile_end", 194.0625, [P, NE])
        tile_end_i = at("tile_end_i", 194.125, [P, NE], I32)
        tile_first = at("tile_first", 194.1875, [P, NE])
        owner_c = at("owner_c", 194.25, [P, XT, NE])
        owner_f = at("owner_f", 195.25, [P, XT])
        owner_i = at("owner_i", 195.375, [P, XT], I32)
        owner_slot = at("owner_slot", 195.5, [P, XT], I32)
        owner_need = at("owner_need", 195.625, [P, XT], I32)
        W1_s = at("W1_s", 92, [P, 2, KC * HID])
        W2_s = at("W2_s", 124, [P, 2, HC * D])
        hrow = at("hrow", 36, [P, 2, D])
        hTt = at("hTt", 40, [P, 2, KC, P])
        hid = at("hid", 44, [P, 2, HID])
        yt = at("yt", 52, [P, 2, D])
        hidT = at("hidT", 196, [P, 1, HC, P])
        back = at("back", 36, [P, 4, D])

        psum = ctx.enter_context(nc.psum_tensor("psum", [P, 8, 512], F32))
        bank = [psum[:, i, :] for i in range(8)]

        def bf(b):
            return bank[b][:, 0:256].bitcast(BF16)

        sent_h = nc.dram_tensor("tokens_by_expert", [XT * P, D], F32, kind="Internal").ap()
        got_y = nc.dram_tensor("expert_rows", [XT * P, D], F32, kind="Internal").ap()
        q_dram = nc.dram_tensor("q_rows", [N, D], F32, kind="Internal").ap()
        x_dram = nc.dram_tensor("residual", [N, D], F32, kind="Internal").ap()
        kv_dram = nc.dram_tensor("kv_rows", [N, 2 * D], F32, kind="Internal").ap()
        table_d = nc.dram_tensor("sorted_edges", [RT * P * S, REC], F32, kind="Internal").ap()

        names = """const_ready consts edges_in pad_ready x_in weights_in empty_ready empty_out onehot_lo_ready
            loT_psum loT_ready same_psum before_ready counts_psum counts_ready first_ready
            rowcount_ready prefix_psum found_psum places_ready staged dve gp se
            xn_ready tr_psum tr_done unit_psum unit_done send_ready kt_psum kmax_ready kt_exp
            ke_psum ke_done q_sub q_exp q_ready qt_psum qt_done ctx_psum ctx_ready m_psum m_ready
            mix_psum mix_copied mixvar_ready mixstd_ready var_ready std_ready
            table_ready kv_zero idx_ready turn_free logit_ready prob_ready pv_ready
            y_psum y_copied lt_psum lt_done nodes_ready seg_chunk m_back m_scan w_ready w_exp
            onehot_n_ready yr_scaled merge_psum merged yn_ready yt_psum yt_done wo_psum wo_done
            x_away x_back zero_ready zero_out den_ready parts_ready weights_asked experts_in tokens_sent th_psum th_ready hid_psum hid_biased hid_ready
            hidT_psum hidT_ready ye_psum ye_ready owners_ready both_ready ranks_psum combined back_zero
            x_done h_ready ht_psum ht_done r_psum r_ready r_exp gate_ready gt_psum gt_done b1_psum b1_done
            b2_psum h_psum h_gelu e_psum e_done out_done dense_psum_free gates_added lt_nodes seg_done sent_q records_ready
            act_passed pool_passed""".split()
        q = {n: sem(n) for n in names}
        scat = [sem(f"scattered{j}") for j in range(8)]
        gath = [sem(f"gathered{j}") for j in range(KVB)]
        sent = [sem(f"sent{j}") for j in range(2)]
        hrow_in = [sem(f"hrow_in{j}") for j in range(2)]
        y_out = [sem(f"y_out{j}") for j in range(2)]
        back_in = [sem(f"back_in{j}") for j in range(4)]
        wts = {n: sem("in_" + n) for n in ("wqkv", "raw", "rawo", "bias", "table", "wo", "wg", "b1", "b2")}
        q = type("Semaphores", (), q)

        block = ctx.enter_context(nc.Block())

        UNITS = 5 * NT

        def in_turns(eng, step):
            for g in range(TURN):
                step(g, g, 0 if g >= 2 else 2 - g, 0)
            with eng.Fori(1, GROUPS // TURN) as n:
                for u in range(TURN):
                    step(n * TURN + u, u, 0, 0)
            for g in range(GROUPS, GROUPS + 2):
                step(g, g % TURN, 0, 1 + g - GROUPS)

        def apart(eng):
            eng.sem_inc(q.act_passed if eng.engine == mybir.EngineType.Activation else q.pool_passed, 1)

        @block.sync
        def _(sp):
            sp.wait_ge(q.pad_ready, 1)
            sp.dma_start(src_i[0:EP, :], src.rearrange("(p t) -> p t", t=ET)).then_inc(q.edges_in, 16)
            sp.dma_start(dst_i[0:EP, :], dst.rearrange("(p t) -> p t", t=ET)).then_inc(q.edges_in, 16)
            sp.dma_start(att[0:EP, :], edge_attr.rearrange("(p t) h -> p (t h)", t=ET)).then_inc(q.edges_in, 16)
            sp.wait_ge(q.pad_ready, 2)
            sp.dma_start(X[:, 0:NT - 1, :], x[0:(NT - 1) * P, :].rearrange("(t p) d -> p t d", p=P)).then_inc(q.x_in, 16)
            sp.dma_start(X[0:LAST, NT - 1, :], x[(NT - 1) * P:N, :]).then_inc(q.x_in, 16)
            sp.dma_start(raw[:, :, :], w_qkv.rearrange("(g p) d -> p g d", p=P)).then_inc(wts["raw"], 16)
            sp.dma_start(raw_o[:, :, :], w_out.rearrange("(g p) d -> p g d", p=P)).then_inc(wts["rawo"], 16)
            for i, w in enumerate((Wq, Wk, Wv)):
                sp.dma_start(Wqkv[:, i, :, :], w.rearrange("(k p) d -> p k d", p=P)).then_inc(wts["wqkv"], 16)
            for t, b in ((bias_q, bq), (bias_k, bk), (bias_v, bv), (bias_o, bo), (gamma_b, gamma)):
                sp.dma_start(t[:, :], b.rearrange("(a d) -> a d", a=1).broadcast_to([P, D])).then_inc(wts["bias"], 16)
            sp.wait_ge(q.empty_ready, 1)
            sp.dma_start(table_d.rearrange("(p r) c -> p (r c)", p=P), empty[:, :, :]).then_inc(q.empty_out, 16)

            sp.wait_ge(q.zero_ready, 1)
            sp.dma_start(sent_h.rearrange("(t p) d -> p t d", p=P), zero_rows[:, :].unsqueeze(1).broadcast_to([P, XT, D])).then_inc(q.zero_out, 16)

            for u in range(3 * NT):
                i, w = divmod(u, 3)
                rows = P if i < NT - 1 else LAST
                to = q_dram[i * P:i * P + rows, :] if w == 0 else kv_dram[i * P:i * P + rows, (w - 1) * D:w * D]
                sp.wait_ge(q.send_ready, u + 1)
                sp.dma_start(to, send[u % 2][0:rows, :]).then_inc(sent[u % 2], 16)

            for j in range(8):
                sp.wait_ge(scat[j], 16 * (ET // 8))
            sp.wait_ge(q.x_done, 1)
            x_parts = ((x_dram[0:(NT - 1) * P, :].rearrange("(t p) d -> p t d", p=P), X[:, 0:NT - 1, :]),
                       (x_dram[(NT - 1) * P:N, :], X[0:LAST, NT - 1, :]))
            for there, here in x_parts:
                sp.dma_start(there, here).then_inc(q.x_away, 16)
            sp.dma_start(table[:, :, :, :], table_d.rearrange("(t p s) c -> p t (s c)", p=P, s=S)
                         .rearrange("p t (s c) -> p t s c", s=S)).then_inc(wts["table"], 16)

            sp.wait_ge(q.y_psum, RT)
            sp.wait_ge(q.x_away, 32)
            for there, here in x_parts:
                sp.dma_start(here, there).then_inc(q.x_back, 16)
            sp.wait_ge(q.merged, RT + 2)
            sp.dma_start(Wo_s[:, :, :], Wo.rearrange("(k p) d -> p k d", p=P)).then_inc(wts["wo"], 16)

            def load_expert(e):
                sp.dma_start(W1_s[:, e % 2, :].rearrange("p (k h) -> p k h", k=KC), W1[e, :, :].rearrange("(k p) h -> p k h", p=P)).then_inc(q.experts_in, 16)
                sp.dma_start(W2_s[:, e % 2, :].rearrange("p (k d) -> p k d", k=HC), W2[e, :, :].rearrange("(k p) d -> p k d", p=P)).then_inc(q.experts_in, 16)
                sp.wait_ge(q.experts_in, 32 * (e + 1))

            load_expert(0)
            load_expert(1)
            sp.wait_ge(q.yn_ready, NT)
            sp.dma_start(b1_all[:, :, :], b1.rearrange("(a e) h -> a e h", a=1).broadcast_to([P, NE, HID])).then_inc(wts["b1"], 16)
            sp.dma_start(Wg_s[:, :, :], Wg.rearrange("(k p) e -> p k e", p=P)).then_inc(wts["wg"], 16)
            sp.wait_ge(q.wo_psum, NT)
            sp.dma_start(b2_all[:, :, :], b2.rearrange("(a e) d -> a e d", a=1).broadcast_to([P, NE, D])).then_inc(wts["b2"], 16)
            sp.wait_ge(q.owners_ready, 1)
            for e in range(2, NE):
                last = sp.value_load(tile_end_i[0:1, e - 2:e - 1], min_val=1, max_val=XT)
                sp.wait_ge(q.ye_psum, last)
                load_expert(e)
            for i in range(NT):
                sp.wait_ge(q.combined, TOPK * (i + 1))
                sp.dma_start(out[i * P:i * P + rows_of(i), :], X[0:rows_of(i), i, :]).then_inc(q.out_done, 16)
            sp.wait_ge(q.out_done, 16 * NT)

        @block.gpsimd
        def _(gp):
            st = Steps(gp, q.gp)
            gp.memset(dst_i[:, :], 0)
            gp.memset(att[:, :], 0.0)
            gp.memset(src_i[:, :], 1 << 20).then_inc(q.pad_ready, 1)
            gp.memset(X[:, NT - 1, :], 0.0).then_inc(q.pad_ready, 1)
            for m in (ident, identb):
                st.link(gp.memset(m[:, :], 0.0))
                st.link(gp.affine_select(out=m[:, :], in_=m[:, :], compare_op=ALU.not_equal, fill=1.0, base=0,
                                         pattern=[[-1, P]], channel_multiplier=1))
            for m in (low_f, lowb):
                st.link(gp.memset(m[:, :], 0.0))
                st.link(gp.affine_select(out=m[:, :], in_=m[:, :], compare_op=ALU.is_ge, fill=1.0, base=0,
                                         pattern=[[-1, P]], channel_multiplier=1))
            gp.memset(ones_f[:, :], 1.0)
            gp.memset(zeros_r[:, :], 0.0)
            gp.memset(eps_c[:, :], EPS)
            st.link(gp.iota(iota_i[:, :], pattern=[[1, 2 * P]], base=0, channel_multiplier=0))
            st.link(gp.iota(tile0_i[:, :], pattern=[[P, RT]], base=0, channel_multiplier=0))
            gp.tensor_copy(tile0[:, :], tile0_i[:, :])
            gp.tensor_copy(iota256[:, :], iota_i[:, :])
            gp.tensor_copy(pos8[:, :], iota_i[:, 0:NE])
            gp.tensor_copy(iota10[:, :], iota_i[:, 0:NT])
            gp.tensor_copy(iotab[:, :], iota_i[:, 0:P]).then_inc(q.consts, 1)
            gp.memset(zero_rows[:, :], 0.0).then_inc(q.zero_ready, 1)
            st.link(gp.memset(valid[:, :], 1.0))
            st.link(gp.affine_select(out=valid[:, :], in_=valid[:, :], compare_op=ALU.is_ge, fill=0.0, base=N - 1,
                                     pattern=[[-P, NT]], channel_multiplier=-1))
            gp.memset(empty[:, :, 0:1], NOBODY)
            gp.memset(empty[:, :, 1:2], NONODE)
            gp.memset(empty[:, :, 2:REC], -BIG).then_inc(q.empty_ready, 1)

            gp.wait_ge(q.places_ready, 1)
            gp.wait_ge(q.empty_out, 16)
            with gp.Fori(0, ET // 8) as n:
                for j in range(8):
                    t = n * 8 + j
                    gp.tensor_copy(stage_i[j][:, :], place_i[:, bass.ds(t, 1)])
                    gp.tensor_copy(stage_r[j][:, :], records[:, bass.ds(t, 1), :]).then_inc(q.staged, 1)
                    gp.wait_ge(q.staged, t + 1)
                    apart(gp)
                    gp.indirect_dma_start(table_d, bass.IndirectOffsetOnAxis(ap=stage_i[j][0:EP, :], axis=0),
                                          stage_r[j][0:EP, :], None,
                                          bounds_check=RT * P * S - 1, oob_is_err=False).then_inc(scat[j], 16)
                for j in range(8):
                    gp.wait_ge(scat[j], n * 16 + 16)
                    apart(gp)

            gp.wait_ge(q.x_done, 1)
            gp.wait_ge(q.x_away, 32)
            for b in range(KVB):
                gp.memset(QG[b][:, :], 0.0)
                gp.memset(KV[b][:, :, :], 0.0).then_inc(q.kv_zero, 1)
            gp.wait_ge(q.kv_zero, KVB)
            gp.wait_ge(wts["table"], 16)
            for j in range(2):
                gp.wait_ge(sent[j], 16 * (3 * NT // 2))

            def gather(t, b):
                for s in range(S):
                    gp.tensor_copy(idx[b][s][:, :], table[:, bass.ds(t, 1), s, 0])
                gp.tensor_copy(idx[b][S][:, :], table[:, bass.ds(t, 1), 0, 1]).then_inc(q.idx_ready, 1)
                gp.wait_ge(q.idx_ready, t + 1)
                apart(gp)
                gp.indirect_dma_start(QG[b][:, :], None, q_dram,
                                      bass.IndirectOffsetOnAxis(ap=idx[b][S][:, :], axis=0),
                                      bounds_check=N - 1, oob_is_err=False).then_inc(gath[b], 16)
                for s in range(S):
                    gp.indirect_dma_start(KV[b][:, s, :], None, kv_dram,
                                          bass.IndirectOffsetOnAxis(ap=idx[b][s][:, :], axis=0),
                                          bounds_check=N - 1, oob_is_err=False).then_inc(gath[b], 16)

            for t in range(KVB):
                gather(t, t)
            with gp.Fori(0, (RT - KVB) // KVB) as n:
                for u in range(KVB):
                    gp.wait_ge(q.y_psum, n * KVB + u + 1)
                    apart(gp)
                    gather(n * KVB + u + KVB, u)
            for t in range(RT // KVB * KVB, RT):
                gp.wait_ge(q.y_psum, t - KVB + 1)
                gather(t, t % KVB)

            gp.wait_ge(q.w_exp, 1)
            with gp.Fori(0, RT) as t:
                y = YR[:, bass.ds(t, 1), :, :].rearrange("p a h d -> p (a h) d")
                gp.tensor_tensor(y, y, rowmax[:, bass.ds(t, 1), :].rearrange("p a h -> p (a h)").unsqueeze(2)
                                 .broadcast_to([P, HEADS, YW]), ALU.mult).then_inc(q.yr_scaled, 1)

            gp.wait_ge(q.owners_ready, 1)
            for i in range(NT):
                for k in range(TOPK):
                    gp.indirect_dma_start(sent_h, bass.IndirectOffsetOnAxis(ap=pos_i[:, k, i:i + 1], axis=0), hn[:, i, :], None,
                                          bounds_check=XT * P - 1, oob_is_err=False).then_inc(q.tokens_sent, 16)
            gp.wait_ge(q.tokens_sent, 16 * NT * TOPK)

            def load_rows(i, b):
                gp.dma_start(hrow[:, b, :], sent_h.rearrange("(t p) d -> p t d", p=P)[:, bass.ds(i, 1), :]
                             .rearrange("p a d -> p (a d)")).then_inc(hrow_in[b], 16)

            def store_rows(i, b):
                gp.dma_start(got_y.rearrange("(t p) d -> p t d", p=P)[:, bass.ds(i, 1), :]
                             .rearrange("p a d -> p (a d)"), yt[:, b, :]).then_inc(y_out[b], 16)

            load_rows(0, 0)
            load_rows(1, 1)
            with gp.Fori(0, (XT - 3) // 2) as n:
                for u in range(2):
                    gp.wait_ge(q.th_psum, n * 2 + u + 1)
                    apart(gp)
                    load_rows(n * 2 + u + 2, u)
                    gp.wait_ge(q.ye_ready, n * 2 + u + 3)
                    apart(gp)
                    store_rows(n * 2 + u, u)
            for i in range(XT - 3, XT):
                if i + 2 < XT:
                    gp.wait_ge(q.th_psum, i + 1)
                    load_rows(i + 2, i % 2)
                gp.wait_ge(q.ye_ready, i + 3)
                store_rows(i, i % 2)
            gp.wait_ge(y_out[0], 16 * ((XT + 1) // 2))
            gp.wait_ge(y_out[1], 16 * (XT // 2))
            gp.memset(back[:, :, :], 0.0).then_inc(q.back_zero, 1)
            gp.wait_ge(q.back_zero, 1)
            for m in range(NT * TOPK):
                i, k = divmod(m, TOPK)
                if m >= 4:
                    gp.wait_ge(q.combined, m - 3)
                gp.indirect_dma_start(back[:, m % 4, :], None, got_y, bass.IndirectOffsetOnAxis(ap=pos_i[:, k, i:i + 1], axis=0),
                                      bounds_check=XT * P - 1, oob_is_err=False).then_inc(back_in[m % 4], 16)

        @block.scalar
        def _(act):
            def sort_act(g, u, first, last):
                if not last:
                    act.wait_ge(q.loT_psum, g + 1)
                    apart(act)
                    act.copy(onehot_loT[:, bass.ds(g * EG, EG), :], bf(u % 2).rearrange("p (a b) -> p a b", a=EG)).then_inc(q.loT_ready, 1)
                if not first:
                    act.wait_ge(q.counts_psum, g - 1)
                    apart(act)
                    bk = bank[4 + u % 2]
                    act.copy(count[:, bass.ds((g - 2) * EG, EG), :], bk[:, 0:EG * NT].rearrange("p (a b) -> p a b", a=EG))
                    act.copy(within[:, bass.ds((g - 2) * EG, EG), :],
                             bk[:, EG * NT:2 * EG * NT].rearrange("p (a b) -> p a b", a=EG)).then_inc(q.counts_ready, 1)

            in_turns(act, sort_act)

            act.wait_ge(q.places_ready, 1)
            act.wait_ge(q.empty_out, 16)
            act.wait_ge(q.zero_out, 16)
            for g in range(16 + NT):
                if g == 16:
                    act.wait_ge(q.var_ready, 1)
                    act.activation(rstd[:, :], mv[:, :, 1], ACT.Sqrt, bias=eps_c[:, :]).then_inc(q.std_ready, 1)
                act.wait_ge(q.tr_psum, g + 1)
                if g < 12:
                    to = mixT[:, :, g * P:(g + 1) * P]
                elif g < 16:
                    to = WoT[:, :, (g - 12) * P:(g - 11) * P]
                else:
                    to = XNT[:, :, (g - 16) * P:(g - 15) * P]
                act.copy(to, bank[g % 2][:, :].rearrange("p (a b) -> p a b", a=KC)).then_inc(q.tr_done, 1)
            for c in range(KC):
                act.wait_ge(q.kmax_ready, c + 1)
                for i, (o, w) in enumerate(NCH):
                    act.activation(KT[:, c, o:o + w], bank[4 + i][:, 0:w], ACT.Exp, bias=kneg[:, c:c + 1],
                                   accum_out=ksum3[:, c, i:i + 1]).then_inc(q.kt_exp, 1)
            for i in range(NT):
                act.wait_ge(q.ke_psum, i + 1)
                act.copy(KE[0:rows_of(i), i, :], bank[i % 2][0:rows_of(i), :]).then_inc(q.ke_done, 1)
            for i in range(NT):
                act.wait_ge(q.q_sub, i + 1)
                act.activation(qs[i % 2][:, :], qs[i % 2][:, :], ACT.Exp).then_inc(q.q_exp, 1)
                if i >= 1:
                    act.wait_ge(q.qt_psum, i)
                    act.copy(QT[:, :, (i - 1) * P:i * P], bank[(i - 1) % 2][:, :].rearrange("p (a b) -> p a b", a=KC)).then_inc(q.qt_done, 1)
            act.wait_ge(q.qt_psum, NT)
            act.copy(QT[:, :, (NT - 1) * P:NPAD], bank[(NT - 1) % 2][:, :].rearrange("p (a b) -> p a b", a=KC)).then_inc(q.qt_done, 1)
            for i in range(NT):
                act.wait_ge(q.mix_psum, i + 1)
                act.copy(mixo[:, i, :], bank[2 + i % 2][:, :]).then_inc(q.mix_copied, 1)
            act.wait_ge(q.mixvar_ready, 1)
            act.activation(rstd[:, :], mv[:, :, 1], ACT.Sqrt, bias=eps_c[:, :]).then_inc(q.mixstd_ready, 1)

            act.wait_ge(q.x_done, 1)
            act.nop().then_inc(q.y_copied, KVB)

            def exp_rows(t, b):
                act.wait_ge(q.logit_ready, t + 1)
                act.activation(prob[:, b, :, :], logit[:, b, :, :], ACT.Exp).then_inc(q.prob_ready, 1)

            def copy_rows(t, b):
                act.wait_ge(q.y_psum, t + 1)
                apart(act)
                act.copy(YR[:, bass.ds(t, 1), :, 0:DK],
                         bank[b][:, :].rearrange("p (a h d) -> p a h d", a=1, h=HEADS)).then_inc(q.y_copied, 1)

            exp_rows(0, 0)
            with act.Fori(0, RT // KVB) as n:
                for u in range(KVB):
                    exp_rows(n * KVB + u + 1, (u + 1) % KVB)
                    copy_rows(n * KVB + u, u)
            copy_rows(RT - 1, (RT - 1) % KVB)
            for g in range(MG):
                w = min(4 * P, RT * P - 4 * P * g)
                act.wait_ge(q.lt_psum, g + 1)
                act.copy(LT[:, 4 * P * g:4 * P * g + w], bank[g % 2][0:HEADS, 0:w]).then_inc(q.lt_done, 1)
            act.wait_ge(q.w_ready, 1)
            act.activation(rowmax[:, :, :], rowmax[:, :, :], ACT.Exp).then_inc(q.w_exp, 1)
            for i in range(NT):
                act.wait_ge(q.yt_psum, i + 1)
                act.copy(YT[:, :, i * P:(i + 1) * P], bank[i % 2][:, :].rearrange("p (a b) -> p a b", a=KC)).then_inc(q.yt_done, 1)
            act.wait_ge(q.var_ready, 2)
            act.activation(rstd[:, :], mv[:, :, 1], ACT.Sqrt, bias=eps_c[:, :]).then_inc(q.std_ready, 1)
            for i in range(NT):
                act.wait_ge(q.ht_psum, i + 1)
                act.copy(HT[:, :, i * P:(i + 1) * P], bank[i % 2][:, :].rearrange("p (a b) -> p a b", a=KC)).then_inc(q.ht_done, 1)
            act.wait_ge(q.r_ready, 1)
            act.activation(rp[:, :, :], rl[:, :, :], ACT.Exp).then_inc(q.r_exp, 1)

            def copy_tokens(i, b):
                act.wait_ge(q.th_psum, i + 1)
                act.copy(hTt[:, b, :, :], bank[0][:, :].rearrange("p (a b) -> p a b", a=KC)).then_inc(q.th_ready, 1)

            def expert_tile(i, b, last=False):
                act.wait_ge(q.hid_biased, i + 1)
                act.activation(hid[:, b, :], hid[:, b, :], ACT.Gelu_apprx_tanh).then_inc(q.hid_ready, 1)
                if not last:
                    copy_tokens(i + 1, 1 - b)
                act.wait_ge(q.hidT_psum, i + 1)
                act.copy(hidT[:, 0, :, :], psum[:, 3:5, :].rearrange("p a (c n) -> p (a c) n", c=4)).then_inc(q.hidT_ready, 1)

            copy_tokens(0, 0)
            with act.Fori(0, (XT - 1) // 2) as n:
                for u in range(2):
                    expert_tile(n * 2 + u, u)
            expert_tile(XT - 1, (XT - 1) % 2, last=True)

        @block.tensor
        def _(pe):
            pe.wait_ge(q.consts, 1)

            def sort_pe(g, u, first, last):
                if not last:
                    pe.wait_ge(q.onehot_lo_ready, g + 1)
                    for c in range(EG):
                        mm = nc.tensor.transpose(bf(u % 2)[:, c * P:(c + 1) * P], onehot_lo[:, u, c, :], identb[:, :])
                    mm.then_inc(q.loT_psum, 1)
                if first != 2 and last != 2:
                    pe.wait_ge(q.loT_ready, g)
                    for c in range(EG):
                        t = bass.ds((g - 1) * EG + c, 1)
                        mm = nc.tensor.matmul(bank[2 + (u - 1) % 2][:, c * P:(c + 1) * P], onehot_loT[:, t, :].rearrange("p a b -> p (a b)"),
                                              onehot_loT[:, t, :].rearrange("p a b -> p (a b)"), start=True, stop=True)
                    mm.then_inc(q.same_psum, 1)
                if not first:
                    pe.wait_ge(q.before_ready, g - 1)
                    if not isinstance(g, int) or g >= 4:
                        pe.wait_ge(q.counts_ready, g - 3)
                    for lhs, off in ((onehot_lo[:, (u - 2) % TURN, :, :], 0), (before[:, u % 2, :, :], EG)):
                        for c in range(EG):
                            mm = nc.tensor.matmul(bank[4 + u % 2][:, (off + c) * NT:(off + c + 1) * NT], lhs[:, c, :],
                                                  onehot_hi[:, bass.ds((g - 2) * EG + c, 1), :].rearrange("p a b -> p (a b)"),
                                                  start=True, stop=True)
                    mm.then_inc(q.counts_psum, 1)

            in_turns(pe, sort_pe)
            pe.wait_ge(q.rowcount_ready, 1)
            nc.tensor.matmul(bank[3][:, 0:NT], low_f[:, :], rows_f[:, :], start=True, stop=True)
            nc.tensor.matmul(bank[3][:, NT:2 * NT], ones_f[:, :], rows_f[:, :], start=True, stop=True).then_inc(q.prefix_psum, 1)
            pe.wait_ge(q.first_ready, 1)

            def look_up(g, b):
                for c in range(LG):
                    mm = nc.tensor.matmul(bank[6 + b][:, c * 2 * NT:(c + 1) * 2 * NT],
                                          onehot_loT[:, bass.ds(g * LG + c, 1), :].rearrange("p a b -> p (a b)"),
                                          first_b[:, bass.ds(g * LG + c, 1), :, :].rearrange("p a b c -> p (a b c)"), start=True, stop=True)
                mm.then_inc(q.found_psum, 1)

            look_up(0, 0)
            look_up(1, 1)
            with pe.Fori(0, ET // LG // 2 - 1) as n:
                for b in range(2):
                    pe.wait_ge(q.parts_ready, n * 2 + b + 1)
                    look_up(n * 2 + b + 2, b)

            pe.wait_ge(wts["raw"], 16)
            pe.wait_ge(wts["rawo"], 16)
            for g in range(16 + NT):
                if g >= 16:
                    pe.wait_ge(q.xn_ready, g - 15)
                if g >= 2:
                    pe.wait_ge(q.tr_done, g - 1)
                for c in range(KC):
                    if g < 12:
                        a = raw[:, g, c * P:(c + 1) * P]
                    elif g < 16:
                        a = raw_o[:, g - 12, c * P:(c + 1) * P]
                    else:
                        a = xn[g % 2][:, c * P:(c + 1) * P]
                    mm = nc.tensor.transpose(bank[g % 2][:, c * P:(c + 1) * P], a, ident[:, :])
                mm.then_inc(q.tr_psum, 1)
            pe.wait_ge(q.tr_done, 16 + NT)
            pe.wait_ge(wts["wqkv"], 48)

            def project(u, i, w_of):
                if u >= 2:
                    pe.wait_ge(q.unit_done, u - 1)
                for c in range(KC):
                    mm = nc.tensor.matmul(bank[2 + u % 2][:, :], XNT[:, c, i * P:(i + 1) * P], w_of(c), start=c == 0, stop=c == KC - 1)
                mm.then_inc(q.unit_psum, 1)

            for u in range(3 * NT):
                i, w = divmod(u, 3)
                project(u, i, lambda c: Wqkv[:, w, c, :])
            for c in range(KC):
                if c >= 1:
                    pe.wait_ge(q.kt_exp, 3 * c)
                for i, (o, w) in enumerate(NCH):
                    for k in range(KC):
                        mm = nc.tensor.matmul(bank[4 + i][:, 0:w], mixT[:, k, D + c * P:D + (c + 1) * P], XNT[:, k, o:o + w],
                                              start=k == 0, stop=k == KC - 1)
                mm.then_inc(q.kt_psum, 1)
            for i in range(NT):
                project(3 * NT + i, i, lambda c: mixT[:, c, 2 * D:3 * D])
            pe.wait_ge(q.kt_exp, 3 * KC)
            for i in range(NT):
                r = rows_of(i)
                if i >= 2:
                    pe.wait_ge(q.ke_done, i - 1)
                for c in range(KC):
                    mm = nc.tensor.transpose(bank[i % 2][0:r, c * P:(c + 1) * P], KT[:, c, i * P:i * P + r], ident[:, :])
                mm.then_inc(q.ke_psum, 1)
            pe.wait_ge(q.ke_done, NT)
            for i in range(NT + 1):
                if i < NT:
                    project(4 * NT + i, i, lambda c: mixT[:, c, 0:D])
                if i >= 1:
                    pe.wait_ge(q.q_ready, i)
                    if i >= 3:
                        pe.wait_ge(q.qt_done, i - 2)
                    for c in range(KC):
                        mm = nc.tensor.transpose(bank[(i - 1) % 2][:, c * P:(c + 1) * P], qs[(i - 1) % 2][:, c * P:(c + 1) * P], ident[:, :])
                    mm.then_inc(q.qt_psum, 1)
            pe.wait_ge(q.unit_done, 4 * NT)
            for c in range(KC):
                for i in range(NT):
                    r = rows_of(i)
                    mm = nc.tensor.matmul(bank[7][:, c * P:(c + 1) * P], V[0:r, i, c * P:(c + 1) * P], KE[0:r, i, c * P:(c + 1) * P],
                                          start=i == 0, stop=i == NT - 1)
            mm.then_inc(q.ctx_psum, 1)
            pe.wait_ge(q.ctx_ready, 1)
            for c in range(KC):
                if c >= 2:
                    pe.wait_ge(q.m_ready, c - 1)
                nc.tensor.matmul(bank[4 + c % 2][:, :], ctxbd[:, c, :], WoT[:, c, :], start=True, stop=True).then_inc(q.m_psum, 1)
            pe.wait_ge(q.m_ready, KC)
            pe.wait_ge(q.qt_done, NT)
            pe.wait_ge(q.unit_done, UNITS)
            for i in range(NT):
                if i >= 2:
                    pe.wait_ge(q.mix_copied, i - 1)
                for c in range(KC):
                    mm = nc.tensor.matmul(bank[2 + i % 2][:, :], QT[:, c, i * P:(i + 1) * P], Mx[:, c, :], start=c == 0, stop=c == KC - 1)
                mm.then_inc(q.mix_psum, 1)

            pe.wait_ge(q.x_done, 1)

            def sum_rows(t, b):
                pe.wait_ge(q.pv_ready, t + 1)
                pe.wait_ge(q.y_copied, t + 1)
                for s in range(S):
                    mm = nc.tensor.matmul(bank[b][:, :], ident[:, :], KV[b][:, s, D:2 * D], start=s == 0, stop=s == S - 1)
                mm.then_inc(q.y_psum, 1)

            with pe.Fori(0, RT // KVB) as n:
                for u in range(KVB):
                    sum_rows(n * KVB + u, u)
            for t in range(RT // KVB * KVB, RT):
                sum_rows(t, t % KVB)
            pe.wait_ge(q.nodes_ready, 1)
            pe.wait_ge(q.y_copied, RT + KVB)
            for g in range(MG):
                if g >= 2:
                    pe.wait_ge(q.lt_done, g - 1)
                    pe.wait_ge(q.seg_chunk, g - 1)
                ts = range(4 * g, min(RT, 4 * g + 4))
                for t in ts:
                    nc.tensor.transpose(bank[g % 2][0:HEADS, (t % 4) * P:(t % 4 + 1) * P], rowmax[:, t, :], ident[:, :])
                for t in ts:
                    mm = nc.tensor.transpose(bank[2 + g % 2][0:HEADS, (t % 4) * P:(t % 4 + 1) * P], nodes8[:, t, :], ident[:, :])
                mm.then_inc(q.lt_psum, 1)
            pe.wait_ge(q.m_scan, 1)
            for t in range(RT):
                mm = nc.tensor.transpose(bank[4][:, t * HEADS:(t + 1) * HEADS], LT[:, t * P:(t + 1) * P], ident[0:HEADS, 0:HEADS])
            mm.then_inc(q.m_back, 1)

            def merge(t, j):
                pe.wait_ge(q.onehot_n_ready, t + 1)
                pe.wait_ge(q.yr_scaled, t + 1)
                pe.wait_ge(q.merged, t + 1)
                for b in range(2):
                    for h in range(2):
                        mm = nc.tensor.matmul(bank[4 * j + 2 * b + h][:, 0:4 * YW], onehot_n[:, j, b * P:(b + 1) * P],
                                              YR[:, bass.ds(t, 1), 4 * h:4 * h + 4, :].rearrange("p a h d -> p (a h d)"),
                                              start=True, stop=True)
                mm.then_inc(q.merge_psum, 1)

            with pe.Fori(0, RT // 2) as n:
                for j in range(2):
                    merge(n * 2 + j, j)
            merge(RT - 1, 0)
            for i in range(NT):
                pe.wait_ge(q.yn_ready, i + 1)
                if i >= 2:
                    pe.wait_ge(q.yt_done, i - 1)
                for c in range(KC):
                    mm = nc.tensor.transpose(bank[i % 2][:, c * P:(c + 1) * P], YN[:, i, c * P:(c + 1) * P], ident[:, :])
                mm.then_inc(q.yt_psum, 1)
            pe.wait_ge(wts["wo"], 16)
            for i in range(NT):
                pe.wait_ge(q.yt_done, i + 1)
                if i >= 2:
                    pe.wait_ge(q.wo_done, i - 1)
                for c in range(KC):
                    mm = nc.tensor.matmul(bank[2 + i % 2][:, :], YT[:, c, i * P:(i + 1) * P], Wo_s[:, c, :], start=c == 0, stop=c == KC - 1)
                mm.then_inc(q.wo_psum, 1)
            for i in range(NT):
                pe.wait_ge(q.h_ready, i + 1)
                if i >= 2:
                    pe.wait_ge(q.ht_done, i - 1)
                for c in range(KC):
                    mm = nc.tensor.transpose(bank[i % 2][:, c * P:(c + 1) * P], hn[:, i, c * P:(c + 1) * P], ident[:, :])
                mm.then_inc(q.ht_psum, 1)
            pe.wait_ge(wts["wg"], 16)
            pe.wait_ge(q.wo_done, NT)
            pe.wait_ge(q.ht_done, NT)
            for i in range(NT):
                for c in range(KC):
                    mm = nc.tensor.matmul(bank[2][:, i * NE:(i + 1) * NE], HT[:, c, i * P:(i + 1) * P], Wg_s[:, c, :], start=c == 0, stop=c == KC - 1)
            mm.then_inc(q.r_psum, 1)
            pe.wait_ge(q.both_ready, 1)
            nc.tensor.matmul(bank[3][:, 0:NT * NE], low_f[:, :], both[:, :, :].rearrange("p t e -> p (t e)"), start=True, stop=True)
            nc.tensor.matmul(bank[4][:, 0:NT * NE], ones_f[:, :], both[:, :, :].rearrange("p t e -> p (t e)"), start=True, stop=True).then_inc(q.ranks_psum, 1)
            pe.wait_ge(q.owners_ready, 1)

            def transpose_tokens(b, count):
                pe.wait_ge(hrow_in[b], count)
                for c in range(KC):
                    mm = nc.tensor.transpose(bank[0][:, c * P:(c + 1) * P], hrow[:, b, c * P:(c + 1) * P], ident[:, :])
                mm.then_inc(q.th_psum, 1)

            def up(i, b):
                slot = pe.value_load(owner_slot[0:1, bass.ds(i, 1)], min_val=0, max_val=1)
                need = pe.value_load(owner_need[0:1, bass.ds(i, 1)], min_val=32, max_val=32 * NE)
                pe.wait_ge(q.experts_in, need)
                pe.wait_ge(q.th_ready, i + 1)
                for h in range(HH):
                    for c in range(KC):
                        mm = nc.tensor.matmul(bank[1 + h][:, :], hTt[:, b, c, :],
                                              W1_s[:, bass.ds(slot, 1), c * HID + h * 512:c * HID + (h + 1) * 512].rearrange("p a n -> p (a n)"),
                                              start=c == 0, stop=c == KC - 1)
                mm.then_inc(q.hid_psum, 1)
                return slot

            def down(i, b):
                slot = pe.value_load(owner_slot[0:1, bass.ds(i, 1)], min_val=0, max_val=1)
                pe.wait_ge(q.hidT_ready, i + 1)
                pe.wait_ge(q.ye_ready, i + 1)
                for c in range(HC):
                    mm = nc.tensor.matmul(bank[5 + b][:, :], hidT[:, 0, c, :],
                                          W2_s[:, bass.ds(slot, 1), c * D:(c + 1) * D].rearrange("p a n -> p (a n)"),
                                          start=c == 0, stop=c == HC - 1)
                mm.then_inc(q.ye_psum, 1)

            def transpose_hidden(i, b):
                pe.wait_ge(q.hid_ready, i + 1)
                for c in range(HC):
                    mm = nc.tensor.transpose(bank[3 + c // 4][:, (c % 4) * P:(c % 4 + 1) * P], hid[:, b, c * P:(c + 1) * P], ident[:, :])
                mm.then_inc(q.hidT_psum, 1)

            transpose_tokens(0, 16)
            up(0, 0)
            transpose_tokens(1, 16)
            transpose_hidden(0, 0)
            with pe.Fori(0, (XT - 1) // 2 - 1) as n:
                for u in range(2):
                    b = 1 - u
                    i = n * 2 + u + 1
                    up(i, b)
                    transpose_tokens(u, n * 16 + 32)
                    down(n * 2 + u, u)
                    transpose_hidden(i, b)
            for i in range(XT - 2, XT):
                up(i, i % 2)
                if i < XT - 1:
                    transpose_tokens((i + 1) % 2, 16 * ((i + 1) // 2 + 1))
                down(i - 1, (i - 1) % 2)
                transpose_hidden(i, i % 2)
            down(XT - 1, (XT - 1) % 2)

        @block.vector
        def _(dve):
            v = Steps(dve, q.dve)
            V_ = nc.vector
            dve.wait_ge(q.consts, 1)
            dve.wait_ge(q.edges_in, 48)
            v.link(V_.tensor_scalar(part_i[:, :], src_i[:, :], P - 1, None, ALU.bitwise_and))
            v.link(V_.tensor_copy(lo_b[:, :], part_i[:, :]))
            v.link(V_.tensor_scalar(part_i[:, :], src_i[:, :], 7, None, ALU.logical_shift_right))
            v.link(V_.tensor_copy(hi_b[:, :], part_i[:, :]))
            v.link(V_.tensor_tensor(onehot_hi[:, :, :], iota10[:, :].unsqueeze(1).broadcast_to([P, ET, NT]),
                                    hi_b[:, :].unsqueeze(2).broadcast_to([P, ET, NT]), ALU.is_equal))
            V_.tensor_copy(records[:, :, 0], dst_i[:, :])
            V_.tensor_copy(records[:, :, 1], src_i[:, :])
            V_.tensor_copy(records[:, :, 2:REC], att[:, :].rearrange("p (t h) -> p t h", h=HEADS)).then_inc(q.records_ready, 1)

            def sort_dve(g, u, first, last):
                if not last:
                    if not isinstance(g, int) or g >= TURN:
                        dve.wait_ge(q.counts_psum, g - 3)
                    V_.tensor_tensor(onehot_lo[:, u, :, :], iotab[:, :].unsqueeze(1).broadcast_to([P, EG, P]),
                                     lo_b[:, bass.ds(g * EG, EG)].unsqueeze(2).broadcast_to([P, EG, P]), ALU.is_equal).then_inc(q.onehot_lo_ready, 1)
                if not first:
                    dve.wait_ge(q.same_psum, g - 1)
                    if not isinstance(g, int) or g >= 4:
                        dve.wait_ge(q.counts_psum, g - 3)
                    V_.tensor_tensor(before[:, u % 2, :, :], bank[2 + u % 2].rearrange("p (a b) -> p a b", a=EG),
                                     lowb[:, :].unsqueeze(1).broadcast_to([P, EG, P]), ALU.mult).then_inc(q.before_ready, 1)

            in_turns(dve, sort_dve)
            dve.wait_ge(q.counts_ready, ET // EG)
            for h in range(NT):
                V_.tensor_tensor_scan(upto[:, :, h], count[:, :, h], zeros_r[:, :], 0.0, ALU.add, ALU.add).then_inc(q.dve, 1)
                v.k += 1
            dve.wait_ge(q.dve, v.done + v.k)
            v.link(V_.tensor_scalar(deg[:, :], upto[:, ET - 1, :], float(S - 1), None, ALU.add))
            v.link(V_.tensor_copy(deg_i[:, :], deg[:, :]))
            v.link(V_.tensor_scalar(deg_i[:, :], deg_i[:, :], S.bit_length() - 1, None, ALU.logical_shift_right))
            v.link(V_.tensor_copy(deg[:, :], deg_i[:, :]))
            V_.tensor_scalar(rows_f[:, :], deg[:, :], 1.0, None, ALU.max).then_inc(q.rowcount_ready, 1)
            v.link(V_.tensor_tensor(first_f[:, :, :], upto[:, :, :], count[:, :, :], ALU.subtract))
            dve.wait_ge(q.prefix_psum, 1)
            v.link(V_.tensor_copy(rows_in[:, :], bank[3][:, 0:NT]))
            v.link(V_.tensor_copy(tot[:, :], bank[3][:, NT:2 * NT]))
            v.link(V_.tensor_tensor_scan(blk0[:, :], tot[:, :], zeros_r[:, 0:NT], 0.0, ALU.add, ALU.add))
            v.link(V_.tensor_tensor(blk0[:, :], blk0[:, :], tot[:, :], ALU.subtract))
            v.link(V_.tensor_tensor(start4[:, :], rows_in[:, :], blk0[:, :], ALU.add))
            v.link(V_.tensor_scalar(start4[:, :], start4[:, :], float(S), None, ALU.mult))
            v.link(V_.tensor_tensor(first_f[:, :, :], first_f[:, :, :], start4[:, :].unsqueeze(1).broadcast_to([P, ET, NT]), ALU.add))
            v.link(V_.tensor_copy(first_i[:, :, :], first_f[:, :, :]))
            v.link(V_.tensor_scalar(halves_i[:, :, :], first_i[:, :, :], 8, None, ALU.logical_shift_right))
            v.link(V_.tensor_copy(first_b[:, :, 0, :], halves_i[:, :, :]))
            v.link(V_.tensor_scalar(halves_i[:, :, :], first_i[:, :, :], 255, None, ALU.bitwise_and))
            v.link(V_.tensor_copy(first_b[:, :, 1, :], halves_i[:, :, :]))
            dve.nop().then_inc(q.first_ready, 1)
            v.link(V_.tensor_tensor(within[:, :, :], within[:, :, :], onehot_hi[:, :, :], ALU.mult))
            v.link(V_.tensor_reduce(ranks[:, :], within[:, :, :], AX.X, ALU.add))
            with dve.Fori(0, ET // LG // 2) as n:
                v.enter(n, 4)
                for b in range(2):
                    g = n * 2 + b
                    dve.wait_ge(q.found_psum, g + 1)
                    v.link(V_.tensor_tensor(found[:, :, :, :], bank[6 + b][:, 0:LG * 2 * NT].rearrange("p (a b c) -> p a b c", a=LG, b=2),
                                            onehot_hi[:, bass.ds(g * LG, LG), :].unsqueeze(2).broadcast_to([P, LG, 2, NT]), ALU.mult))
                    v.link(V_.tensor_reduce(parts[:, bass.ds(g * LG, LG), :], found[:, :, :, :], AX.X, ALU.add))
                    dve.nop().then_inc(q.parts_ready, 1)
            v.leave(ET // LG // 2)
            dve.wait_ge(q.parts_ready, ET // LG)
            v.link(V_.scalar_tensor_tensor(place_f[:, :], parts[:, :, 0], 256.0, parts[:, :, 1], ALU.mult, ALU.add))
            v.link(V_.tensor_tensor(place_f[:, :], place_f[:, :], ranks[:, :], ALU.add))
            dve.wait_ge(q.records_ready, 1)
            v.link(V_.tensor_copy(place_i[:, :], place_f[:, :]))
            dve.nop().then_inc(q.places_ready, 1)
            v.link(V_.tensor_tensor(cmp_b[:, :, :], blk0[:, :].unsqueeze(1).broadcast_to([P, RT, NT]),
                                    tile0[:, :].unsqueeze(2).broadcast_to([P, RT, NT]), ALU.is_le))
            v.link(V_.tensor_reduce(block_f[:, :], cmp_b[:, :, :], AX.X, ALU.add))
            v.link(V_.tensor_scalar(block_f[:, :], block_f[:, :], -1.0, None, ALU.add))
            v.link(V_.tensor_scalar(nodebase[:, :], block_f[:, :], float(P), None, ALU.mult))
            v.link(V_.tensor_copy(block_i[:, :], block_f[:, :]))

            def norm_stats(of, eps_done):
                for i in range(NT):
                    v.link(V_.bn_stats(stats[:, :], of(i)))
                    v.link(V_.bn_aggr(mv[:, i, :], stats[:, :]))

            dve.wait_ge(q.x_in, 32)
            norm_stats(lambda i: X[:, i, :], None)
            dve.nop().then_inc(q.var_ready, 1)
            dve.wait_ge(q.std_ready, 1)
            v.link(V_.reciprocal(rstd[:, :], rstd[:, :]))
            for i in range(NT):
                if i >= 2:
                    dve.wait_ge(q.tr_psum, 16 + i - 1)
                V_.tensor_scalar(xn[i % 2][:, :], X[:, i, :], mv[:, i, 0:1], rstd[:, i:i + 1], ALU.subtract, ALU.mult).then_inc(q.xn_ready, 1)
            dve.wait_ge(wts["bias"], 80)
            for u in range(3 * NT):
                dve.wait_ge(q.unit_psum, u + 1)
                if u >= 2:
                    dve.wait_ge(sent[u % 2], 16 * (u // 2))
                b = (bias_q, bias_k, bias_v)[u % 3]
                V_.tensor_tensor(send[u % 2][:, :], bank[2 + u % 2][:, :], b[:, :], ALU.add).then_inc(q.send_ready, 1)
                dve.wait_ge(q.send_ready, u + 1)
                dve.nop().then_inc(q.unit_done, 1)
            for c in range(KC):
                dve.wait_ge(q.kt_psum, c + 1)
                for i, (o, w) in enumerate(NCH):
                    v.link(V_.tensor_reduce(kmax3[:, c, i:i + 1], bank[4 + i][:, 0:w], AX.X, ALU.max))
                v.link(V_.tensor_reduce(kneg[:, c:c + 1], kmax3[:, c, :], AX.X, ALU.max))
                v.link(V_.tensor_scalar(kneg[:, c:c + 1], kneg[:, c:c + 1], -1.0, None, ALU.mult))
                dve.nop().then_inc(q.kmax_ready, 1)
            for i in range(NT):
                dve.wait_ge(q.unit_psum, 3 * NT + i + 1)
                V_.tensor_copy(V[:, i, :], bank[2 + i % 2][:, :]).then_inc(q.unit_done, 1)
            dve.wait_ge(q.kt_exp, 3 * KC)
            v.link(V_.tensor_reduce(krec[:, :], ksum3[:, :, :], AX.X, ALU.add))
            v.link(V_.reciprocal(krec[:, :], krec[:, :]))

            def q_finish(i):
                dve.wait_ge(q.q_exp, i + 1)
                t = qs[i % 2][:, :].rearrange("p (h d) -> p h d", h=HEADS)
                v.link(V_.tensor_reduce(qsum[:, :], t, AX.X, ALU.add))
                v.link(V_.reciprocal(qrec[:, :], qsum[:, :]))
                v.link(V_.tensor_scalar(qrec[:, :], qrec[:, :], DK ** -0.5, None, ALU.mult))
                V_.tensor_tensor(t, t, qrec[:, :].unsqueeze(2).broadcast_to([P, HEADS, DK]), ALU.mult).then_inc(q.q_ready, 1)

            for i in range(NT):
                u = 4 * NT + i
                dve.wait_ge(q.unit_psum, u + 1)
                if i >= 2:
                    dve.wait_ge(q.qt_psum, i - 1)
                b = bank[2 + u % 2][:, :].rearrange("p (h d) -> p h d", h=HEADS)
                v.link(V_.tensor_reduce(qmax[:, :], b, AX.X, ALU.max))
                v.link(V_.tensor_tensor(qs[i % 2][:, :].rearrange("p (h d) -> p h d", h=HEADS), b,
                                        qmax[:, :].unsqueeze(2).broadcast_to([P, HEADS, DK]), ALU.subtract))
                dve.nop().then_inc(q.unit_done, 1)
                dve.nop().then_inc(q.q_sub, 1)
                q_finish(i)
            v.link(V_.memset(ctxbd[:, :, :], 0.0))
            dve.wait_ge(q.ctx_psum, 1)
            for h in range(2):
                a = slice(h * DK, (h + 1) * DK)
                v.link(V_.tensor_copy(ctxbd[a, :, a], bank[7][:, :].rearrange("p (c d) -> p c d", c=KC)[a, :, a]))
            dve.nop().then_inc(q.ctx_ready, 1)
            for c in range(KC):
                dve.wait_ge(q.m_psum, c + 1)
                V_.tensor_scalar(Mx[:, c, :], bank[4 + c % 2][:, :], krec[:, c:c + 1], None, ALU.mult).then_inc(q.m_ready, 1)
            dve.wait_ge(q.mix_copied, NT)
            norm_stats(lambda i: mixo[:, i, :], None)
            dve.nop().then_inc(q.mixvar_ready, 1)
            dve.wait_ge(q.mixstd_ready, 1)
            v.link(V_.reciprocal(rstd[:, :], rstd[:, :]))
            for i in range(NT):
                v.link(V_.tensor_scalar(mixo[:, i, :], mixo[:, i, :], mv[:, i, 0:1], rstd[:, i:i + 1], ALU.subtract, ALU.mult))
                v.link(V_.tensor_tensor(mixo[:, i, :], mixo[:, i, :], gamma_b[:, :], ALU.mult))
                v.link(V_.tensor_tensor(X[:, i, :], X[:, i, :], mixo[:, i, :], ALU.add))
            dve.nop().then_inc(q.x_done, 1)

            dve.wait_ge(wts["table"], 16)

            def logits(t, b, arrived):
                dve.wait_ge(gath[b], arrived)
                k, lg = KV[b][:, :, 0:D], logit[:, b, :, :]
                rm = rowmax[:, bass.ds(t, 1), :].rearrange("p a h -> p (a h)")
                v.link(V_.tensor_tensor(k, k, QG[b][:, :].unsqueeze(1).broadcast_to([P, S, D]), ALU.mult))
                v.link(V_.tensor_reduce(lg, k.rearrange("p s (h d) -> p s h d", h=HEADS), AX.X, ALU.add))
                v.link(V_.scalar_tensor_tensor(lg, lg, DK ** -0.5, table[:, bass.ds(t, 1), :, 2:REC]
                                               .rearrange("p a s h -> p (a s) h"), ALU.mult, ALU.add))
                v.link(V_.tensor_reduce(rm, lg.rearrange("p s h -> p h s"), AX.X, ALU.max))
                v.link(V_.tensor_scalar(rowfloor[:, :], rm, -BIG / 10, None, ALU.max))
                V_.tensor_tensor(lg, lg, rowfloor[:, :].unsqueeze(1).broadcast_to([P, S, HEADS]), ALU.subtract).then_inc(q.logit_ready, 1)

            def weigh(t, b):
                dve.wait_ge(q.prob_ready, t + 1)
                p, val = prob[:, b, :, :], KV[b][:, :, D:2 * D].rearrange("p s (h d) -> p s h d", h=HEADS)
                V_.tensor_tensor(val, val, p.unsqueeze(3).broadcast_to([P, S, HEADS, DK]), ALU.mult).then_inc(q.pv_ready, 1)
                V_.tensor_reduce(YR[:, bass.ds(t, 1), :, DK].rearrange("p a h -> p (a h)"), p.rearrange("p s h -> p h s"),
                                 AX.X, ALU.add).then_inc(q.den_ready, 1)

            logits(0, 0, 16 * (S + 1))
            with dve.Fori(0, RT // KVB) as n:
                v.enter(n, 5 * KVB)
                for u in range(KVB):
                    t = n * KVB + u
                    logits(t + 1, (u + 1) % KVB, (n + (u + 1) // KVB) * (16 * (S + 1)) + 16 * (S + 1))
                    weigh(t, u)
            v.leave(RT // KVB)
            weigh(RT - 1, (RT - 1) % KVB)
            dve.wait_ge(q.den_ready, RT)

            v.link(V_.tensor_copy(nodes8[:, :, :], table[:, :, 0, 1:2].broadcast_to([P, RT, HEADS])))
            v.link(V_.tensor_tensor(node_off[:, :], table[:, :, 0, 1], nodebase[:, :], ALU.subtract))
            dve.nop().then_inc(q.nodes_ready, 1)
            dve.wait_ge(q.y_psum, RT)
            V_.memset(seg[:, RT * P:RT * P + 1], -BIG)
            v.link(V_.memset(nodes_c[:, 0:1], -1.0))
            for g in range(MG):
                w = min(4 * P, RT * P - 4 * P * g)
                dve.wait_ge(q.lt_psum, g + 1)
                V_.tensor_copy(nodes_c[:, 1:w + 1], bank[2 + g % 2][0:HEADS, 0:w]).then_inc(q.seg_chunk, 1)
                dve.wait_ge(q.seg_chunk, g + 1)
                v.link(V_.tensor_tensor(seg[:, 4 * P * g:4 * P * g + w], nodes_c[:, 1:w + 1], nodes_c[:, 0:w], ALU.not_equal))
                v.link(V_.tensor_scalar(seg[:, 4 * P * g:4 * P * g + w], seg[:, 4 * P * g:4 * P * g + w], -BIG, None, ALU.mult))
                v.link(V_.tensor_copy(nodes_c[:, 0:1], nodes_c[:, w:w + 1]))
            dve.wait_ge(q.lt_done, MG)
            v.link(V_.tensor_tensor_scan(LT[:, :], seg[:, 0:RT * P], LT[:, :], -BIG, ALU.add, ALU.max))
            V_.tensor_tensor_scan(LT[:, ::-1], seg[:, 1:RT * P + 1][:, ::-1], LT[:, ::-1], -BIG, ALU.add, ALU.max).then_inc(q.m_scan, 1)
            dve.wait_ge(q.m_back, 1)
            v.link(V_.tensor_scalar(Mrow[:, :, :], bank[4][:, 0:RT * HEADS].rearrange("p (t h) -> p t h", h=HEADS), -BIG / 10, None, ALU.max))
            V_.tensor_tensor(rowmax[:, :, :], rowmax[:, :, :], Mrow[:, :, :], ALU.subtract).then_inc(q.w_ready, 1)
            v.link(V_.memset(Y[:, :, :, :], 0.0))
            dve.wait_ge(q.w_exp, 1)
            dve.nop().then_inc(q.merged, 2)

            def node_onehot(t, j):
                V_.tensor_scalar(onehot_n[:, j, :], iota256[:, :], node_off[:, bass.ds(t, 1)], None, ALU.is_equal).then_inc(q.onehot_n_ready, 1)

            def add_rows(t, j):
                blk = dve.value_load(block_i[0:1, bass.ds(t, 1)], min_val=0, max_val=NT - 1)
                dve.wait_ge(q.merge_psum, t + 1)
                y = Y[:, bass.ds(blk, 2), :, :].rearrange("p a (g h) d -> p (a g) (h d)", g=2)
                V_.tensor_tensor(y, y, psum[:, 4 * j:4 * j + 4, 0:4 * YW], ALU.add).then_inc(q.merged, 1)
                dve.wait_ge(q.merged, t + 3)

            node_onehot(0, 0)
            with dve.Fori(0, RT // 2) as n:
                for j in range(2):
                    node_onehot(n * 2 + j + 1, 1 - j)
                    add_rows(n * 2 + j, j)
            add_rows(RT - 1, 0)
            v.link(V_.tensor_scalar(yden[:, :, :], Y[:, 0:NT, :, DK], 1e-37, None, ALU.max))
            v.link(V_.reciprocal(yden[:, :, :], yden[:, :, :]))
            for i in range(NT):
                V_.tensor_tensor(YN[:, i, :].rearrange("p (h d) -> p h d", h=HEADS), Y[:, i, :, 0:DK],
                                 yden[:, i, :].unsqueeze(2).broadcast_to([P, HEADS, DK]), ALU.mult).then_inc(q.yn_ready, 1)
            dve.wait_ge(q.x_back, 32)
            for i in range(NT):
                v.link(V_.tensor_tensor(X[:, i, :], X[:, i, :], bias_o[:, :], ALU.add))
            for i in range(NT):
                dve.wait_ge(q.wo_psum, i + 1)
                V_.tensor_tensor(X[:, i, :], X[:, i, :], bank[2 + i % 2][:, :], ALU.add).then_inc(q.wo_done, 1)
            dve.wait_ge(q.wo_done, NT)

            norm_stats(lambda i: X[:, i, :], None)
            dve.nop().then_inc(q.var_ready, 1)
            dve.wait_ge(q.std_ready, 2)
            v.link(V_.reciprocal(rstd[:, :], rstd[:, :]))
            for i in range(NT):
                V_.tensor_scalar(hn[:, i, :], X[:, i, :], mv[:, i, 0:1], rstd[:, i:i + 1], ALU.subtract, ALU.mult).then_inc(q.h_ready, 1)
            dve.wait_ge(q.r_psum, 1)

            def over(a):
                return a[:, :].unsqueeze(2).broadcast_to([P, NT, NE])

            pos = pos8[:, :].unsqueeze(1).broadcast_to([P, NT, NE])
            rb = bank[2][:, 0:NT * NE].rearrange("p (t e) -> p t e", e=NE)
            v.link(V_.tensor_reduce(r1[:, :], rb, AX.X, ALU.max))
            V_.tensor_tensor(rl[:, :, :], rb, over(r1), ALU.subtract).then_inc(q.r_ready, 1)
            dve.wait_ge(q.r_exp, 1)
            v.link(V_.tensor_reduce(r1[:, :], rp[:, :, :], AX.X, ALU.add))
            v.link(V_.reciprocal(r1[:, :], r1[:, :]))
            v.link(V_.tensor_tensor(rp[:, :, :], rp[:, :, :], over(r1), ALU.mult))
            v.link(V_.tensor_copy(rl[:, :, :], rp[:, :, :]))
            for k in range(2):
                v.link(V_.tensor_reduce(r1[:, :], rl[:, :, :], AX.X, ALU.max))
                v.link(V_.tensor_tensor(rt[:, :, :], rl[:, :, :], over(r1), ALU.is_equal))
                v.link(V_.tensor_scalar(rt[:, :, :], rt[:, :, :], -100.0, 100.0, ALU.mult, ALU.add))
                v.link(V_.tensor_tensor(rt[:, :, :], rt[:, :, :], pos, ALU.add))
                v.link(V_.tensor_reduce(r1[:, :], rt[:, :, :], AX.X, ALU.min))
                v.link(V_.tensor_tensor(pick[:, k, :, :], over(r1), pos, ALU.is_equal))
                if k == 0:
                    v.link(V_.tensor_scalar(rt[:, :, :], pick[:, k, :, :], -2.0, None, ALU.mult))
                    v.link(V_.tensor_tensor(rl[:, :, :], rl[:, :, :], rt[:, :, :], ALU.add))
            v.link(V_.tensor_tensor(both[:, :, :], pick[:, 0, :, :], pick[:, 1, :, :], ALU.add))
            V_.tensor_tensor(both[:, :, :], both[:, :, :], over(valid), ALU.mult).then_inc(q.both_ready, 1)
            v.link(V_.tensor_tensor(picked[:, :, :, :], pick[:, :, :, :], rp[:, :, :].unsqueeze(1).broadcast_to([P, TOPK, NT, NE]), ALU.mult))
            v.link(V_.tensor_reduce(gate[:, :, :], picked[:, :, :, :], AX.X, ALU.add))
            dve.wait_ge(q.ranks_psum, 1)
            v.link(V_.tensor_copy(before_t[:, :, :], bank[3][:, 0:NT * NE].rearrange("p (t e) -> p t e", e=NE)))
            v.link(V_.tensor_copy(total_t[:, :, :], bank[4][:, 0:NT * NE].rearrange("p (t e) -> p t e", e=NE)))
            for e in range(NE):
                v.link(V_.tensor_tensor_scan(upto_t[:, :, e], total_t[:, :, e], zeros_r[:, 0:NT], 0.0, ALU.add, ALU.add))
            v.link(V_.tensor_scalar(tiles_f[:, :], upto_t[:, NT - 1, :], float(P - 1), None, ALU.add))
            v.link(V_.tensor_copy(tiles_i[:, :], tiles_f[:, :]))
            v.link(V_.tensor_scalar(tiles_i[:, :], tiles_i[:, :], P.bit_length() - 1, None, ALU.logical_shift_right))
            v.link(V_.tensor_copy(tiles_f[:, :], tiles_i[:, :]))
            v.link(V_.tensor_scalar(tiles_f[:, :], tiles_f[:, :], 1.0, None, ALU.max))
            v.link(V_.tensor_tensor_scan(tile_end[:, :], tiles_f[:, :], zeros_r[:, 0:NE], 0.0, ALU.add, ALU.add))
            v.link(V_.tensor_tensor(tile_first[:, :], tile_end[:, :], tiles_f[:, :], ALU.subtract))
            v.link(V_.tensor_copy(tile_end_i[:, :], tile_end[:, :]))
            v.link(V_.tensor_scalar(tile_first[:, :], tile_first[:, :], float(P), None, ALU.mult))
            v.link(V_.tensor_tensor(pos_e[:, :, :], upto_t[:, :, :], total_t[:, :, :], ALU.subtract))
            v.link(V_.tensor_tensor(pos_e[:, :, :], pos_e[:, :, :], before_t[:, :, :], ALU.add))
            v.link(V_.tensor_tensor(pos_e[:, :, :], pos_e[:, :, :], tile_first[:, :].unsqueeze(1).broadcast_to([P, NT, NE]), ALU.add))
            v.link(V_.tensor_tensor(picked[:, :, :, :], pick[:, :, :, :], pos_e[:, :, :].unsqueeze(1).broadcast_to([P, TOPK, NT, NE]), ALU.mult))
            v.link(V_.tensor_reduce(pos_f[:, :, :], picked[:, :, :, :], AX.X, ALU.add))
            v.link(V_.tensor_scalar(r1[:, :], valid[:, :], -NOBODY, NOBODY, ALU.mult, ALU.add))
            v.link(V_.tensor_tensor(pos_f[:, :, :], pos_f[:, :, :], r1[:, :].unsqueeze(1).broadcast_to([P, TOPK, NT]), ALU.add))
            v.link(V_.tensor_copy(pos_i[:, :, :], pos_f[:, :, :]))
            v.link(V_.tensor_tensor(owner_c[:, :, :], tile_end[:, :].unsqueeze(1).broadcast_to([P, XT, NE]),
                                    iota256[:, 0:XT].unsqueeze(2).broadcast_to([P, XT, NE]), ALU.is_le))
            v.link(V_.tensor_reduce(owner_f[:, :], owner_c[:, :, :], AX.X, ALU.add))
            v.link(V_.tensor_scalar(owner_f[:, :], owner_f[:, :], NE - 1.0, None, ALU.min))
            v.link(V_.tensor_copy(owner_i[:, :], owner_f[:, :]))
            v.link(V_.tensor_scalar(owner_slot[:, :], owner_i[:, :], 1, None, ALU.bitwise_and))
            v.link(V_.tensor_scalar(owner_f[:, :], owner_f[:, :], 32.0, 32.0, ALU.mult, ALU.add))
            v.link(V_.tensor_copy(owner_need[:, :], owner_f[:, :]))
            dve.nop().then_inc(q.owners_ready, 1)
            dve.wait_ge(wts["b1"], 16)
            dve.wait_ge(wts["b2"], 16)
            dve.nop().then_inc(q.ye_ready, 2)

            def hidden_bias(i, b):
                e = dve.value_load(owner_i[0:1, bass.ds(i, 1)], min_val=0, max_val=NE - 1)
                dve.wait_ge(q.hid_psum, i + 1)
                V_.tensor_tensor(hid[:, b, :], psum[:, 1:3, :].rearrange("p a n -> p (a n)"),
                                 b1_all[:, bass.ds(e, 1), :].rearrange("p a n -> p (a n)"), ALU.add).then_inc(q.hid_biased, 1)

            def result_bias(i, b, stored):
                e = dve.value_load(owner_i[0:1, bass.ds(i, 1)], min_val=0, max_val=NE - 1)
                if stored is not None:
                    dve.wait_ge(y_out[b], stored)
                dve.wait_ge(q.ye_psum, i + 1)
                V_.tensor_tensor(yt[:, b, :], bank[5 + b][:, :], b2_all[:, bass.ds(e, 1), :].rearrange("p a n -> p (a n)"),
                                 ALU.add).then_inc(q.ye_ready, 1)

            hidden_bias(0, 0)
            for i in range(1, 3):
                hidden_bias(i, i % 2)
                result_bias(i - 1, (i - 1) % 2, None)
            with dve.Fori(0, (XT - 3) // 2) as n:
                for u in range(2):
                    hidden_bias(n * 2 + u + 3, 1 - u)
                    result_bias(n * 2 + u + 2, u, n * 16 + 16)
            result_bias(XT - 1, (XT - 1) % 2, 16 * ((XT - 1) // 2))
            for m in range(NT * TOPK):
                i, k = divmod(m, TOPK)
                r = rows_of(i)
                dve.wait_ge(back_in[m % 4], 16 * (m // 4 + 1))
                if k:
                    dve.wait_ge(q.combined, m)
                V_.scalar_tensor_tensor(X[0:r, i, :], back[0:r, m % 4, :], gate[0:r, k, i:i + 1], X[0:r, i, :],
                                        ALU.mult, ALU.add).then_inc(q.combined, 1)


def rows_of(i):
    return P if i < NT - 1 else LAST


_INS = ["x", "src", "dst", "edge_attr_8", "L0_gnn_Wq", "L0_gnn_bq", "L0_gnn_Wk", "L0_gnn_bk", "L0_gnn_Wv", "L0_gnn_bv",
        "L0_gnn_Wo", "L0_gnn_bo", "L0_mix_w_qkv", "L0_mix_w_out", "L0_mix_gamma", "L0_ffn_Wg", "L0_ffn_W1", "L0_ffn_b1",
        "L0_ffn_W2", "L0_ffn_b2"]


def kernel(**inputs):
    import concourse.bacc as bacc
    from concourse.bass_utils import run_bass_kernel_spmd

    nc = bacc.Bacc("TRN2", target_bir_lowering=False, num_devices=1)
    arrays, args = {}, []
    for name in _INS:
        a = np.ascontiguousarray(inputs[name])
        arrays[f"in_{name}"] = a
        args.append(nc.dram_tensor(f"in_{name}", a.shape, mybir.dt.from_np(a.dtype), kind="ExternalInput").ap())
    args.append(nc.dram_tensor("out_x", (N, D), F32, kind="ExternalOutput").ap())
    gps_layer(nc, *args)
    r = run_bass_kernel_spmd(nc, [arrays], core_ids=[0])
    return r.results[0]["out_x"]
```

```python
import numpy as np
import concourse.bass as bass
from concourse import mybir
from contextlib import ExitStack

F32, BF16, I32 = mybir.dt.float32, mybir.dt.bfloat16, mybir.dt.int32
F32R = mybir.dt.float32r
ALU, ACT, AX = mybir.AluOpType, mybir.ActivationFunctionType, mybir.AxisListType

P = 128
N, D = 1250, 512
HEADS, DK = 8, 64
E = 20000
NT = (N + P - 1) // P
NPAD = NT * P
LAST = N - (NT - 1) * P
KC = D // P
EPS = 1e-5

EP = 125
ET = E // EP
EG = 4
GROUPS = ET // EG
TURN = 4
KVB = 4
SD = 2
VA = NT // 2
assert NT == 2 * VA
SG = 10
LG = 16
S = 4
ROWS = N + E // S
RT = (ROWS + P - 1) // P
MG = (RT + 3) // 4
REC = 2 + HEADS
BIG = 1e30
NOBODY = 1e6
NONODE = 4096.0
YW = DK + 1

NE, HID = 8, 1024
HC = HID // P
TOPK = 2
XT = (TOPK * N + NE * (P - 1) + NE) // P
HH = HID // 512
NCH = [(0, 512), (512, 512), (1024, N - 1024)]
KB = 1024


class Steps:

    def __init__(self, eng, sem):
        self.eng, self.sem, self.done, self.base, self.k = eng, sem, 0, None, 0

    def link(self, ins):
        ins.then_inc(self.sem, 1)
        self.k += 1
        self.eng.wait_ge(self.sem, self.k + (self.done if self.base is None else self.base))

    def enter(self, n, per_turn):
        self.done += self.k
        self.k, self.per_turn = 0, per_turn
        self.base = n * per_turn + self.done

    def leave(self, turns):
        assert self.k == self.per_turn, self.k
        self.done += turns * self.per_turn
        self.base, self.k = None, 0




def gps_layer(nc, x, src, dst, edge_attr, Wq, bq, Wk, bk, Wv, bv, Wo, bo, w_qkv, w_out, gamma,
              Wg, W1, b1, W2, b2, out):
    ctx = ExitStack()
    with ctx:
        base = ((nc.sbuf_base + 63) // 64) * 64

        def at(name, kb, shape, dt=F32):
            return place(name, shape, dt, base + int(kb * KB))

        def place(name, shape, dt, offset):
            size = int(np.prod(shape[1:])) * mybir.dt.size(dt)
            assert offset + size <= base + 206 * KB, name
            return nc.alloc_sbuf_tensor_at(name, shape, dt, offset=offset)

        def sem(name):
            return ctx.enter_context(nc.semaphore(name))

        ident = at("ident", 0, [P, P])
        low_f = at("low_f", 0.5, [P, P])
        ones_f = at("ones_f", 1, [P, P])
        identb = at("identb", 1.5, [P, P], BF16)
        lowb = at("lowb", 1.75, [P, P], BF16)
        iotab = at("iotab", 2, [P, P], BF16)
        iota256 = at("iota256", 2.25, [P, 2 * P])
        iota_i = at("iota_i", 3.25, [P, 2 * P], I32)
        iota10 = at("iota10", 4.25, [P, NT], BF16)
        tile0 = at("tile0", 4.375, [P, RT])
        tile0_i = at("tile0_i", 4.625, [P, RT], I32)
        zeros_r = at("zeros_r", 4.875, [P, ET])
        eps_c = at("eps_c", 5.5, [P, 1])
        pos8 = at("pos8", 5.5625, [P, NE])
        zero_rows = at("zero_rows", 95, [P, D])
        valid = at("valid", 205.75, [P, NT])
        bias_q = at("bias_q", 6, [P, D])
        bias_k = at("bias_k", 8, [P, D])
        bias_v = at("bias_v", 10, [P, D])
        bias_o = at("bias_o", 14, [P, D])
        gamma_b = at("gamma_b", 202.75, [P, D])

        X = at("X", 16, [P, NT, D])

        att = at("att", 90, [P, ET * HEADS])
        empty = at("empty", 104, [P, RT * S, REC])
        onehot_lo = at("onehot_lo", 100, [P, TURN, EG, P], BF16)
        before = at("before", 97, [P, 2, EG, P], BF16)
        src_i = at("src_i", 112, [P, ET], I32)
        dst_i = at("dst_i", 112.75, [P, ET], I32)
        part_i = at("part_i", 113.5, [P, ET], I32)
        lo_b = at("lo_b", 114.25, [P, ET], BF16)
        hi_b = at("hi_b", 114.625, [P, ET], BF16)
        records = at("records", 120, [P, ET, REC])
        place_i = at("place_i", 126.25, [P, ET], I32)
        stage_r = [at(f"stage_r{j}", 126.875 + 0.40625 * j, [P, SG, REC]) for j in range(2)]
        stage_i = [at(f"stage_i{j}", 127.6875 + 0.0625 * j, [P, SG], I32) for j in range(2)]
        onehot_loT = at("onehot_loT", 128, [P, ET, P], BF16)
        onehot_hi = at("onehot_hi", 168, [P, ET, NT], BF16)
        count = at("count", 172, [P, ET, NT])
        upto = at("upto", 178.5, [P, ET, NT])
        within = at("within", 185, [P, ET, NT])
        first_b = at("first_b", 191.5, [P, ET, 2, NT], BF16)
        first_f = at("first_f", 198, [P, ET, NT])
        first_i = at("first_i", 172, [P, ET, NT], I32)
        halves_i = at("halves_i", 178.5, [P, ET, NT], I32)
        found = at("found", 172, [P, LG, 2, NT])
        parts = at("parts", 174, [P, ET, 2])
        ranks = at("ranks", 176, [P, ET])
        place_f = at("place_f", 177, [P, ET])
        deg = at("deg", 204.5, [P, NT])
        deg_i = at("deg_i", 204.5625, [P, NT], I32)
        rows_f = at("rows_f", 204.625, [P, NT])
        rows_in = at("rows_in", 204.6875, [P, NT])
        blk0 = at("blk0", 204.75, [P, NT])
        start4 = at("start4", 204.8125, [P, NT])
        tot = at("tot", 204.875, [P, NT])
        cmp_b = at("cmp_b", 189, [P, RT, NT])
        block_f = at("block_f", 5.625, [P, RT])
        block_i = at("block_i", 205, [P, RT], I32)
        nodebase = at("nodebase", 205.25, [P, RT])

        XNT = at("XNT", 36, [P, KC, NPAD])
        XNTh = at("XNTh", 148, [P, KC, NPAD], F32R)
        XNTl = at("XNTl", 36, [P, KC, NPAD], F32R)
        Wqkv = at("Wqkv", 56, [P, 3, KC, D])
        send = [at(f"send{j}", 116 + 2 * j, [P, D]) for j in range(2)]
        xn = [at(f"xn{j}", 84 + 2 * j, [P, D]) for j in range(2)]
        XNs = at("XNs", 88, [P, KC, P])
        raw = at("raw", 56, [P, 8, D])
        raw_v = at("raw_v", 180, [P, 4, D])
        raw_o = at("raw_o", 104, [P, KC, D])
        WoT = at("WoT", 112, [P, KC, D])
        mixT = at("mixT", 80, [P, KC, 3 * D], F32R)
        mixTl = [at(f"mixTl{j}", (172, 192, 104)[j], [P, KC, D], F32R) for j in range(3)]
        QT = at("QT", 56, [P, KC, NPAD])
        qs = [at(f"qs{j}", (76, 78, 168)[j], [P, D]) for j in range(3)]
        KT = at("KT", 172, [P, KC, NPAD])
        KE = at("KE", 36, [P, NT, D])
        V = at("V", 128, [P, NT, D])
        Mx = at("Mx", 104, [P, KC, D])
        ctxbd = at("ctxbd", 100, [P, KC, P])
        mixo = [at(f"mixo{j}", 80 + 2 * j, [P, D]) for j in range(2)]
        sm = 202
        stats = at("stats", sm, [P, 6])
        mv = at("mv", sm + 0.0625, [P, NT, 2])
        rstd = at("rstd", sm + 0.1875, [P, NT])
        kmax3 = at("kmax3", sm + 0.25, [P, KC, 3])
        kneg = at("kneg", sm + 0.3125, [P, KC])
        ksum3 = at("ksum3", sm + 0.375, [P, KC, 3])
        krec = at("krec", sm + 0.4375, [P, KC])
        qmax = at("qmax", sm + 0.5, [P, HEADS])
        qsum = at("qsum", sm + 0.5625, [P, HEADS])
        qrec = at("qrec", sm + 0.625, [P, HEADS])

        table = at("table", 6, [P, RT, S, REC])
        YR = at("YR", 44, [P, RT, HEADS, YW])
        kv_at = [148, 166, 184, 16]
        KV = [at(f"KV{b}", kv_at[b], [P, S, 2 * D]) for b in range(KVB)]
        QG = [at(f"QG{b}", kv_at[b] + 16, [P, D]) for b in range(KVB)]
        logit = at("logit", 145.125, [P, KVB, S, HEADS])
        prob = at("prob", 145.625, [P, KVB, S, HEADS])
        rowmax = at("rowmax", 143.5625, [P, RT, HEADS])
        rowfloor = at("rowfloor", 146.125, [P, HEADS])
        idx = [at(f"idx{b}", 13.6875 + 0.03125 * b, [P, S + 1], I32) for b in range(KVB)]
        nodes8 = at("nodes8", 202, [P, RT, HEADS])
        LT = at("LT", 148, [HEADS, RT * P])
        seg = at("seg", 172.75, [HEADS, RT * P + 1])
        nodes_c = [at(f"nodes_c{j}", 197.375 + 2.125 * j, [HEADS, 4 * P + 1]) for j in range(2)]
        node_off = at("node_off", 205.5, [P, RT])
        Mrow = at("Mrow", 202, [P, RT, HEADS])
        onehot_n = at("onehot_n", 148, [P, 4, 2 * P])
        Y = at("Y", 176, [P, NT + 1, HEADS, YW])
        yden = at("yden", 202, [P, NT, HEADS])
        YN = at("YN", 44, [P, NT, D])
        YT = at("YT", 64, [P, KC, NPAD])
        Wo_s = at("Wo_s", 84, [P, KC, D])

        HT = at("HT", 36, [P, KC, NPAD])
        hn = at("hn", 72, [P, NT, D])
        b1_s = at("b1_s", 6, [P, 2, HID])
        b2_s = at("b2_s", 189, [P, 2, D])
        Wg_s = at("Wg_s", 188, [P, KC, NE])
        rl, rp, rt, both, pos_e, before_t, total_t, upto_t = (
            at(n, 189 + 0.375 * i, [P, NT, NE]) for i, n in enumerate(
                ["rl", "rp", "rt", "both", "pos_e", "before_t", "total_t", "upto_t"]))
        pick = at("pick", 192, [P, TOPK, NT, NE])
        picked = at("picked", 192.75, [P, TOPK, NT, NE])
        gate = at("gate", 193.5, [P, TOPK, NT])
        pos_f = at("pos_f", 193.625, [P, TOPK, NT])
        pos_i = at("pos_i", 193.75, [P, TOPK, NT], I32)
        r1 = at("r1", 193.875, [P, NT])
        tiles_f = at("tiles_f", 193.9375, [P, NE])
        tiles_i = at("tiles_i", 194, [P, NE], I32)
        tile_end = at("tile_end", 194.0625, [P, NE])
        tile_end_i = at("tile_end_i", 194.125, [P, NE], I32)
        tile_first = at("tile_first", 194.1875, [P, NE])
        owner_c = at("owner_c", 194.25, [P, XT, NE])
        owner_f = at("owner_f", 195.25, [P, XT])
        owner_i = at("owner_i", 195.375, [P, XT], I32)
        owner_slot = at("owner_slot", 195.5, [P, XT], I32)
        owner_need = at("owner_need", 195.625, [P, XT], I32)
        W1_s = at("W1_s", 124, [P, 2, 2, KC * HID], F32R)
        W2_s = at("W2_s", 60, [P, 2, 2, HC * D], F32R)
        hrow = at("hrow", 36, [P, 2, D])
        hTt = at("hTt", 40, [P, 2, 2, KC, P], F32R)
        hid = at("hid", 48, [P, 2, HID])
        yt = at("yt", 56, [P, 2, D])
        hidT = at("hidT", 196, [P, 2, HC, P], F32R)
        back = at("back", 36, [P, 4, D])

        psum = ctx.enter_context(nc.psum_tensor("psum", [P, 8, 512], F32))
        bank = [psum[:, i, :] for i in range(8)]

        def bf(b):
            return bank[b][:, 0:256].bitcast(BF16)

        sent_h = nc.dram_tensor("tokens_by_expert", [XT * P, D], F32, kind="Internal").ap()
        got_y = nc.dram_tensor("expert_rows", [XT * P, D], F32, kind="Internal").ap()
        q_dram = nc.dram_tensor("q_rows", [NPAD, D], F32, kind="Internal").ap()
        x_dram = nc.dram_tensor("residual", [NPAD, D], F32, kind="Internal").ap()
        kv_dram = nc.dram_tensor("kv_rows", [NPAD, 2 * D], F32, kind="Internal").ap()
        table_d = nc.dram_tensor("sorted_edges", [RT * P * S, REC], F32, kind="Internal").ap()

        names = """consts pos_ready x_high x_low mix_low edges_in pad_ready x_in empty_ready empty_out
            onehot_lo_ready loT_psum loT_ready same_psum before_ready counts_psum counts_ready
            first_ready rowcount_ready prefix_psum found_psum places_ready staged dve gp xn_ready
            tr_psum tr_done unit_psum send_ready kt_psum kmax_ready kt_exp ke_psum ke_done q_sub
            q_exp q_ready qt_psum qt_done ctx_psum ctx_ready m_psum m_ready mix_psum mix_copied
            mixvar_ready mixstd_ready var_ready std_ready kv_zero idx_ready pv_act logit_ready
            prob_ready pv_ready y_psum y_copied lt_psum lt_done nodes_ready seg_chunk seg_scaled
            nodes_in m_back m_scan w_ready w_exp onehot_n_ready yr_scaled merge_psum merged yn_ready
            yt_psum yt_done wo_psum wo_done x_away x_back xs_ready lin_psum lin_done zero_ready
            zero_out den_ready parts_ready weights_split th_high hidT_high tokens_sent th_psum
            th_ready hid_psum hid_biased hid_ready hidT_psum hidT_ready ye_psum ye_ready owners_ready
            both_ready ranks_psum combined x_done h_ready ht_psum ht_done r_psum r_ready r_exp
            out_done records_ready act_passed pool_passed""".split()
        q = {n: sem(n) for n in names}
        scat = [sem(f"scattered{j}") for j in range(2)]
        gath = [sem(f"gathered{j}") for j in range(KVB)]
        sent = [sem(f"sent{j}") for j in range(2)]
        hrow_in = [sem(f"hrow_in{j}") for j in range(2)]
        y_out = [sem(f"y_out{j}") for j in range(2)]
        w1_in, w2_in = ([sem(f"{n}{j}") for j in range(4)] for n in ("w1_in", "w2_in"))
        b1_in, b2_in, cast = ([sem(f"{n}{j}") for j in range(2)] for n in ("b1_in", "b2_in", "high_parts"))
        back_in = [sem(f"back_in{j}") for j in range(4)]
        wts = {n: sem("in_" + n) for n in ("wqkv", "raw_q", "raw_k", "raw_v", "rawo", "bias", "gamma", "table", "wo", "wg")}
        q = type("Semaphores", (), q)

        block = ctx.enter_context(nc.Block())

        def in_turns(eng, step):
            assert GROUPS == TURN * NT
            for g in range(TURN):
                step(g, 0, g, max(0, 2 - g), 0)
            with eng.Fori(1, NT - 1) as n:
                for u in range(TURN):
                    step(n * TURN + u, n, u, 0, 0)
            for g in range(GROUPS - TURN, GROUPS + 2):
                step(g, g // TURN, g % TURN, 0, max(0, 1 + g - GROUPS))

        def apart(eng):
            eng.sem_inc(q.act_passed if eng.engine == mybir.EngineType.Activation else q.pool_passed, 1)

        @block.sync
        def _(sp):
            sp.wait_ge(q.pad_ready, 1)
            sp.dma_start(X[:, 0:NT - 1, :], x[0:(NT - 1) * P, :].rearrange("(t p) d -> p t d", p=P)).then_inc(q.x_in, 16)
            sp.dma_start(X[0:LAST, NT - 1, :], x[(NT - 1) * P:N, :]).then_inc(q.x_in, 16)
            sp.wait_ge(q.pad_ready, 2)
            sp.dma_start(src_i[0:EP, :], src.rearrange("(p t) -> p t", t=ET)).then_inc(q.edges_in, 16)
            sp.dma_start(dst_i[0:EP, :], dst.rearrange("(p t) -> p t", t=ET)).then_inc(q.edges_in, 16)
            sp.dma_start(att[0:EP, :], edge_attr.rearrange("(p t) h -> p (t h)", t=ET)).then_inc(q.edges_in, 16)
            for i, w in enumerate((Wq, Wk, Wv)):
                sp.dma_start(Wqkv[:, i, :, :], w.rearrange("(k p) d -> p k d", p=P)).then_inc(wts["wqkv"], 16)

            def row(to, b, arrived):
                sp.dma_start(to[:, :], b.rearrange("(a d) -> a d", a=1).broadcast_to([P, D])).then_inc(arrived, 16)

            for t, b in ((bias_q, bq), (bias_k, bk), (bias_v, bv), (bias_o, bo)):
                row(t, b, wts["bias"])
            sp.wait_ge(q.empty_ready, 1)
            sp.dma_start(table_d.rearrange("(p r) c -> p (r c)", p=P), empty[:, :, :]).then_inc(q.empty_out, 16)
            sp.wait_ge(q.zero_ready, 1)
            sp.dma_start(sent_h.rearrange("(t p) d -> p t d", p=P), zero_rows[:, :].unsqueeze(1).broadcast_to([P, XT, D])).then_inc(q.zero_out, 16)
            sp.wait_ge(q.empty_out, 16)
            sp.dma_start(raw_o[:, :, :], w_out.rearrange("(g p) d -> p g d", p=P)).then_inc(wts["rawo"], 16)

            q_rows, kv_rows = (d.rearrange("(t p) d -> p t d", p=P) for d in (q_dram, kv_dram))
            with sp.Fori(0, NT) as n:
                sp.wait_ge(q.send_ready, n + 1)
                sp.dma_start(q_rows[:, bass.ds(n, 1), :].rearrange("p a d -> p (a d)"), send[0][:, :]).then_inc(sent[0], 16)

            def load_raw(to, first):
                return sp.dma_start(to, w_qkv[first * P:(first + 4) * P, :].rearrange("(g p) d -> p g d", p=P))

            load_raw(raw[:, 0:4, :], 0).then_inc(wts["raw_q"], 16)
            for m in range(2 * NT):
                if m == VA:
                    sp.wait_ge(q.places_ready, 1)
                    load_raw(raw_v[:, :, :], 8).then_inc(wts["raw_v"], 16)
                if m == NT:
                    load_raw(raw[:, 4:8, :], 4).then_inc(wts["raw_k"], 16)
                i, half = m % NT, m // NT
                sp.wait_ge(q.send_ready, NT + m + 1)
                sp.dma_start(kv_rows[:, i, half * D:(half + 1) * D], send[m % 2][:, :]).then_inc(sent[m % 2], 16)
            sp.wait_ge(q.places_ready, 1)
            row(gamma_b, gamma, wts["gamma"])

            for j in range(2):
                sp.wait_ge(scat[j], 16 * (ET // 2))
            sp.dma_start(table[:, :, :, :], table_d.rearrange("(t p s) c -> p t (s c)", p=P, s=S)
                         .rearrange("p t (s c) -> p t s c", s=S)).then_inc(wts["table"], 16)
            for i in range(NT):
                sp.wait_ge(q.x_done, i + 1)
                sp.dma_start(x_dram[i * P:(i + 1) * P, :], X[:, i, :]).then_inc(q.x_away, 16)

            sp.wait_ge(q.y_psum, RT)
            sp.dma_start(X[:, :, :], x_dram.rearrange("(t p) d -> p t d", p=P)).then_inc(q.x_back, 16)
            sp.wait_ge(q.merged, RT + 2)
            sp.dma_start(Wo_s[:, :, :], Wo.rearrange("(k p) d -> p k d", p=P)).then_inc(wts["wo"], 16)

            def load_halves(parts, w, chunks, e, arrived):
                width = w.shape[2]
                for j in range(2):
                    rows = slice(j * chunks // 2 * P, (j + 1) * chunks // 2 * P)
                    to = parts[:, (e + 1) % 2, 1, j * chunks // 2 * width:(j + 1) * chunks // 2 * width].bitcast(F32)
                    sp.dma_start(to.rearrange("p (k h) -> p k h", h=width),
                                 w[e, rows, :].rearrange("(k p) h -> p k h", p=P)).then_inc(arrived[2 * (e % 2) + j], 16)

            def load_up(e):
                load_halves(W1_s, W1, KC, e, w1_in)

            def load_down(e):
                load_halves(W2_s, W2, HC, e, w2_in)

            def load_bias(to, b, e, arrived):
                sp.dma_start(to[:, (e + 1) % 2, :], b[e:e + 1, :].broadcast_to([P, b.shape[1]])).then_inc(arrived[e % 2], 16)

            load_down(0)
            load_up(1)
            for e in range(2):
                load_bias(b1_s, b1, e, b1_in)
            sp.wait_ge(q.yn_ready, NT)
            load_up(0)
            sp.dma_start(Wg_s[:, :, :], Wg.rearrange("(k p) e -> p k e", p=P)).then_inc(wts["wg"], 16)
            sp.wait_ge(q.owners_ready, 1)
            for e in range(2):
                load_bias(b2_s, b2, e, b2_in)
            sp.wait_ge(q.tokens_sent, 16 * NT * TOPK)
            load_down(1)
            for e in range(2, NE):
                last = sp.value_load(tile_end_i[0:1, e - 2:e - 1], min_val=1, max_val=XT)
                sp.wait_ge(q.hid_psum, last)
                load_up(e)
                sp.wait_ge(q.hid_biased, last)
                load_bias(b1_s, b1, e, b1_in)
                sp.wait_ge(q.ye_psum, last)
                load_down(e)
                sp.wait_ge(q.ye_ready, last + 2)
                load_bias(b2_s, b2, e, b2_in)
            for i in range(NT):
                sp.wait_ge(q.combined, TOPK * (i + 1))
                sp.dma_start(out[i * P:i * P + rows_of(i), :], X[0:rows_of(i), i, :]).then_inc(q.out_done, 16)
            sp.wait_ge(q.out_done, 16 * NT)

        @block.gpsimd
        def _(gp):
            st = Steps(gp, q.gp)
            gp.memset(X[:, NT - 1, :], 0.0).then_inc(q.pad_ready, 1)
            gp.memset(dst_i[:, :], 0)
            gp.memset(att[:, :], 0.0)
            gp.memset(src_i[:, :], 1 << 20).then_inc(q.pad_ready, 1)
            for m in (ident, identb):
                st.link(gp.memset(m[:, :], 0.0))
                st.link(gp.affine_select(out=m[:, :], in_=m[:, :], compare_op=ALU.not_equal, fill=1.0, base=0,
                                         pattern=[[-1, P]], channel_multiplier=1))
            for m in (low_f, lowb):
                st.link(gp.memset(m[:, :], 0.0))
                st.link(gp.affine_select(out=m[:, :], in_=m[:, :], compare_op=ALU.is_ge, fill=1.0, base=0,
                                         pattern=[[-1, P]], channel_multiplier=1))
            gp.memset(ones_f[:, :], 1.0)
            gp.memset(zeros_r[:, :], 0.0)
            gp.memset(eps_c[:, :], EPS)
            st.link(gp.iota(iota_i[:, :], pattern=[[1, 2 * P]], base=0, channel_multiplier=0))
            st.link(gp.iota(tile0_i[:, :], pattern=[[P, RT]], base=0, channel_multiplier=0))
            gp.tensor_copy(tile0[:, :], tile0_i[:, :])
            gp.tensor_copy(iota256[:, :], iota_i[:, :])
            gp.tensor_copy(pos8[:, :], iota_i[:, 0:NE])
            gp.tensor_copy(iota10[:, :], iota_i[:, 0:NT])
            gp.tensor_copy(iotab[:, :], iota_i[:, 0:P]).then_inc(q.consts, 1)
            gp.memset(zero_rows[:, :], 0.0).then_inc(q.zero_ready, 1)
            st.link(gp.memset(valid[:, :], 1.0))
            st.link(gp.affine_select(out=valid[:, :], in_=valid[:, :], compare_op=ALU.is_ge, fill=0.0, base=N - 1,
                                     pattern=[[-P, NT]], channel_multiplier=-1))
            gp.memset(empty[:, :, 0:1], NOBODY)
            gp.memset(empty[:, :, 1:2], NONODE)
            gp.memset(empty[:, :, 2:REC], -BIG).then_inc(q.empty_ready, 1)

            gp.wait_ge(q.places_ready, 1)
            gp.wait_ge(q.empty_out, 16)
            def scatter(n, b, left):
                if left is not None:
                    gp.wait_ge(scat[b], left)
                    apart(gp)
                gp.tensor_copy(stage_i[b][:, :], place_i[:, bass.ds(n * SG, SG)])
                gp.tensor_copy(stage_r[b][:, :, :], records[:, bass.ds(n * SG, SG), :]).then_inc(q.staged, 1)
                gp.wait_ge(q.staged, n + 1)
                apart(gp)
                for j in range(SG):
                    gp.indirect_dma_start(table_d, bass.IndirectOffsetOnAxis(ap=stage_i[b][0:EP, j:j + 1], axis=0),
                                          stage_r[b][0:EP, j, :], None,
                                          bounds_check=RT * P * S - 1, oob_is_err=False).then_inc(scat[b], 16)

            scatter(0, 0, None)
            scatter(1, 1, None)
            with gp.Fori(1, ET // SG // 2) as n:
                for b in range(2):
                    scatter(n * 2 + b, b, n * (16 * SG))

            gp.wait_ge(q.ke_done, NT)

            def clear(b):
                gp.memset(QG[b][:, :], 0.0)
                gp.memset(KV[b][:, :, :], 0.0).then_inc(q.kv_zero, 1)
                gp.wait_ge(q.kv_zero, b + 1)

            for b in range(KVB - 1):
                clear(b)
            gp.wait_ge(wts["table"], 16)
            gp.wait_ge(sent[0], 16 * 2 * NT)
            gp.wait_ge(sent[1], 16 * NT)

            def gather(t, b):
                gp.tensor_copy(idx[b][:, 0:S], table[:, bass.ds(t, 1), :, 0].rearrange("p a s -> p (a s)"))
                gp.tensor_copy(idx[b][:, S:S + 1], table[:, bass.ds(t, 1), 0, 1]).then_inc(q.idx_ready, 1)
                gp.wait_ge(q.idx_ready, t + 1)
                apart(gp)
                gp.indirect_dma_start(QG[b][:, :], None, q_dram,
                                      bass.IndirectOffsetOnAxis(ap=idx[b][:, S:S + 1], axis=0),
                                      bounds_check=N - 1, oob_is_err=False).then_inc(gath[b], 16)
                for s in range(S):
                    gp.indirect_dma_start(KV[b][:, s, :], None, kv_dram,
                                          bass.IndirectOffsetOnAxis(ap=idx[b][:, s:s + 1], axis=0),
                                          bounds_check=N - 1, oob_is_err=False).then_inc(gath[b], 16)

            for t in range(KVB):
                if t == KVB - 1:
                    gp.wait_ge(q.x_away, 16 * NT)
                    clear(t)
                gather(t, t)
            with gp.Fori(0, (RT - KVB) // KVB) as n:
                for u in range(KVB):
                    gp.wait_ge(q.y_psum, n * KVB + u + 1)
                    apart(gp)
                    gather(n * KVB + u + KVB, u)
            for t in range(RT // KVB * KVB, RT):
                gp.wait_ge(q.y_psum, t - KVB + 1)
                gather(t, t % KVB)

            for g in range(0, MG, 2):
                gp.wait_ge(q.seg_chunk, g + 1)
                a = seg[:, 4 * P * g:min(4 * P * g + 4 * P, RT * P)]
                gp.tensor_scalar(a, a, -BIG, None, ALU.mult).then_inc(q.seg_scaled, 1)

            gp.wait_ge(q.w_exp, 1)
            with gp.Fori(0, RT) as t:
                y = YR[:, bass.ds(t, 1), :, :].rearrange("p a h d -> p (a h) d")
                gp.tensor_tensor(y, y, rowmax[:, bass.ds(t, 1), :].rearrange("p a h -> p (a h)").unsqueeze(2)
                                 .broadcast_to([P, HEADS, YW]), ALU.mult).then_inc(q.yr_scaled, 1)

            def split_weights(e, n):
                b, parts, half = (e + 1) % 2, (W1_s, W2_s)[n], KC * HID // 2
                if e >= 2 or n == 0:
                    gp.wait_ge((b1_in, b2_in)[n][e % 2], 16 * (e // 2 + 1))
                for j in range(2):
                    o = slice(j * half, (j + 1) * half)
                    gp.wait_ge((w1_in, w2_in)[n][2 * (e % 2) + j], 16 * (e // 2 + 1))
                    gp.dma_start(parts[:, b, 0, o], parts[:, b, 1, o].bitcast(F32)).then_inc(cast[j], 16)
                for j in range(2):
                    o = slice(j * half, (j + 1) * half)
                    gp.wait_ge(cast[j], 16 * (2 * e + n + 1))
                    i = gp.tensor_tensor(parts[:, b, 1, o], parts[:, b, 1, o].bitcast(F32), parts[:, b, 0, o].bitcast(F32), ALU.subtract)
                i.then_inc(q.weights_split, 1)

            for e, n in ((0, 0), (0, 1), (1, 0)):
                split_weights(e, n)
            gp.wait_ge(q.pos_ready, 1)
            for i in range(NT):
                for k in range(TOPK):
                    gp.indirect_dma_start(sent_h, bass.IndirectOffsetOnAxis(ap=pos_i[:, k, i:i + 1], axis=0), hn[:, i, :], None,
                                          bounds_check=XT * P - 1, oob_is_err=False).then_inc(q.tokens_sent, 16)

            split_weights(1, 1)
            for e in range(2, NE):
                for n in range(2):
                    split_weights(e, n)
            gp.wait_ge(y_out[0], 16 * ((XT + 1) // 2))
            gp.wait_ge(y_out[1], 16 * (XT // 2))
            for m in range(NT * TOPK):
                i, k = divmod(m, TOPK)
                if m >= 4:
                    gp.wait_ge(q.combined, m - 3)
                gp.indirect_dma_start(back[:, m % 4, :], None, got_y, bass.IndirectOffsetOnAxis(ap=pos_i[:, k, i:i + 1], axis=0),
                                      bounds_check=XT * P - 1, oob_is_err=False).then_inc(back_in[m % 4], 16)

        @block.scalar
        def _(act):
            act.wait_ge(q.consts, 1)
            act.wait_ge(q.var_ready, 1)
            act.activation(rstd[:, :], mv[:, :, 1], ACT.Sqrt, bias=eps_c[:, :]).then_inc(q.std_ready, 1)

            def transposed(g, to):
                act.wait_ge(q.tr_psum, g + 1)
                act.copy(to, bank[g % 2][:, :].rearrange("p (a b) -> p a b", a=KC)).then_inc(q.tr_done, 1)

            for i in range(NT):
                transposed(i, XNT[:, :, i * P:(i + 1) * P])
            act.wait_ge(q.tr_done, NT)
            act.copy(XNs[:, :, :], XNT[:, :, 0:P]).then_inc(q.xs_ready, 1)

            def sort_act(g, n, u, first, last):
                if not last:
                    act.wait_ge(q.loT_psum, g + 1)
                    apart(act)
                    act.copy(onehot_loT[:, bass.ds(g * EG, EG), :], bf(u % 2).rearrange("p (a b) -> p a b", a=EG)).then_inc(q.loT_ready, 1)
                if not last and u == 3 and not (isinstance(n, int) and n == NT - 1):
                    act.wait_ge(q.unit_psum, n + 1)
                    apart(act)
                    act.copy(XNs[:, :, :], XNT[:, :, bass.ds(n * P + P, P)]).then_inc(q.xs_ready, 1)
                if not first:
                    act.wait_ge(q.counts_psum, g - 1)
                    apart(act)
                    bk = bank[4 + u % 2]
                    act.copy(count[:, bass.ds((g - 2) * EG, EG), :], bk[:, 0:EG * NT].rearrange("p (a b) -> p a b", a=EG))
                    act.copy(within[:, bass.ds((g - 2) * EG, EG), :],
                             bk[:, EG * NT:2 * EG * NT].rearrange("p (a b) -> p a b", a=EG)).then_inc(q.counts_ready, 1)

            in_turns(act, sort_act)

            act.wait_ge(q.places_ready, 1)
            act.wait_ge(q.zero_out, 16)
            for g in range(4):
                transposed(NT + g, mixT[:, :, g * P:(g + 1) * P])
            for i in range(NT):
                act.copy(XNTh[:, :, i * P:(i + 1) * P], XNT[:, :, i * P:(i + 1) * P]).then_inc(q.x_high, 1)
            for g in range(4, 8):
                transposed(NT + g, mixT[:, :, g * P:(g + 1) * P])
            act.wait_ge(sent[0], 16 * 2 * NT)
            act.wait_ge(sent[1], 16 * NT)
            for g in range(4):
                transposed(NT + 8 + g, WoT[:, :, g * P:(g + 1) * P])
            for g in range(8, 12):
                transposed(NT + 4 + g, mixT[:, :, g * P:(g + 1) * P])
            def q_transposed(i):
                act.wait_ge(q.qt_psum, i + 1)
                act.copy(QT[:, :, i * P:(i + 1) * P], bank[i % 2][:, :].rearrange("p (a b) -> p a b", a=KC)).then_inc(q.qt_done, 1)

            for i in range(NT):
                act.wait_ge(q.q_sub, i + 1)
                act.activation(qs[i % 3][:, :], qs[i % 3][:, :], ACT.Exp).then_inc(q.q_exp, 1)
                if i >= 2:
                    q_transposed(i - 2)
            q_transposed(NT - 2)
            q_transposed(NT - 1)
            for c in range(KC):
                act.wait_ge(q.kmax_ready, c + 1)
                for i, (o, w) in enumerate(NCH):
                    act.activation(KT[:, c, o:o + w], bank[4 + i][:, 0:w], ACT.Exp, bias=kneg[:, c:c + 1],
                                   accum_out=ksum3[:, c, i:i + 1]).then_inc(q.kt_exp, 1)
            for i in range(NT):
                act.wait_ge(q.ke_psum, i + 1)
                act.copy(KE[0:rows_of(i), i, :], bank[i % 2][0:rows_of(i), :]).then_inc(q.ke_done, 1)
            for i in range(NT):
                act.wait_ge(q.mixvar_ready, i + 1)
                act.activation(rstd[:, i:i + 1], mv[:, i, 1:2], ACT.Sqrt, bias=eps_c[:, :]).then_inc(q.mixstd_ready, 1)

            act.wait_ge(q.x_done, NT)
            act.nop().then_inc(q.y_copied, KVB)

            def exp_rows(t, b):
                act.wait_ge(q.logit_ready, t + 1)
                act.activation(prob[:, b, :, :], logit[:, b, :, :], ACT.Exp).then_inc(q.prob_ready, 1)
                act.wait_ge(q.prob_ready, t + 1)
                for s in range(SD, S):
                    for h in range(HEADS):
                        val = KV[b][:, s, D + h * DK:D + (h + 1) * DK]
                        a = act.activation(val, val, ACT.Copy, scale=prob[:, b, s, h:h + 1])
                a.then_inc(q.pv_act, 1)

            def copy_rows(t, b):
                act.wait_ge(q.y_psum, t + 1)
                apart(act)
                act.copy(YR[:, bass.ds(t, 1), :, 0:DK],
                         bank[b][:, :].rearrange("p (a h d) -> p a h d", a=1, h=HEADS)).then_inc(q.y_copied, 1)

            exp_rows(0, 0)
            with act.Fori(0, RT // KVB) as n:
                for u in range(KVB):
                    exp_rows(n * KVB + u + 1, (u + 1) % KVB)
                    copy_rows(n * KVB + u, u)
            copy_rows(RT - 1, (RT - 1) % KVB)

            def seg_addend(g):
                act.wait_ge(q.seg_chunk, g + 1)
                a = seg[:, 4 * P * g:4 * P * (g + 1)]
                act.activation(a, a, ACT.Copy, scale=-BIG).then_inc(q.seg_scaled, 1)

            for g in range(MG):
                w = min(4 * P, RT * P - 4 * P * g)
                act.wait_ge(q.lt_psum, g + 1)
                act.copy(LT[:, 4 * P * g:4 * P * g + w], bank[g % 2][0:HEADS, 0:w]).then_inc(q.lt_done, 1)
                if g >= 2:
                    act.wait_ge(q.seg_chunk, g - 1)
                act.copy(nodes_c[g % 2][:, 1:w + 1], bank[2 + g % 2][0:HEADS, 0:w]).then_inc(q.nodes_in, 1)
                if g >= 2 and g % 2 == 0:
                    seg_addend(g - 1)
            act.wait_ge(q.w_ready, 1)
            act.activation(rowmax[:, :, :], rowmax[:, :, :], ACT.Exp).then_inc(q.w_exp, 1)
            for i in range(NT):
                act.wait_ge(q.yt_psum, i + 1)
                act.copy(YT[:, :, i * P:(i + 1) * P], bank[i % 2][:, :].rearrange("p (a b) -> p a b", a=KC)).then_inc(q.yt_done, 1)
            act.wait_ge(q.var_ready, 2)
            act.activation(rstd[:, :], mv[:, :, 1], ACT.Sqrt, bias=eps_c[:, :]).then_inc(q.std_ready, 1)
            for i in range(NT):
                act.wait_ge(q.ht_psum, i + 1)
                act.copy(HT[:, :, i * P:(i + 1) * P], bank[i % 2][:, :].rearrange("p (a b) -> p a b", a=KC)).then_inc(q.ht_done, 1)
            act.wait_ge(q.r_ready, 1)
            act.activation(rp[:, :, :], rl[:, :, :], ACT.Exp).then_inc(q.r_exp, 1)

            def load_rows(i, b):
                act.dma_start(hrow[:, b, :], sent_h.rearrange("(t p) d -> p t d", p=P)[:, bass.ds(i, 1), :]
                              .rearrange("p a d -> p (a d)")).then_inc(hrow_in[b], 16)

            def store_rows(i, b):
                act.wait_ge(q.ye_ready, i + 3)
                apart(act)
                act.dma_start(got_y.rearrange("(t p) d -> p t d", p=P)[:, bass.ds(i, 1), :]
                              .rearrange("p a d -> p (a d)"), yt[:, b, :]).then_inc(y_out[b], 16)

            def tokens_high(i, b, more=True):
                act.wait_ge(q.th_psum, i + 1)
                if more:
                    apart(act)
                    load_rows(i + 2, b)
                act.copy(hTt[:, b, 0, :, :], bank[0][:, :].rearrange("p (a b) -> p a b", a=KC)).then_inc(q.th_high, 1)

            def hidden(i, b):
                act.wait_ge(q.hid_biased, i + 1)
                act.activation(hid[:, b, :], hid[:, b, :], ACT.Gelu_apprx_tanh).then_inc(q.hid_ready, 1)
                act.wait_ge(q.hidT_psum, i + 1)
                act.copy(hidT[:, 0, :, :], psum[:, 3:5, :].rearrange("p a (c n) -> p (a c) n", c=4)).then_inc(q.hidT_high, 1)

            act.wait_ge(q.tokens_sent, 16 * NT * TOPK)
            load_rows(0, 0)
            load_rows(1, 1)
            tokens_high(0, 0)
            tokens_high(1, 1)
            hidden(0, 0)
            with act.Fori(0, (XT - 5) // 2) as n:
                for u in range(2):
                    tokens_high(n * 2 + u + 2, u)
                    hidden(n * 2 + u + 1, 1 - u)
                    store_rows(n * 2 + u, u)
            for i in range(XT - 5, XT):
                if i + 2 < XT:
                    tokens_high(i + 2, i % 2, more=i + 4 < XT)
                if i + 1 < XT:
                    hidden(i + 1, (i + 1) % 2)
                store_rows(i, i % 2)

        @block.tensor
        def _(pe):
            pe.wait_ge(q.consts, 1)

            def three_passes(to, high, low, w_of, n):
                for c in range(n):
                    for k, (x_of, part) in enumerate(((high, 0), (high, 1), (low, 0))):
                        mm = nc.tensor.matmul(to, x_of(c), w_of(c, part), start=c == k == 0, stop=c == n - 1 and k == 2)
                return mm

            def transpose_tile(g, of):
                if g >= 2:
                    pe.wait_ge(q.tr_done, g - 1)
                for c in range(KC):
                    mm = nc.tensor.transpose(bank[g % 2][:, c * P:(c + 1) * P], of[:, c * P:(c + 1) * P], ident[:, :])
                mm.then_inc(q.tr_psum, 1)

            for i in range(NT):
                pe.wait_ge(q.xn_ready, i + 1)
                transpose_tile(i, xn[i % 2])
            pe.wait_ge(q.tr_done, NT)
            pe.wait_ge(wts["wqkv"], 48)

            def sort_pe(g, n, u, first, last):
                if not last:
                    pe.wait_ge(q.onehot_lo_ready, g + 1)
                    for c in range(EG):
                        mm = nc.tensor.transpose(bf(u % 2)[:, c * P:(c + 1) * P], onehot_lo[:, u, c, :], identb[:, :])
                    mm.then_inc(q.loT_psum, 1)
                if first != 2 and last != 2:
                    pe.wait_ge(q.loT_ready, g)
                    for c in range(EG):
                        low = onehot_loT.rearrange("p (g c) b -> p g c b", c=EG)[:, bass.ds(g - 1, 1), c, :].rearrange("p a b -> p (a b)")
                        mm = nc.tensor.matmul(bank[2 + (u - 1) % 2][:, c * P:(c + 1) * P], low, low, start=True, stop=True)
                    mm.then_inc(q.same_psum, 1)
                if not first:
                    pe.wait_ge(q.before_ready, g - 1)
                    if not isinstance(g, int) or g >= 4:
                        pe.wait_ge(q.counts_ready, g - 3)
                    for lhs, off in ((onehot_lo[:, (u - 2) % TURN, :, :], 0), (before[:, u % 2, :, :], EG)):
                        for c in range(EG):
                            mm = nc.tensor.matmul(bank[4 + u % 2][:, (off + c) * NT:(off + c + 1) * NT], lhs[:, c, :],
                                                  onehot_hi.rearrange("p (g c) b -> p g c b", c=EG)[:, bass.ds(g - 2, 1), c, :]
                                                  .rearrange("p a b -> p (a b)"),
                                                  start=True, stop=True)
                    mm.then_inc(q.counts_psum, 1)
                if u == 0 and not last:
                    pe.wait_ge(q.xs_ready, n + 1)
                    if not isinstance(n, int) or n > 0:
                        pe.wait_ge(q.send_ready, n)
                    for c in range(KC):
                        mm = nc.tensor.matmul(bank[6][:, :], XNs[:, c, :], Wqkv[:, 0, c, :], start=c == 0, stop=c == KC - 1)
                    mm.then_inc(q.unit_psum, 1)

            in_turns(pe, sort_pe)
            pe.wait_ge(q.counts_ready, GROUPS)

            def keys_values(ms):
                for m in ms:
                    i = m % NT
                    if m >= 2:
                        pe.wait_ge(q.send_ready, NT + m - 1)
                    for c in range(KC):
                        mm = nc.tensor.matmul(bank[4 + m % 2][:, :], XNT[:, c, i * P:(i + 1) * P], Wqkv[:, 1 + m // NT, c, :],
                                              start=c == 0, stop=c == KC - 1)
                    mm.then_inc(q.unit_psum, 1)

            keys_values(range(1))
            pe.wait_ge(q.rowcount_ready, 1)
            nc.tensor.matmul(bank[3][:, 0:NT], low_f[:, :], rows_f[:, :], start=True, stop=True)
            nc.tensor.matmul(bank[3][:, NT:2 * NT], ones_f[:, :], rows_f[:, :], start=True, stop=True).then_inc(q.prefix_psum, 1)
            keys_values(range(1, VA))
            pe.wait_ge(q.first_ready, 1)

            def look_up(g, b):
                for c in range(LG):
                    mm = nc.tensor.matmul(bank[6 + b][:, c * 2 * NT:(c + 1) * 2 * NT],
                                          onehot_loT[:, g * LG + c, :],
                                          first_b[:, g * LG + c, :, :].rearrange("p a b -> p (a b)"),
                                          start=True, stop=True)
                mm.then_inc(q.found_psum, 1)

            look_up(0, 0)
            look_up(1, 1)
            for g in range(2, ET // LG):
                pe.wait_ge(q.parts_ready, g - 1)
                look_up(g, g % 2)
            keys_values(range(VA, NT))
            pe.wait_ge(wts["raw_q"], 16)

            def transpose_weights(k, of):
                if k >= 2:
                    pe.wait_ge(q.mix_low, min(k - 1, 8) if k < 14 else k - 5)
                transpose_tile(NT + k, of)

            for g in range(4):
                transpose_weights(g, raw[:, g, :])
            keys_values(range(NT, NT + VA))
            pe.wait_ge(wts["raw_k"], 16)
            for g in range(4, 8):
                transpose_weights(g, raw[:, g, :])
            keys_values(range(NT + VA, 2 * NT))
            pe.wait_ge(wts["rawo"], 16)
            for g in range(4):
                transpose_weights(8 + g, raw_o[:, g, :])
            pe.wait_ge(wts["raw_v"], 16)
            for g in range(4):
                transpose_weights(12 + g, raw_v[:, g, :])
            pe.wait_ge(q.tr_done, NT + 16)
            pe.wait_ge(q.mix_low, 12)
            pe.wait_ge(q.x_low, NT)

            def mix_weights(u, c, part, o=0, w=D):
                return mixTl[u][:, c, o:o + w] if part else mixT[:, c, u * D + o:u * D + o + w]

            def project(u, i, which):
                if u >= 2:
                    pe.wait_ge(q.lin_done, u - 1)
                a = slice(i * P, (i + 1) * P)
                three_passes(bank[2 + u % 2][:, :], lambda c: XNTh[:, c, a], lambda c: XNTl[:, c, a],
                             lambda c, part: mix_weights(which, c, part), KC).then_inc(q.lin_psum, 1)

            for i in range(NT + 2):
                if i < NT:
                    project(i, i, 0)
                if i >= 2:
                    pe.wait_ge(q.q_ready, i - 1)
                    if i >= 4:
                        pe.wait_ge(q.qt_done, i - 3)
                    for c in range(KC):
                        mm = nc.tensor.transpose(bank[i % 2][:, c * P:(c + 1) * P], qs[(i - 2) % 3][:, c * P:(c + 1) * P], ident[:, :])
                    mm.then_inc(q.qt_psum, 1)
            for c in range(KC):
                if c >= 1:
                    pe.wait_ge(q.kt_exp, 3 * c)
                for i, (o, w) in enumerate(NCH):
                    mm = three_passes(bank[4 + i][:, 0:w], lambda k: mix_weights(1, k, 0, c * P, P), lambda k: mix_weights(1, k, 1, c * P, P),
                                      lambda k, part: (XNTl if part else XNTh)[:, k, o:o + w], KC)
                mm.then_inc(q.kt_psum, 1)
                for i in range(NT * c // KC, NT * (c + 1) // KC):
                    project(NT + i, i, 2)
            pe.wait_ge(q.kt_exp, 3 * KC)
            pe.wait_ge(q.qt_done, NT)
            for i in range(NT):
                r = rows_of(i)
                if i >= 2:
                    pe.wait_ge(q.ke_done, i - 1)
                for c in range(KC):
                    mm = nc.tensor.transpose(bank[i % 2][0:r, c * P:(c + 1) * P], KT[:, c, i * P:i * P + r], ident[:, :])
                mm.then_inc(q.ke_psum, 1)
            pe.wait_ge(q.ke_done, NT)
            pe.wait_ge(q.lin_done, 2 * NT)
            for c in range(KC):
                for i in range(NT):
                    r = rows_of(i)
                    mm = nc.tensor.matmul(bank[7][:, c * P:(c + 1) * P], V[0:r, i, c * P:(c + 1) * P], KE[0:r, i, c * P:(c + 1) * P],
                                          start=i == 0, stop=i == NT - 1)
            mm.then_inc(q.ctx_psum, 1)
            pe.wait_ge(q.ctx_ready, 1)
            for c in range(KC):
                if c >= 2:
                    pe.wait_ge(q.m_ready, c - 1)
                nc.tensor.matmul(bank[4 + c % 2][:, :], ctxbd[:, c, :], WoT[:, c, :], start=True, stop=True).then_inc(q.m_psum, 1)
            pe.wait_ge(q.m_ready, KC)
            for i in range(NT):
                if i >= 3:
                    pe.wait_ge(q.mix_copied, i - 2)
                for c in range(KC):
                    mm = nc.tensor.matmul(bank[2 + i % 3][:, :], QT[:, c, i * P:(i + 1) * P], Mx[:, c, :], start=c == 0, stop=c == KC - 1)
                mm.then_inc(q.mix_psum, 1)

            pe.wait_ge(q.x_done, NT)

            def sum_rows(t, b):
                pe.wait_ge(q.pv_ready, t + 1)
                pe.wait_ge(q.y_copied, t + 1)
                for s in range(S):
                    if s == SD:
                        pe.wait_ge(q.pv_act, t + 1)
                    mm = nc.tensor.matmul(bank[b][:, :], ident[:, :], KV[b][:, s, D:2 * D], start=s == 0, stop=s == S - 1)
                mm.then_inc(q.y_psum, 1)

            with pe.Fori(0, RT // KVB) as n:
                for u in range(KVB):
                    sum_rows(n * KVB + u, u)
            for t in range(RT // KVB * KVB, RT):
                sum_rows(t, t % KVB)
            pe.wait_ge(q.nodes_ready, 1)
            pe.wait_ge(q.y_copied, RT + KVB)
            for g in range(MG):
                if g >= 2:
                    pe.wait_ge(q.lt_done, g - 1)
                    pe.wait_ge(q.nodes_in, g - 1)
                ts = range(4 * g, min(RT, 4 * g + 4))
                for t in ts:
                    nc.tensor.transpose(bank[g % 2][0:HEADS, (t % 4) * P:(t % 4 + 1) * P], rowmax[:, t, :], ident[:, :])
                for t in ts:
                    mm = nc.tensor.transpose(bank[2 + g % 2][0:HEADS, (t % 4) * P:(t % 4 + 1) * P], nodes8[:, t, :], ident[:, :])
                mm.then_inc(q.lt_psum, 1)
            pe.wait_ge(q.m_scan, 1)
            for t in range(RT):
                mm = nc.tensor.transpose(bank[4][:, t * HEADS:(t + 1) * HEADS], LT[:, t * P:(t + 1) * P], ident[0:HEADS, 0:HEADS])
            mm.then_inc(q.m_back, 1)

            def merge(t, j, n=None):
                rows = YR[:, t:t + 1] if n is None else YR[:, 0:RT // 4 * 4].rearrange("p (n j) h d -> p n j h d", j=4)[:, bass.ds(n, 1), j]
                pe.wait_ge(q.onehot_n_ready, t + 1)
                pe.wait_ge(q.yr_scaled, t + 1)
                pe.wait_ge(q.merged, t + 1)
                for b in range(2):
                    for h in range(2):
                        mm = nc.tensor.matmul(bank[4 * (j % 2) + 2 * b + h][:, 0:4 * YW], onehot_n[:, j, b * P:(b + 1) * P],
                                              rows[:, :, 4 * h:4 * h + 4, :].rearrange("p a h d -> p (a h d)"),
                                              start=True, stop=True)
                mm.then_inc(q.merge_psum, 1)

            with pe.Fori(0, RT // 4) as n:
                for j in range(4):
                    merge(n * 4 + j, j, n)
            merge(RT - 1, 0)
            for i in range(NT):
                pe.wait_ge(q.yn_ready, i + 1)
                if i >= 2:
                    pe.wait_ge(q.yt_done, i - 1)
                for c in range(KC):
                    mm = nc.tensor.transpose(bank[i % 2][:, c * P:(c + 1) * P], YN[:, i, c * P:(c + 1) * P], ident[:, :])
                mm.then_inc(q.yt_psum, 1)
            pe.wait_ge(wts["wo"], 16)
            for i in range(NT):
                pe.wait_ge(q.yt_done, i + 1)
                if i >= 2:
                    pe.wait_ge(q.wo_done, i - 1)
                for c in range(KC):
                    mm = nc.tensor.matmul(bank[2 + i % 2][:, :], YT[:, c, i * P:(i + 1) * P], Wo_s[:, c, :], start=c == 0, stop=c == KC - 1)
                mm.then_inc(q.wo_psum, 1)
            for i in range(NT):
                pe.wait_ge(q.h_ready, i + 1)
                if i >= 2:
                    pe.wait_ge(q.ht_done, i - 1)
                for c in range(KC):
                    mm = nc.tensor.transpose(bank[i % 2][:, c * P:(c + 1) * P], hn[:, i, c * P:(c + 1) * P], ident[:, :])
                mm.then_inc(q.ht_psum, 1)
            pe.wait_ge(wts["wg"], 16)
            pe.wait_ge(q.wo_done, NT)
            pe.wait_ge(q.ht_done, NT)
            for i in range(NT):
                for c in range(KC):
                    mm = nc.tensor.matmul(bank[2][:, i * NE:(i + 1) * NE], HT[:, c, i * P:(i + 1) * P], Wg_s[:, c, :], start=c == 0, stop=c == KC - 1)
            mm.then_inc(q.r_psum, 1)
            pe.wait_ge(q.both_ready, 1)
            nc.tensor.matmul(bank[3][:, 0:NT * NE], low_f[:, :], both[:, :, :].rearrange("p t e -> p (t e)"), start=True, stop=True)
            nc.tensor.matmul(bank[4][:, 0:NT * NE], ones_f[:, :], both[:, :, :].rearrange("p t e -> p (t e)"), start=True, stop=True).then_inc(q.ranks_psum, 1)
            pe.wait_ge(q.owners_ready, 1)

            def transpose_tokens(b, count):
                pe.wait_ge(hrow_in[b], count)
                for c in range(KC):
                    mm = nc.tensor.transpose(bank[0][:, c * P:(c + 1) * P], hrow[:, b, c * P:(c + 1) * P], ident[:, :])
                mm.then_inc(q.th_psum, 1)

            def up(i, b):
                slot = pe.value_load(owner_slot[0:1, bass.ds(i, 1)], min_val=0, max_val=1)
                need = pe.value_load(owner_need[0:1, bass.ds(i, 1)], min_val=1, max_val=2 * NE)
                pe.wait_ge(q.weights_split, need)
                pe.wait_ge(q.th_ready, i + 1)
                for h in range(HH):
                    mm = three_passes(bank[1 + h][:, :], lambda c: hTt[:, b, 0, c, :], lambda c: hTt[:, b, 1, c, :],
                                      lambda c, part: W1_s[:, bass.ds(slot, 1), part, c * HID + h * 512:c * HID + (h + 1) * 512]
                                      .rearrange("p a n -> p (a n)"), KC)
                mm.then_inc(q.hid_psum, 1)
                return slot

            def down(i, b):
                slot = pe.value_load(owner_slot[0:1, bass.ds(i, 1)], min_val=0, max_val=1)
                need = pe.value_load(owner_need[0:1, bass.ds(i, 1)], min_val=1, max_val=2 * NE)
                pe.wait_ge(q.weights_split, need + 1)
                pe.wait_ge(q.hidT_ready, i + 1)
                pe.wait_ge(q.ye_ready, i + 1)
                mm = three_passes(bank[5 + b][:, :], lambda c: hidT[:, 0, c, :], lambda c: hidT[:, 1, c, :],
                                  lambda c, part: W2_s[:, bass.ds(slot, 1), part, c * D:(c + 1) * D]
                                  .rearrange("p a n -> p (a n)"), HC)
                mm.then_inc(q.ye_psum, 1)

            def transpose_hidden(i, b):
                pe.wait_ge(q.hid_ready, i + 1)
                for c in range(HC):
                    mm = nc.tensor.transpose(bank[3 + c // 4][:, (c % 4) * P:(c % 4 + 1) * P], hid[:, b, c * P:(c + 1) * P], ident[:, :])
                mm.then_inc(q.hidT_psum, 1)

            transpose_tokens(0, 16)
            up(0, 0)
            transpose_tokens(1, 16)
            transpose_hidden(0, 0)
            with pe.Fori(0, (XT - 1) // 2 - 1) as n:
                for u in range(2):
                    b = 1 - u
                    i = n * 2 + u + 1
                    up(i, b)
                    transpose_tokens(u, n * 16 + 32)
                    down(n * 2 + u, u)
                    transpose_hidden(i, b)
            for i in range(XT - 2, XT):
                up(i, i % 2)
                if i < XT - 1:
                    transpose_tokens((i + 1) % 2, 16 * ((i + 1) // 2 + 1))
                down(i - 1, (i - 1) % 2)
                transpose_hidden(i, i % 2)
            down(XT - 1, (XT - 1) % 2)

        @block.vector
        def _(dve):
            v = Steps(dve, q.dve)
            V_ = nc.vector

            def norm_stats(of):
                for i in range(NT):
                    v.link(V_.bn_stats(stats[:, :], of(i)))
                    v.link(V_.bn_aggr(mv[:, i, :], stats[:, :]))

            dve.wait_ge(q.x_in, 32)
            norm_stats(lambda i: X[:, i, :])
            dve.nop().then_inc(q.var_ready, 1)
            dve.wait_ge(q.std_ready, 1)
            v.link(V_.reciprocal(rstd[:, :], rstd[:, :]))
            for i in range(NT):
                if i >= 2:
                    dve.wait_ge(q.tr_psum, i - 1)
                V_.tensor_scalar(xn[i % 2][:, :], X[:, i, :], mv[:, i, 0:1], rstd[:, i:i + 1], ALU.subtract, ALU.mult).then_inc(q.xn_ready, 1)
            dve.wait_ge(q.consts, 1)
            dve.wait_ge(q.edges_in, 48)
            v.link(V_.tensor_scalar(part_i[:, :], src_i[:, :], P - 1, None, ALU.bitwise_and))
            v.link(V_.tensor_copy(lo_b[:, :], part_i[:, :]))
            v.link(V_.tensor_scalar(part_i[:, :], src_i[:, :], 7, None, ALU.logical_shift_right))
            v.link(V_.tensor_copy(hi_b[:, :], part_i[:, :]))
            v.link(V_.tensor_tensor(onehot_hi[:, :, :], iota10[:, :].unsqueeze(1).broadcast_to([P, ET, NT]),
                                    hi_b[:, :].unsqueeze(2).broadcast_to([P, ET, NT]), ALU.is_equal))
            V_.tensor_copy(records[:, :, 0], dst_i[:, :])
            V_.tensor_copy(records[:, :, 1], src_i[:, :])
            V_.tensor_copy(records[:, :, 2:REC], att[:, :].rearrange("p (t h) -> p t h", h=HEADS)).then_inc(q.records_ready, 1)

            def send_queries(n):
                dve.wait_ge(q.unit_psum, n + 1)
                if not isinstance(n, int) or n > 0:
                    dve.wait_ge(sent[0], n * 16)
                V_.tensor_tensor(send[0][:, :], bank[6][:, :], bias_q[:, :], ALU.add).then_inc(q.send_ready, 1)

            def send_rows(m):
                dve.wait_ge(q.unit_psum, NT + m + 1)
                if m != 1:
                    dve.wait_ge(sent[m % 2], 16 * (m // 2 + (0 if m % 2 else NT)))
                V_.tensor_tensor(send[m % 2][:, :], bank[4 + m % 2][:, :], (bias_k, bias_v)[m // NT][:, :], ALU.add).then_inc(q.send_ready, 1)

            def sort_dve(g, n, u, first, last):
                if not last:
                    if not isinstance(g, int) or g >= TURN:
                        dve.wait_ge(q.counts_psum, g - 3)
                    V_.tensor_tensor(onehot_lo[:, u, :, :], iotab[:, :].unsqueeze(1).broadcast_to([P, EG, P]),
                                     lo_b[:, bass.ds(g * EG, EG)].unsqueeze(2).broadcast_to([P, EG, P]), ALU.is_equal).then_inc(q.onehot_lo_ready, 1)
                if not first:
                    dve.wait_ge(q.same_psum, g - 1)
                    if not isinstance(g, int) or g >= 4:
                        dve.wait_ge(q.counts_psum, g - 3)
                    V_.tensor_tensor(before[:, u % 2, :, :], bank[2 + u % 2].rearrange("p (a b) -> p a b", a=EG),
                                     lowb[:, :].unsqueeze(1).broadcast_to([P, EG, P]), ALU.mult).then_inc(q.before_ready, 1)
                if u == 1 and not last:
                    send_queries(n)

            dve.wait_ge(wts["bias"], 64)
            in_turns(dve, sort_dve)
            dve.wait_ge(q.counts_ready, ET // EG)
            for h in range(NT):
                V_.tensor_tensor_scan(upto[:, :, h], count[:, :, h], zeros_r[:, :], 0.0, ALU.add, ALU.add).then_inc(q.dve, 1)
                v.k += 1
            dve.wait_ge(q.dve, v.done + v.k)
            v.link(V_.tensor_scalar(deg[:, :], upto[:, ET - 1, :], float(S - 1), None, ALU.add))
            v.link(V_.tensor_copy(deg_i[:, :], deg[:, :]))
            v.link(V_.tensor_scalar(deg_i[:, :], deg_i[:, :], S.bit_length() - 1, None, ALU.logical_shift_right))
            v.link(V_.tensor_copy(deg[:, :], deg_i[:, :]))
            V_.tensor_scalar(rows_f[:, :], deg[:, :], 1.0, None, ALU.max).then_inc(q.rowcount_ready, 1)
            send_rows(0)
            v.link(V_.tensor_tensor(first_f[:, :, :], upto[:, :, :], count[:, :, :], ALU.subtract))
            dve.wait_ge(q.prefix_psum, 1)
            v.link(V_.tensor_copy(rows_in[:, :], bank[3][:, 0:NT]))
            v.link(V_.tensor_copy(tot[:, :], bank[3][:, NT:2 * NT]))
            v.link(V_.tensor_tensor_scan(blk0[:, :], tot[:, :], zeros_r[:, 0:NT], 0.0, ALU.add, ALU.add))
            v.link(V_.tensor_tensor(blk0[:, :], blk0[:, :], tot[:, :], ALU.subtract))
            v.link(V_.tensor_tensor(start4[:, :], rows_in[:, :], blk0[:, :], ALU.add))
            v.link(V_.tensor_scalar(start4[:, :], start4[:, :], float(S), None, ALU.mult))
            v.link(V_.tensor_tensor(first_f[:, :, :], first_f[:, :, :], start4[:, :].unsqueeze(1).broadcast_to([P, ET, NT]), ALU.add))
            v.link(V_.tensor_copy(first_i[:, :, :], first_f[:, :, :]))
            send_rows(1)
            v.link(V_.tensor_scalar(halves_i[:, :, :], first_i[:, :, :], 8, None, ALU.logical_shift_right))
            v.link(V_.tensor_copy(first_b[:, :, 0, :], halves_i[:, :, :]))
            send_rows(2)
            v.link(V_.tensor_scalar(halves_i[:, :, :], first_i[:, :, :], 255, None, ALU.bitwise_and))
            v.link(V_.tensor_copy(first_b[:, :, 1, :], halves_i[:, :, :]))
            dve.nop().then_inc(q.first_ready, 1)
            for i in range(3, VA):
                send_rows(i)
            v.link(V_.tensor_tensor(within[:, :, :], within[:, :, :], onehot_hi[:, :, :], ALU.mult))
            v.link(V_.tensor_reduce(ranks[:, :], within[:, :, :], AX.X, ALU.add))
            with dve.Fori(0, ET // LG // 2) as n:
                v.enter(n, 4)
                for b in range(2):
                    g = n * 2 + b
                    dve.wait_ge(q.found_psum, g + 1)
                    v.link(V_.tensor_tensor(found[:, :, :, :], bank[6 + b][:, 0:LG * 2 * NT].rearrange("p (a b c) -> p a b c", a=LG, b=2),
                                            onehot_hi[:, bass.ds(g * LG, LG), :].unsqueeze(2).broadcast_to([P, LG, 2, NT]), ALU.mult))
                    v.link(V_.tensor_reduce(parts[:, bass.ds(g * LG, LG), :], found[:, :, :, :], AX.X, ALU.add))
                    dve.nop().then_inc(q.parts_ready, 1)
            v.leave(ET // LG // 2)
            dve.wait_ge(q.parts_ready, ET // LG)
            v.link(V_.scalar_tensor_tensor(place_f[:, :], parts[:, :, 0], 256.0, parts[:, :, 1], ALU.mult, ALU.add))
            v.link(V_.tensor_tensor(place_f[:, :], place_f[:, :], ranks[:, :], ALU.add))
            dve.wait_ge(q.records_ready, 1)
            v.link(V_.tensor_copy(place_i[:, :], place_f[:, :]))
            dve.nop().then_inc(q.places_ready, 1)
            v.link(V_.tensor_tensor(cmp_b[:, :, :], blk0[:, :].unsqueeze(1).broadcast_to([P, RT, NT]),
                                    tile0[:, :].unsqueeze(2).broadcast_to([P, RT, NT]), ALU.is_le))
            v.link(V_.tensor_reduce(block_f[:, :], cmp_b[:, :, :], AX.X, ALU.add))
            v.link(V_.tensor_scalar(block_f[:, :], block_f[:, :], -1.0, None, ALU.add))
            v.link(V_.tensor_scalar(nodebase[:, :], block_f[:, :], float(P), None, ALU.mult))
            v.link(V_.tensor_copy(block_i[:, :], block_f[:, :]))

            def weights_low(g):
                dve.wait_ge(q.tr_done, NT + g + 1 + (4 if g >= 8 else 0))
                o = slice(g % 4 * P, (g % 4 + 1) * P)
                V_.tensor_tensor(mixTl[g // 4][:, :, o], bank[(NT + g) % 2].rearrange("p (a b) -> p a b", a=KC),
                                 mixT[:, :, g * P:(g + 1) * P].bitcast(F32), ALU.subtract).then_inc(q.mix_low, 1)

            def nodes_low(i):
                a = slice(i * P, (i + 1) * P)
                dve.wait_ge(q.unit_psum, 2 * NT + i + 1)
                dve.wait_ge(q.x_high, i + 1)
                V_.tensor_tensor(XNTl[:, :, a], XNT[:, :, a], XNTh[:, :, a].bitcast(F32), ALU.subtract).then_inc(q.x_low, 1)

            for m in range(VA, NT):
                send_rows(m)
            for g in range(4):
                weights_low(g)
            for i in range(VA):
                send_rows(NT + i)
            for g in range(4, 8):
                weights_low(g)
            for i in range(VA, NT):
                send_rows(NT + i)
                nodes_low(i - VA)
            for i in range(VA, NT):
                nodes_low(i)
            for g in range(8, 12):
                weights_low(g)

            def q_finish(i):
                dve.wait_ge(q.q_exp, i + 1)
                t = qs[i % 3][:, :].rearrange("p (h d) -> p h d", h=HEADS)
                v.link(V_.tensor_reduce(qsum[:, :], t, AX.X, ALU.add))
                v.link(V_.reciprocal(qrec[:, :], qsum[:, :]))
                v.link(V_.tensor_scalar(qrec[:, :], qrec[:, :], DK ** -0.5, None, ALU.mult))
                V_.tensor_tensor(t, t, qrec[:, :].unsqueeze(2).broadcast_to([P, HEADS, DK]), ALU.mult).then_inc(q.q_ready, 1)

            for i in range(NT):
                dve.wait_ge(q.lin_psum, i + 1)
                if i >= 3:
                    dve.wait_ge(q.qt_psum, i - 2)
                b = bank[2 + i % 2][:, :].rearrange("p (h d) -> p h d", h=HEADS)
                v.link(V_.tensor_reduce(qmax[:, :], b, AX.X, ALU.max))
                v.link(V_.tensor_tensor(qs[i % 3][:, :].rearrange("p (h d) -> p h d", h=HEADS), b,
                                        qmax[:, :].unsqueeze(2).broadcast_to([P, HEADS, DK]), ALU.subtract))
                dve.nop().then_inc(q.lin_done, 1)
                dve.nop().then_inc(q.q_sub, 1)
                if i >= 1:
                    q_finish(i - 1)
            q_finish(NT - 1)
            for c in range(KC):
                dve.wait_ge(q.kt_psum, c + 1)
                for i, (o, w) in enumerate(NCH):
                    v.link(V_.tensor_reduce(kmax3[:, c, i:i + 1], bank[4 + i][:, 0:w], AX.X, ALU.max))
                v.link(V_.tensor_reduce(kneg[:, c:c + 1], kmax3[:, c, :], AX.X, ALU.max))
                v.link(V_.tensor_scalar(kneg[:, c:c + 1], kneg[:, c:c + 1], -1.0, None, ALU.mult))
                dve.nop().then_inc(q.kmax_ready, 1)
                for i in range(NT * c // KC, NT * (c + 1) // KC):
                    dve.wait_ge(q.lin_psum, NT + i + 1)
                    V_.tensor_copy(V[:, i, :], bank[2 + i % 2][:, :]).then_inc(q.lin_done, 1)
            dve.wait_ge(q.kt_exp, 3 * KC)
            v.link(V_.tensor_reduce(krec[:, :], ksum3[:, :, :], AX.X, ALU.add))
            v.link(V_.reciprocal(krec[:, :], krec[:, :]))
            dve.wait_ge(q.ke_done, NT)
            v.link(V_.memset(ctxbd[:, :, :], 0.0))
            dve.wait_ge(q.ctx_psum, 1)
            for h in range(2):
                a = slice(h * DK, (h + 1) * DK)
                v.link(V_.tensor_copy(ctxbd[a, :, a], bank[7][:, :].rearrange("p (c d) -> p c d", c=KC)[a, :, a]))
            dve.nop().then_inc(q.ctx_ready, 1)
            for c in range(KC):
                dve.wait_ge(q.m_psum, c + 1)
                V_.tensor_scalar(Mx[:, c, :], bank[4 + c % 2][:, :], krec[:, c:c + 1], None, ALU.mult).then_inc(q.m_ready, 1)
            dve.wait_ge(wts["gamma"], 16)

            def mix_finish(i):
                dve.wait_ge(q.mixstd_ready, i + 1)
                v.link(V_.reciprocal(rstd[:, i:i + 1], rstd[:, i:i + 1]))
                m = mixo[i % 2][:, :]
                V_.tensor_scalar(m, bank[2 + i % 3][:, :], mv[:, i, 0:1], rstd[:, i:i + 1], ALU.subtract, ALU.mult).then_inc(q.mix_copied, 1)
                dve.wait_ge(q.mix_copied, i + 1)
                v.link(V_.tensor_tensor(m, m, gamma_b[:, :], ALU.mult))
                V_.tensor_tensor(X[:, i, :], X[:, i, :], m, ALU.add).then_inc(q.x_done, 1)
                dve.wait_ge(q.x_done, i + 1)

            for i in range(NT):
                dve.wait_ge(q.mix_psum, i + 1)
                v.link(V_.bn_stats(stats[:, :], bank[2 + i % 3][:, :]))
                V_.bn_aggr(mv[:, i, :], stats[:, :]).then_inc(q.mixvar_ready, 1)
                dve.wait_ge(q.mixvar_ready, i + 1)
                if i >= 1:
                    mix_finish(i - 1)
            mix_finish(NT - 1)

            dve.wait_ge(wts["table"], 16)

            def multiply(b, arrived):
                dve.wait_ge(gath[b], arrived)
                k = KV[b][:, :, 0:D]
                v.link(V_.tensor_tensor(k, k, QG[b][:, :].unsqueeze(1).broadcast_to([P, S, D]), ALU.mult))

            def logits(t, b):
                k, lg = KV[b][:, :, 0:D], logit[:, b, :, :]
                rm = rowmax[:, bass.ds(t, 1), :].rearrange("p a h -> p (a h)")
                v.link(V_.tensor_reduce(lg, k.rearrange("p s (h d) -> p s h d", h=HEADS), AX.X, ALU.add))
                v.link(V_.scalar_tensor_tensor(lg, lg, DK ** -0.5, table[:, bass.ds(t, 1), :, 2:REC]
                                               .rearrange("p a s h -> p (a s) h"), ALU.mult, ALU.add))
                v.link(V_.tensor_reduce(rm, lg.rearrange("p s h -> p h s"), AX.X, ALU.max))
                v.link(V_.tensor_scalar(rowfloor[:, :], rm, -BIG / 10, None, ALU.max))
                V_.tensor_tensor(lg, lg, rowfloor[:, :].unsqueeze(1).broadcast_to([P, S, HEADS]), ALU.subtract).then_inc(q.logit_ready, 1)

            def weigh(t, b):
                dve.wait_ge(q.prob_ready, t + 1)
                p, val = prob[:, b, :, :], KV[b][:, :, D:2 * D].rearrange("p s (h d) -> p s h d", h=HEADS)
                V_.tensor_tensor(val[:, 0:SD], val[:, 0:SD], p[:, 0:SD].unsqueeze(3).broadcast_to([P, SD, HEADS, DK]), ALU.mult).then_inc(q.pv_ready, 1)
                V_.tensor_reduce(YR[:, bass.ds(t, 1), :, DK].rearrange("p a h -> p (a h)"), p.rearrange("p s h -> p h s"),
                                 AX.X, ALU.add).then_inc(q.den_ready, 1)

            multiply(0, 16 * (S + 1))
            logits(0, 0)
            with dve.Fori(0, RT // KVB) as n:
                v.enter(n, 5 * KVB)
                for u in range(KVB):
                    t = n * KVB + u
                    multiply((u + 1) % KVB, (n + (u + 1) // KVB) * (16 * (S + 1)) + 16 * (S + 1))
                    weigh(t, u)
                    logits(t + 1, (u + 1) % KVB)
            v.leave(RT // KVB)
            weigh(RT - 1, (RT - 1) % KVB)
            dve.wait_ge(q.den_ready, RT)

            v.link(V_.tensor_copy(nodes8[:, :, :], table[:, :, 0, 1:2].broadcast_to([P, RT, HEADS])))
            v.link(V_.tensor_tensor(node_off[:, :], table[:, :, 0, 1], nodebase[:, :], ALU.subtract))
            dve.nop().then_inc(q.nodes_ready, 1)
            dve.wait_ge(q.y_psum, RT)
            v.link(V_.memset(nodes_c[0][:, 0:1], -1.0))
            for g in range(MG):
                w = min(4 * P, RT * P - 4 * P * g)
                dve.wait_ge(q.lt_psum, g + 1)
                here = nodes_c[g % 2]
                dve.wait_ge(q.nodes_in, g + 1)
                V_.tensor_tensor(seg[:, 4 * P * g:4 * P * g + w], here[:, 1:w + 1], here[:, 0:w], ALU.not_equal)
                V_.tensor_copy(nodes_c[1 - g % 2][:, 0:1], here[:, w:w + 1]).then_inc(q.seg_chunk, 1)
                dve.wait_ge(q.seg_chunk, g + 1)
            dve.wait_ge(q.seg_scaled, MG)
            v.link(V_.memset(seg[:, RT * P:RT * P + 1], -BIG))
            dve.wait_ge(q.lt_done, MG)
            v.link(V_.tensor_tensor_scan(LT[:, :], seg[:, 0:RT * P], LT[:, :], -BIG, ALU.add, ALU.max))
            V_.tensor_tensor_scan(LT[:, ::-1], seg[:, 1:RT * P + 1][:, ::-1], LT[:, ::-1], -BIG, ALU.add, ALU.max).then_inc(q.m_scan, 1)
            dve.wait_ge(q.m_back, 1)
            v.link(V_.tensor_scalar(Mrow[:, :, :], bank[4][:, 0:RT * HEADS].rearrange("p (t h) -> p t h", h=HEADS), -BIG / 10, None, ALU.max))
            V_.tensor_tensor(rowmax[:, :, :], rowmax[:, :, :], Mrow[:, :, :], ALU.subtract).then_inc(q.w_ready, 1)
            v.link(V_.memset(Y[:, :, :, :], 0.0))
            dve.wait_ge(q.w_exp, 1)
            dve.nop().then_inc(q.merged, 2)

            def node_onehot(t, j, n=None):
                off = node_off[:, t:t + 1] if n is None else (
                    node_off[:, 2:2 + RT // 4 * 4 - 4].rearrange("p (n j) -> p n j", j=4)[:, bass.ds(n, 1), j - 2])
                V_.tensor_scalar(onehot_n[:, j % 4, :], iota256[:, :], off, None, ALU.is_equal).then_inc(q.onehot_n_ready, 1)

            def block_of(t):
                return dve.value_load(block_i[0:1, bass.ds(t, 1)], min_val=0, max_val=NT - 1)

            def add_rows(t, j, blk):
                dve.wait_ge(q.merged, t + 2)
                dve.wait_ge(q.merge_psum, t + 1)
                y = Y[:, bass.ds(blk, 2), :, :].rearrange("p a (g h) d -> p (a g) (h d)", g=2)
                V_.tensor_tensor(y, y, psum[:, 4 * j:4 * j + 4, 0:4 * YW], ALU.add).then_inc(q.merged, 1)

            assert RT % 4 == 1
            node_onehot(0, 0)
            node_onehot(1, 1)
            with dve.Fori(0, RT // 4 - 1) as n:
                blk = block_of(n * 4)
                for j in range(4):
                    node_onehot(n * 4 + j + 2, j + 2, n)
                    add_rows(n * 4 + j, j % 2, blk)
                    if j < 3:
                        blk = block_of(n * 4 + j + 1)
            for t in range(RT - 5, RT):
                if t + 2 < RT:
                    node_onehot(t + 2, (t + 2) % 4)
                add_rows(t, t % 2, block_of(t))
            dve.wait_ge(q.merged, RT + 2)
            v.link(V_.tensor_scalar(yden[:, :, :], Y[:, 0:NT, :, DK], 1e-37, None, ALU.max))
            v.link(V_.reciprocal(yden[:, :, :], yden[:, :, :]))
            for i in range(NT):
                V_.tensor_tensor(YN[:, i, :].rearrange("p (h d) -> p h d", h=HEADS), Y[:, i, :, 0:DK],
                                 yden[:, i, :].unsqueeze(2).broadcast_to([P, HEADS, DK]), ALU.mult).then_inc(q.yn_ready, 1)
            dve.wait_ge(q.x_back, 16)
            for i in range(NT):
                v.link(V_.tensor_tensor(X[:, i, :], X[:, i, :], bias_o[:, :], ALU.add))
            for i in range(NT):
                dve.wait_ge(q.wo_psum, i + 1)
                V_.tensor_tensor(X[:, i, :], X[:, i, :], bank[2 + i % 2][:, :], ALU.add).then_inc(q.wo_done, 1)
            dve.wait_ge(q.wo_done, NT)

            norm_stats(lambda i: X[:, i, :])
            dve.nop().then_inc(q.var_ready, 1)
            dve.wait_ge(q.std_ready, 2)
            v.link(V_.reciprocal(rstd[:, :], rstd[:, :]))
            for i in range(NT):
                V_.tensor_scalar(hn[:, i, :], X[:, i, :], mv[:, i, 0:1], rstd[:, i:i + 1], ALU.subtract, ALU.mult).then_inc(q.h_ready, 1)
            dve.wait_ge(q.r_psum, 1)

            def over(a):
                return a[:, :].unsqueeze(2).broadcast_to([P, NT, NE])

            pos = pos8[:, :].unsqueeze(1).broadcast_to([P, NT, NE])
            rb = bank[2][:, 0:NT * NE].rearrange("p (t e) -> p t e", e=NE)
            v.link(V_.tensor_reduce(r1[:, :], rb, AX.X, ALU.max))
            V_.tensor_tensor(rl[:, :, :], rb, over(r1), ALU.subtract).then_inc(q.r_ready, 1)
            dve.wait_ge(q.r_exp, 1)
            v.link(V_.tensor_reduce(r1[:, :], rp[:, :, :], AX.X, ALU.add))
            v.link(V_.reciprocal(r1[:, :], r1[:, :]))
            v.link(V_.tensor_tensor(rp[:, :, :], rp[:, :, :], over(r1), ALU.mult))
            v.link(V_.tensor_copy(rl[:, :, :], rp[:, :, :]))
            for k in range(2):
                v.link(V_.tensor_reduce(r1[:, :], rl[:, :, :], AX.X, ALU.max))
                v.link(V_.tensor_tensor(rt[:, :, :], rl[:, :, :], over(r1), ALU.is_equal))
                v.link(V_.tensor_scalar(rt[:, :, :], rt[:, :, :], -100.0, 100.0, ALU.mult, ALU.add))
                v.link(V_.tensor_tensor(rt[:, :, :], rt[:, :, :], pos, ALU.add))
                v.link(V_.tensor_reduce(r1[:, :], rt[:, :, :], AX.X, ALU.min))
                v.link(V_.tensor_tensor(pick[:, k, :, :], over(r1), pos, ALU.is_equal))
                if k == 0:
                    v.link(V_.tensor_scalar(rt[:, :, :], pick[:, k, :, :], -2.0, None, ALU.mult))
                    v.link(V_.tensor_tensor(rl[:, :, :], rl[:, :, :], rt[:, :, :], ALU.add))
            v.link(V_.tensor_tensor(both[:, :, :], pick[:, 0, :, :], pick[:, 1, :, :], ALU.add))
            V_.tensor_tensor(both[:, :, :], both[:, :, :], over(valid), ALU.mult).then_inc(q.both_ready, 1)
            v.link(V_.tensor_tensor(picked[:, :, :, :], pick[:, :, :, :], rp[:, :, :].unsqueeze(1).broadcast_to([P, TOPK, NT, NE]), ALU.mult))
            v.link(V_.tensor_reduce(gate[:, :, :], picked[:, :, :, :], AX.X, ALU.add))
            dve.wait_ge(q.ranks_psum, 1)
            v.link(V_.tensor_copy(before_t[:, :, :], bank[3][:, 0:NT * NE].rearrange("p (t e) -> p t e", e=NE)))
            v.link(V_.tensor_copy(total_t[:, :, :], bank[4][:, 0:NT * NE].rearrange("p (t e) -> p t e", e=NE)))
            for e in range(NE):
                v.link(V_.tensor_tensor_scan(upto_t[:, :, e], total_t[:, :, e], zeros_r[:, 0:NT], 0.0, ALU.add, ALU.add))
            v.link(V_.tensor_scalar(tiles_f[:, :], upto_t[:, NT - 1, :], float(P - 1), None, ALU.add))
            v.link(V_.tensor_copy(tiles_i[:, :], tiles_f[:, :]))
            v.link(V_.tensor_scalar(tiles_i[:, :], tiles_i[:, :], P.bit_length() - 1, None, ALU.logical_shift_right))
            v.link(V_.tensor_copy(tiles_f[:, :], tiles_i[:, :]))
            v.link(V_.tensor_scalar(tiles_f[:, :], tiles_f[:, :], 1.0, None, ALU.max))
            v.link(V_.tensor_tensor_scan(tile_end[:, :], tiles_f[:, :], zeros_r[:, 0:NE], 0.0, ALU.add, ALU.add))
            v.link(V_.tensor_tensor(tile_first[:, :], tile_end[:, :], tiles_f[:, :], ALU.subtract))
            v.link(V_.tensor_copy(tile_end_i[:, :], tile_end[:, :]))
            v.link(V_.tensor_scalar(tile_first[:, :], tile_first[:, :], float(P), None, ALU.mult))
            v.link(V_.tensor_tensor(pos_e[:, :, :], upto_t[:, :, :], total_t[:, :, :], ALU.subtract))
            v.link(V_.tensor_tensor(pos_e[:, :, :], pos_e[:, :, :], before_t[:, :, :], ALU.add))
            v.link(V_.tensor_tensor(pos_e[:, :, :], pos_e[:, :, :], tile_first[:, :].unsqueeze(1).broadcast_to([P, NT, NE]), ALU.add))
            v.link(V_.tensor_tensor(picked[:, :, :, :], pick[:, :, :, :], pos_e[:, :, :].unsqueeze(1).broadcast_to([P, TOPK, NT, NE]), ALU.mult))
            v.link(V_.tensor_reduce(pos_f[:, :, :], picked[:, :, :, :], AX.X, ALU.add))
            v.link(V_.tensor_scalar(r1[:, :], valid[:, :], -NOBODY, NOBODY, ALU.mult, ALU.add))
            v.link(V_.tensor_tensor(pos_f[:, :, :], pos_f[:, :, :], r1[:, :].unsqueeze(1).broadcast_to([P, TOPK, NT]), ALU.add))
            V_.tensor_copy(pos_i[:, :, :], pos_f[:, :, :]).then_inc(q.pos_ready, 1)
            v.link(V_.tensor_tensor(owner_c[:, :, :], tile_end[:, :].unsqueeze(1).broadcast_to([P, XT, NE]),
                                    iota256[:, 0:XT].unsqueeze(2).broadcast_to([P, XT, NE]), ALU.is_le))
            v.link(V_.tensor_reduce(owner_f[:, :], owner_c[:, :, :], AX.X, ALU.add))
            v.link(V_.tensor_scalar(owner_f[:, :], owner_f[:, :], NE - 1.0, None, ALU.min))
            v.link(V_.tensor_copy(owner_i[:, :], owner_f[:, :]))
            v.link(V_.tensor_scalar(owner_slot[:, :], owner_i[:, :], 1, None, ALU.bitwise_and))
            v.link(V_.tensor_scalar(owner_slot[:, :], owner_slot[:, :], 0, None, ALU.is_equal))
            v.link(V_.tensor_scalar(owner_f[:, :], owner_f[:, :], 2.0, 1.0, ALU.mult, ALU.add))
            v.link(V_.tensor_copy(owner_need[:, :], owner_f[:, :]))
            dve.nop().then_inc(q.owners_ready, 1)
            for j in range(2):
                dve.wait_ge(b2_in[j], 16)
            dve.nop().then_inc(q.ye_ready, 2)

            def tokens_low(i, b):
                dve.wait_ge(q.th_high, i + 1)
                V_.tensor_tensor(hTt[:, b, 1, :, :], bank[0][:, :].rearrange("p (a b) -> p a b", a=KC), hTt[:, b, 0, :, :].bitcast(F32),
                                 ALU.subtract).then_inc(q.th_ready, 1)

            def hidden_bias(i, b):
                slot = dve.value_load(owner_slot[0:1, bass.ds(i, 1)], min_val=0, max_val=1)
                dve.wait_ge(q.hid_psum, i + 1)
                V_.tensor_tensor(hid[:, b, :], psum[:, 1:3, :].rearrange("p a n -> p (a n)"),
                                 b1_s[:, bass.ds(slot, 1), :].rearrange("p a n -> p (a n)"), ALU.add).then_inc(q.hid_biased, 1)

            def hidden_low(i):
                dve.wait_ge(q.hidT_high, i + 1)
                V_.tensor_tensor(hidT[:, 1, :, :], psum[:, 3:5, :].rearrange("p a (c n) -> p (a c) n", c=4), hidT[:, 0, :, :].bitcast(F32),
                                 ALU.subtract).then_inc(q.hidT_ready, 1)

            def result_bias(i, b, stored):
                slot = dve.value_load(owner_slot[0:1, bass.ds(i, 1)], min_val=0, max_val=1)
                if stored is not None:
                    dve.wait_ge(y_out[b], stored)
                dve.wait_ge(q.ye_psum, i + 1)
                V_.tensor_tensor(yt[:, b, :], bank[5 + b][:, :], b2_s[:, bass.ds(slot, 1), :].rearrange("p a n -> p (a n)"),
                                 ALU.add).then_inc(q.ye_ready, 1)

            tokens_low(0, 0)
            hidden_bias(0, 0)
            tokens_low(1, 1)
            hidden_low(0)
            for i in range(1, 3):
                hidden_bias(i, i % 2)
                tokens_low(i + 1, (i + 1) % 2)
                result_bias(i - 1, (i - 1) % 2, None)
                hidden_low(i)
            with dve.Fori(0, (XT - 5) // 2) as n:
                for u in range(2):
                    hidden_bias(n * 2 + u + 3, 1 - u)
                    tokens_low(n * 2 + u + 4, u)
                    result_bias(n * 2 + u + 2, u, n * 16 + 16)
                    hidden_low(n * 2 + u + 3)
            for i in range(XT - 2, XT):
                hidden_bias(i, i % 2)
                if i + 1 < XT:
                    tokens_low(i + 1, (i + 1) % 2)
                result_bias(i - 1, (i - 1) % 2, 16 * ((i - 1) // 2))
                hidden_low(i)
            result_bias(XT - 1, (XT - 1) % 2, 16 * ((XT - 1) // 2))
            for m in range(NT * TOPK):
                i, k = divmod(m, TOPK)
                r = rows_of(i)
                dve.wait_ge(back_in[m % 4], 16 * (m // 4 + 1))
                if k:
                    dve.wait_ge(q.combined, m)
                V_.scalar_tensor_tensor(X[0:r, i, :], back[0:r, m % 4, :], gate[0:r, k, i:i + 1], X[0:r, i, :],
                                        ALU.mult, ALU.add).then_inc(q.combined, 1)


def rows_of(i):
    return P if i < NT - 1 else LAST


_INS = ["x", "src", "dst", "edge_attr_8", "L0_gnn_Wq", "L0_gnn_bq", "L0_gnn_Wk", "L0_gnn_bk", "L0_gnn_Wv", "L0_gnn_bv",
        "L0_gnn_Wo", "L0_gnn_bo", "L0_mix_w_qkv", "L0_mix_w_out", "L0_mix_gamma", "L0_ffn_Wg", "L0_ffn_W1", "L0_ffn_b1",
        "L0_ffn_W2", "L0_ffn_b2"]


def kernel(**inputs):
    import concourse.bacc as bacc
    from concourse.bass_utils import run_bass_kernel_spmd

    nc = bacc.Bacc("TRN2", target_bir_lowering=False, num_devices=1)
    arrays, args = {}, []
    for name in _INS:
        a = np.ascontiguousarray(inputs[name])
        arrays[f"in_{name}"] = a
        args.append(nc.dram_tensor(f"in_{name}", a.shape, mybir.dt.from_np(a.dtype), kind="ExternalInput").ap())
    args.append(nc.dram_tensor("out_x", (N, D), F32, kind="ExternalOutput").ap())
    gps_layer(nc, *args)
    r = run_bass_kernel_spmd(nc, [arrays], core_ids=[0])
    return r.results[0]["out_x"]
```
